# Optimizing a Trainium2 kernel written in Bass

```python
import numpy as np
import jax
import jax.numpy as jnp

def _softmax(x, axis=-1):
    return jax.nn.softmax(x, axis=axis)

def _gelu(x):
    return jax.nn.gelu(x, approximate=True)

def _silu(x):
    return jax.nn.silu(x)

def _sigmoid(x):
    return jax.nn.sigmoid(x)

def _layernorm(x, axis=-1, eps=1e-05):
    m = jnp.mean(x, axis=axis, keepdims=True)
    v = jnp.var(x, axis=axis, keepdims=True)
    return (x - m) / jnp.sqrt(v + eps)

def _scatter_add(tgt, idx, src, axis=0):
    return tgt.at[idx].add(src)

def _segment_sum(src, seg, n):
    return jax.ops.segment_sum(src, seg, n)
kernel_name = 'mk_early_fusion_d1_tok_img768_r4_a2e494'

def setup_inputs(seed: int=0):
    np.random.seed(seed)
    _w = jnp.asarray

    def _rec_inputs():
        import jax
        import jax.numpy as jnp
        _rk = jax.random.key(seed)
        x = -0.000125008 + 0.999885 * jax.random.normal(jax.random.fold_in(_rk, 1), (64, 1, 96, 96), jnp.float32)
        txt = 3.85875e-05 + 0.319609 * jax.random.normal(jax.random.fold_in(_rk, 2), (64, 128, 192), jnp.float32)
        return (x, txt)
    x, txt = _rec_inputs()

    def _L0_tok_setup():
        import jax, jax.numpy as jnp
        import numpy as np
        PATCH = 16
        LATENT = 192

        def _extract_patches(x, p):
            B, C, H, W_ = x.shape
            nh, nw = (H // p, W_ // p)
            patches = x.reshape(B, C, nh, p, nw, p).transpose(0, 1, 2, 4, 3, 5)
            return patches.reshape(B, nh * nw, C * p * p)
        key = jax.random.key(seed)
        k1, k2 = jax.random.split(key)
        x = jax.random.normal(k1, (32, 1, 256, 256), dtype=jnp.float32)
        W = jax.random.normal(k2, (LATENT, PATCH * PATCH), dtype=jnp.float32) * 0.02
        return {'x': x, 'W': W}
    _L0_tok_all = _L0_tok_setup()
    _L0_tok_in = {k: v for k, v in _L0_tok_all.items() if k in ('W',)}
    del _L0_tok_all

    def _L0_attn_setup():
        import jax, jax.numpy as jnp
        import numpy as np
        EMBED_DIM = 192
        NUM_HEADS = 12
        HEAD_DIM = EMBED_DIM // NUM_HEADS
        SCALE = HEAD_DIM ** (-0.5)
        EPS = 1e-05

        def _layernorm(x, g, b):
            m = jnp.mean(x, axis=-1, keepdims=True)
            v = jnp.mean(jnp.square(x - m), axis=-1, keepdims=True)
            return (x - m) * jax.lax.rsqrt(v + EPS) * g + b
        key = jax.random.key(seed)
        ks = jax.random.split(key, 8)
        B, N, D, Hd = (16, 256, EMBED_DIM, HEAD_DIM)
        x = jax.random.normal(ks[0], (B, N, D), dtype=jnp.float32)
        W_qkv = jax.random.normal(ks[1], (D, 3 * D), dtype=jnp.float32) * D ** (-0.5)
        b_qkv = jnp.zeros((3 * D,), dtype=jnp.float32)
        W_proj = jax.random.normal(ks[2], (D, D), dtype=jnp.float32) * D ** (-0.5)
        b_proj = jnp.zeros((D,), dtype=jnp.float32)
        return {'x': x, 'ln_g': jnp.ones((D,), jnp.float32), 'ln_b': jnp.zeros((D,), jnp.float32), 'W_qkv': W_qkv, 'b_qkv': b_qkv, 'qn_g': jnp.ones((Hd,), jnp.float32), 'qn_b': jnp.zeros((Hd,), jnp.float32), 'kn_g': jnp.ones((Hd,), jnp.float32), 'kn_b': jnp.zeros((Hd,), jnp.float32), 'W_proj': W_proj, 'b_proj': b_proj}
    _L0_attn_all = _L0_attn_setup()
    _L0_attn_in = {k: v for k, v in _L0_attn_all.items() if k in ('ln_g', 'ln_b', 'W_qkv', 'b_qkv', 'qn_g', 'qn_b', 'kn_g', 'kn_b', 'W_proj', 'b_proj')}
    del _L0_attn_all

    def _L0_ffn_setup():
        import jax, jax.numpy as jnp
        import numpy as np
        H = 12
        ALPHA = (1, 2, 3)
        DEPTH = 5
        BLOCK_DEPTH = 3
        TOTAL_DEPTH_M1 = 14 - 1
        SMALL_ACTIVE = BLOCK_DEPTH <= DEPTH <= TOTAL_DEPTH_M1 - BLOCK_DEPTH

        def _ln(x, g, b, eps=1e-05):
            m = jnp.mean(x, axis=-1, keepdims=True)
            v = jnp.mean((x - m) ** 2, axis=-1, keepdims=True)
            return (x - m) * jax.lax.rsqrt(v + eps) * g + b

        def _attn_branch(xp, w_qkv, w_proj, b_proj, keep_heads, keep_ch):
            B2, N, C = xp.shape
            hd = C // H
            scale = hd ** (-0.5)
            qkv = (xp @ w_qkv).reshape(B2, N, 3, H, hd).transpose(2, 0, 3, 1, 4)
            hmask = (jnp.arange(H) < keep_heads).astype(xp.dtype)[None, :, None, None]
            q, k, v = (qkv[0] * hmask, qkv[1] * hmask, qkv[2] * hmask)
            a = jax.nn.softmax(jnp.einsum('bhnd,bhmd->bhnm', q, k) * scale, axis=-1)
            o = jnp.einsum('bhnm,bhmd->bhnd', a, v).transpose(0, 2, 1, 3).reshape(B2, N, C)
            o = o @ w_proj + b_proj
            cmask = (jnp.arange(C) < keep_ch).astype(xp.dtype)
            return o * cmask

        def _mlp_branch(xp, w1, b1, w2, b2, keep_ch):
            C = xp.shape[-1]
            cmask = (jnp.arange(C) < keep_ch).astype(xp.dtype)
            h = jax.nn.gelu(xp * cmask @ w1 + b1, approximate=False)
            return (h @ w2 + b2) * cmask
        key = jax.random.key(seed)
        ks = jax.random.split(key, 8)
        B, N, C = (64, 257, 192)
        HID = 4 * C

        def w(k, shape):
            return jax.random.normal(k, shape, jnp.float32) * 0.02
        return {'x': jax.random.normal(ks[0], (B, N, C), jnp.float32), 'gumbel_weights': jax.random.uniform(ks[1], (3,), jnp.float32), 'n1l_g': jnp.ones((C,), jnp.float32), 'n1l_b': jnp.zeros((C,), jnp.float32), 'n1s_g': jnp.ones((C,), jnp.float32), 'n1s_b': jnp.zeros((C,), jnp.float32), 'w_qkv': w(ks[2], (C, 3 * C)), 'w_proj': w(ks[3], (C, C)), 'b_proj': jnp.zeros((C,), jnp.float32), 'n2l_g': jnp.ones((C,), jnp.float32), 'n2l_b': jnp.zeros((C,), jnp.float32), 'n2s_g': jnp.ones((C,), jnp.float32), 'n2s_b': jnp.zeros((C,), jnp.float32), 'w_fc1': w(ks[4], (C, HID)), 'b_fc1': jnp.zeros((HID,), jnp.float32), 'w_fc2': w(ks[5], (HID, C)), 'b_fc2': jnp.zeros((C,), jnp.float32)}
    _L0_ffn_all = _L0_ffn_setup()
    _L0_ffn_in = {k: v for k, v in _L0_ffn_all.items() if k in ('gumbel_weights', 'n1l_g', 'n1l_b', 'n1s_g', 'n1s_b', 'w_qkv', 'w_proj', 'b_proj', 'n2l_g', 'n2l_b', 'n2s_g', 'n2s_b', 'w_fc1', 'b_fc1', 'w_fc2', 'b_fc2')}
    del _L0_ffn_all
    return {'x': x, 'txt': txt, 'L0_tok_W': _L0_tok_in['W'], 'L0_attn_ln_g': _L0_attn_in['ln_g'], 'L0_attn_ln_b': _L0_attn_in['ln_b'], 'L0_attn_W_qkv': _L0_attn_in['W_qkv'], 'L0_attn_b_qkv': _L0_attn_in['b_qkv'], 'L0_attn_qn_g': _L0_attn_in['qn_g'], 'L0_attn_qn_b': _L0_attn_in['qn_b'], 'L0_attn_kn_g': _L0_attn_in['kn_g'], 'L0_attn_kn_b': _L0_attn_in['kn_b'], 'L0_attn_W_proj': _L0_attn_in['W_proj'], 'L0_attn_b_proj': _L0_attn_in['b_proj'], 'L0_ffn_gumbel_weights': _L0_ffn_in['gumbel_weights'], 'L0_ffn_n1l_g': _L0_ffn_in['n1l_g'], 'L0_ffn_n1l_b': _L0_ffn_in['n1l_b'], 'L0_ffn_n1s_g': _L0_ffn_in['n1s_g'], 'L0_ffn_n1s_b': _L0_ffn_in['n1s_b'], 'L0_ffn_w_qkv': _L0_ffn_in['w_qkv'], 'L0_ffn_w_proj': _L0_ffn_in['w_proj'], 'L0_ffn_b_proj': _L0_ffn_in['b_proj'], 'L0_ffn_n2l_g': _L0_ffn_in['n2l_g'], 'L0_ffn_n2l_b': _L0_ffn_in['n2l_b'], 'L0_ffn_n2s_g': _L0_ffn_in['n2s_g'], 'L0_ffn_n2s_b': _L0_ffn_in['n2s_b'], 'L0_ffn_w_fc1': _L0_ffn_in['w_fc1'], 'L0_ffn_b_fc1': _L0_ffn_in['b_fc1'], 'L0_ffn_w_fc2': _L0_ffn_in['w_fc2'], 'L0_ffn_b_fc2': _L0_ffn_in['b_fc2']}

def reference(x, txt, L0_tok_W, L0_attn_ln_g, L0_attn_ln_b, L0_attn_W_qkv, L0_attn_b_qkv, L0_attn_qn_g, L0_attn_qn_b, L0_attn_kn_g, L0_attn_kn_b, L0_attn_W_proj, L0_attn_b_proj, L0_ffn_gumbel_weights, L0_ffn_n1l_g, L0_ffn_n1l_b, L0_ffn_n1s_g, L0_ffn_n1s_b, L0_ffn_w_qkv, L0_ffn_w_proj, L0_ffn_b_proj, L0_ffn_n2l_g, L0_ffn_n2l_b, L0_ffn_n2s_g, L0_ffn_n2s_b, L0_ffn_w_fc1, L0_ffn_b_fc1, L0_ffn_w_fc2, L0_ffn_b_fc2):
    import jax
    import jax.numpy as jnp

    def _L0_tok_ref(x, W):
        import jax, jax.numpy as jnp
        import numpy as np
        PATCH = 16
        LATENT = 192

        def _extract_patches(x, p):
            B, C, H, W_ = x.shape
            nh, nw = (H // p, W_ // p)
            patches = x.reshape(B, C, nh, p, nw, p).transpose(0, 1, 2, 4, 3, 5)
            return patches.reshape(B, nh * nw, C * p * p)
        patches = _extract_patches(x, PATCH)
        return jnp.einsum('bnk,ok->bno', patches, W)

    def _L0_attn_ref(x, ln_g, ln_b, W_qkv, b_qkv, qn_g, qn_b, kn_g, kn_b, W_proj, b_proj):
        import jax, jax.numpy as jnp
        import numpy as np
        EMBED_DIM = 192
        NUM_HEADS = 12
        HEAD_DIM = EMBED_DIM // NUM_HEADS
        SCALE = HEAD_DIM ** (-0.5)
        EPS = 1e-05

        def _layernorm(x, g, b):
            m = jnp.mean(x, axis=-1, keepdims=True)
            v = jnp.mean(jnp.square(x - m), axis=-1, keepdims=True)
            return (x - m) * jax.lax.rsqrt(v + EPS) * g + b
        B, N, D = x.shape
        H, Hd = (NUM_HEADS, HEAD_DIM)
        xn = _layernorm(x, ln_g, ln_b)
        qkv = xn @ W_qkv + b_qkv
        qkv = qkv.reshape(B, N, 3, H, Hd)
        q = jnp.transpose(qkv[:, :, 0], (0, 2, 1, 3))
        k = jnp.transpose(qkv[:, :, 1], (0, 2, 1, 3))
        v = jnp.transpose(qkv[:, :, 2], (0, 2, 1, 3))
        q = _layernorm(q, qn_g, qn_b)
        k = _layernorm(k, kn_g, kn_b)
        attn = jnp.einsum('bhnd,bhmd->bhnm', q, k) * SCALE
        attn = jax.nn.softmax(attn, axis=-1)
        out = jnp.einsum('bhnm,bhmd->bhnd', attn, v)
        out = jnp.transpose(out, (0, 2, 1, 3)).reshape(B, N, D)
        return out @ W_proj + b_proj

    def _L0_ffn_ref(x, gumbel_weights, n1l_g, n1l_b, n1s_g, n1s_b, w_qkv, w_proj, b_proj, n2l_g, n2l_b, n2s_g, n2s_b, w_fc1, b_fc1, w_fc2, b_fc2):
        import jax, jax.numpy as jnp
        import numpy as np
        H = 12
        ALPHA = (1, 2, 3)
        DEPTH = 5
        BLOCK_DEPTH = 3
        TOTAL_DEPTH_M1 = 14 - 1
        SMALL_ACTIVE = BLOCK_DEPTH <= DEPTH <= TOTAL_DEPTH_M1 - BLOCK_DEPTH

        def _ln(x, g, b, eps=1e-05):
            m = jnp.mean(x, axis=-1, keepdims=True)
            v = jnp.mean((x - m) ** 2, axis=-1, keepdims=True)
            return (x - m) * jax.lax.rsqrt(v + eps) * g + b

        def _attn_branch(xp, w_qkv, w_proj, b_proj, keep_heads, keep_ch):
            B2, N, C = xp.shape
            hd = C // H
            scale = hd ** (-0.5)
            qkv = (xp @ w_qkv).reshape(B2, N, 3, H, hd).transpose(2, 0, 3, 1, 4)
            hmask = (jnp.arange(H) < keep_heads).astype(xp.dtype)[None, :, None, None]
            q, k, v = (qkv[0] * hmask, qkv[1] * hmask, qkv[2] * hmask)
            a = jax.nn.softmax(jnp.einsum('bhnd,bhmd->bhnm', q, k) * scale, axis=-1)
            o = jnp.einsum('bhnm,bhmd->bhnd', a, v).transpose(0, 2, 1, 3).reshape(B2, N, C)
            o = o @ w_proj + b_proj
            cmask = (jnp.arange(C) < keep_ch).astype(xp.dtype)
            return o * cmask

        def _mlp_branch(xp, w1, b1, w2, b2, keep_ch):
            C = xp.shape[-1]
            cmask = (jnp.arange(C) < keep_ch).astype(xp.dtype)
            h = jax.nn.gelu(xp * cmask @ w1 + b1, approximate=False)
            return (h @ w2 + b2) * cmask
        B, N, C = x.shape
        B2 = B // 2
        nl = _ln(x[:B2], n1l_g, n1l_b)
        ns = _ln(x[B2:], n1s_g, n1s_b)
        a_large = _attn_branch(nl, w_qkv, w_proj, b_proj, H, C)
        if SMALL_ACTIVE:
            a_small = sum((gumbel_weights[i] * _attn_branch(ns, w_qkv, w_proj, b_proj, H // ALPHA[i], C // ALPHA[i]) for i in range(3)))
            attn_out = jnp.concatenate([a_large, a_small], axis=0)
        else:
            attn_out = jnp.concatenate([a_large, a_large], axis=0)
        x = x + attn_out
        nl2 = _ln(x[:B2], n2l_g, n2l_b)
        ns2 = _ln(x[B2:], n2s_g, n2s_b)
        m_large = _mlp_branch(nl2, w_fc1, b_fc1, w_fc2, b_fc2, C)
        if SMALL_ACTIVE:
            m_small = sum((gumbel_weights[i] * _mlp_branch(ns2, w_fc1, b_fc1, w_fc2, b_fc2, C // ALPHA[i]) for i in range(3)))
            mlp_out = jnp.concatenate([m_large, m_small], axis=0)
        else:
            mlp_out = jnp.concatenate([m_large, m_large], axis=0)
        return x + mlp_out
    h = _L0_tok_ref(x, L0_tok_W)
    h = jnp.concatenate([h, txt], axis=1)
    h = h + _L0_attn_ref(_layernorm(h, axis=-1), L0_attn_ln_g, L0_attn_ln_b, L0_attn_W_qkv, L0_attn_b_qkv, L0_attn_qn_g, L0_attn_qn_b, L0_attn_kn_g, L0_attn_kn_b, L0_attn_W_proj, L0_attn_b_proj)
    h = h + _L0_ffn_ref(_layernorm(h, axis=-1), L0_ffn_gumbel_weights, L0_ffn_n1l_g, L0_ffn_n1l_b, L0_ffn_n1s_g, L0_ffn_n1s_b, L0_ffn_w_qkv, L0_ffn_w_proj, L0_ffn_b_proj, L0_ffn_n2l_g, L0_ffn_n2l_b, L0_ffn_n2s_g, L0_ffn_n2s_b, L0_ffn_w_fc1, L0_ffn_b_fc1, L0_ffn_w_fc2, L0_ffn_b_fc2)
    return h

_drawn_inputs = setup_inputs


def setup_inputs(seed=0):
    import zlib

    import numpy as np

    out = dict(_drawn_inputs(seed))
    spreads = {'L0_attn_ln_g': (1.0, 0.2),
     'L0_attn_ln_b': (0.0, 0.1),
     'L0_attn_b_qkv': (0.0, 0.1),
     'L0_attn_qn_g': (1.0, 0.2),
     'L0_attn_qn_b': (0.0, 0.1),
     'L0_attn_kn_g': (1.0, 0.2),
     'L0_attn_kn_b': (0.0, 2.0),
     'L0_attn_b_proj': (0.0, 0.1),
     'L0_ffn_n1l_g': (1.0, 0.6),
     'L0_ffn_n1l_b': (0.0, 0.8),
     'L0_ffn_n1s_g': (1.0, 0.6),
     'L0_ffn_n1s_b': (0.0, 0.8),
     'L0_ffn_b_proj': (0.0, 0.1),
     'L0_ffn_n2l_g': (1.0, 0.6),
     'L0_ffn_n2l_b': (0.0, 0.8),
     'L0_ffn_n2s_g': (1.0, 0.6),
     'L0_ffn_n2s_b': (0.0, 2.0),
     'L0_ffn_b_fc1': (0.0, 0.532),
     'L0_ffn_b_fc2': (0.0, 0.1)}
    factors = {'L0_ffn_gumbel_weights': 4.261, 'L0_ffn_w_qkv': 2.882, 'L0_ffn_w_proj': 2.689}
    for name, (base, spread) in spreads.items():
        noise = np.random.default_rng([zlib.crc32(name.encode()), seed]).standard_normal(out[name].shape)
        drawn = base * np.exp(spread * noise) if base else spread * noise
        out[name] = jnp.asarray(drawn.astype(out[name].dtype))
    for name, factor in factors.items():
        out[name] = (out[name] * factor).astype(out[name].dtype)
    return out
```

```python
from contextlib import ExitStack

import concourse.bass as bass
from concourse import mybir

F32 = mybir.dt.float32
F16 = mybir.dt.float16
ALU = mybir.AluOpType
ACT = mybir.ActivationFunctionType
AX_X = mybir.AxisListType.X

BATCH = 64
IMG = 36
TXT = 128
SEQ = IMG + TXT
D = 192
H = 12
HD = D // H
PK = 256
HID = 4 * D
EPS = 1e-5
PAIRS = BATCH // 2
LARGE = PAIRS // 2
KEEP = (D, D // 2, D // 3)

P = 128
C = 3
IMG_AT = (0, 64)
IMG_END = 64 + IMG
KT = D // 2
LO = D - P
BLK = 64
NPT = H // 2
HG = 3
NHG = H // HG
TILES = C * NHG
WS = 64.0
SCALE = HD ** -0.5
NHT = HID // P


def heads_of(g):
    h = 2 * HG * (g // 2) + g % 2
    return slice(h, h + 2 * HG - 1, 2)


def at(n, per, k):
    if isinstance(n, int):
        return n * per + k
    j, off = n
    return j * (2 * per) + (off * per + k)


def later(n, k):
    return not isinstance(n, int) or n >= k


def build(nc, a):
    ctx = ExitStack()
    with ctx:
        def sb(name, shape, dt=F32):
            return ctx.enter_context(nc.sbuf_tensor(name, shape, dt))

        def sem(name):
            return ctx.enter_context(nc.semaphore(name))

        def sems(name):
            return [sem(f"{name}{i}") for i in range(2)]

        h1_dram = nc.dram_tensor("h1_scratch", [PAIRS, P, C * D], F32, kind="Internal").ap()
        x2_dram = nc.dram_tensor("x2_scratch", [PAIRS, P, C * D], F32, kind="Internal").ap()

        bank = [ctx.enter_context(nc.psum_tensor(f"bank{i}", [P, 512], F32)) for i in range(8)]
        SM = [bank[0], bank[1]]
        SE = [bank[2], bank[3]]
        TP = [bank[4], bank[5]]
        G0, G1 = bank[6], bank[7]

        def half(b):
            return b[:, :].bitcast(F16)

        def item(b):
            return half(TP[b])[:, 0:NPT * SEQ].rearrange("p (t s) -> p t s", t=NPT)

        idf = sb("idf", [P, P])
        idh = sb("idh", [P, P], F16)
        ones = sb("ones", [P, P])
        neghalf = sb("neghalf", [P, 72])
        tokw = sb("tokw", [P, 2, D])
        w_qkv = {k: sb(f"w_qkv_{k}", [P, 4, 3 * D], F16) for k in ("A", "L", "S")}
        w_prj = {k: sb(f"w_prj_{k}", [P, 4, D], F16) for k in ("A", "L", "S")}
        w_fc1 = {k: sb(f"w_fc1_{k}", [P, 4, HID], F16) for k in ("L", "S")}
        w_fc2 = [sb(f"w_fc2_{i}", [P, NHT, k]) for i, k in enumerate((D,) + KEEP)]
        b_qkv = {k: sb(f"b_qkv_{k}", [P, 3 * D]) for k in ("A", "L", "S")}
        b_prj = {k: sb(f"b_prj_{k}", [P, D]) for k in ("A", "L", "S")}
        b_fc1 = sb("b_fc1", [P, 4, NHT])
        b_fc2 = {k: sb(f"b_fc2_{k}", [P, D]) for k in ("L", "S")}
        gains = sb("gains", [P, 2, D])
        shifts = sb("shifts", [P, 2, D])
        gw = sb("gw", [P, 3])
        zeros = sb("zeros", [P, 1])
        carrier = sb("carrier", [P, 1])

        hin = [sb(f"hin{i}", [P, C, D]) for i in range(2)]
        patches = [sb(f"patches{i}", [P, 2, IMG_END]) for i in range(2)]
        stats = sb("stats", [P, C, 6])
        mv = sb("mv", [P, C, 2])
        ve = sb("ve", [P, 2, C])
        rstd = sb("rstd", [P, 2, C])
        xn = sb("xn", [P, C, D])
        xs = sb("xs", [P, C, 3 * P], F16)
        xt = sb("xt", [P, C, 3, P], F16)
        resx = [sb(f"resx{i}", [P, C, D]) for i in range(2)]
        resb = [sb(f"resb{i}", [P, C, D]) for i in range(2)]
        qk = sb("qk", [P, 2, C, D])
        sq = sb("sq", [P, 2, C, D])
        hvar = sb("hvar", [P, 72])
        hrstd = sb("hrstd", [P, 72])
        qs = sb("qs", [P, C * H, BLK], F16)
        ks = sb("ks", [P, C * H, BLK], F16)
        qT = sb("qT", [P, NPT, 2 * SEQ], F16)
        kT = sb("kT", [P, NPT, 2 * SEQ], F16)
        v1 = [sb(f"v1_{i}", [P, C, H, 32]) for i in range(2)]
        negmax = sb("negmax", [P, C, H])
        probs = sb("probs", [P, C, H, SEQ])
        oT = sb("oT", [P, 3, C, P])
        rden = sb("rden", [P, C, H])
        on = sb("on", [P, C, D])
        os_ = sb("os_", [P, C, 3 * P], F16)
        ou = sb("ou", [P, C, 3, P], F16)
        outb = [sb(f"outb{i}", [P, C, D]) for i in range(2)]
        flat = probs[:, :, :, :].rearrange("p c h s -> p (c h s)")
        raw_qkv = [flat[:, i * 1152:(i + 1) * 1152].rearrange("p (t n) -> p t n", t=2) for i in range(2)]
        raw_prj = [flat[:, 2304 + i * 384:2304 + (i + 1) * 384].rearrange("p (t n) -> p t n", t=2)
                   for i in range(2)]
        raw_fc1 = flat[:, 3072:3072 + 1536].rearrange("p (t n) -> p t n", t=2)
        bcol = sb("bcol", [P, 10, 2])
        bwide = sb("bwide", [P, 2, P])
        gmean = sb("gmean", [P, 2, 24])
        tmpw = sb("tmpw", [P, 2, D])
        coef = sb("coef", [P, D])
        x2in = [sb(f"x2in{i}", [P, C, D]) for i in range(2)]
        h1in = [sb(f"h1in{i}", [P, C, D]) for i in range(2)]
        mT = sb("mT", [P, 3, C * P], F16)
        gT = [sb(f"gT{i}", [P, NHT, C * P]) for i in range(2)]

        s_w = sem("weights_loaded")
        s_cst = sem("constants_set")
        s_idm = sem("identity_cleared")
        s_zero = sem("padding_set")
        s_bw = sem("shift_widened")
        s_bmm = sem("shift_multiplied")
        s_wv = sem("setup_vector_step")
        s_tokin, s_hin = sems("tokens_loaded"), sems("h1_loaded")
        s_tokmm, s_toksb = sem("tok_multiplied"), sem("tok_copied")
        s_stats, s_aggr, s_ve, s_rstd = sem("stats"), sem("aggr"), sem("var_eps"), sem("rstd")
        s_xn, s_resx, s_resb = sem("xn_ready"), sem("resx_ready"), sem("resb_ready")
        s_xhi, s_xlo, s_xtpe, s_xt = sem("x_hi"), sem("x_lo"), sem("x_transposed"), sem("xT_ready")
        s_qkmm, s_qk, s_vmm, s_v = sem("qk_multiplied"), sem("qk_copied"), sem("v_multiplied"), sem("v_copied")
        s_sq, s_hvar, s_hve, s_hrstd = sem("qk_squared"), sem("head_var"), sem("head_var_eps"), sem("head_rstd")
        s_qkn, s_qkg, s_qkb = sem("qk_normed"), sem("qk_gained"), sem("qk_shifted")
        s_qhi, s_khi, s_qlo, s_klo, s_mz = sem("q_hi"), sem("k_hi"), sem("q_lo"), sem("k_lo"), sem("shift_cleared")
        s_ktpe, s_kt, s_qtpe, s_qt = sem("k_transposed"), sem("kT_ready"), sem("q_transposed"), sem("qT_ready")
        s_sc, s_mx = sem("scores_for_max"), sem("max_taken")
        s_mh, s_ml = sem("max_hi"), sem("max_lo")
        s_qmpe, s_qm = sem("shifted_q_transposed"), sem("shifted_qT_ready")
        s_st, s_ex = sem("scores_for_exp"), sem("exp_done")
        s_otpe, s_ot = sem("pv_multiplied"), sem("oT_copied")
        s_onpe, s_rden, s_on = sem("o_transposed"), sem("denominators"), sem("o_normed")
        s_ohi, s_olo, s_oupe, s_ou = sem("o_hi"), sem("o_lo"), sem("ou_transposed"), sem("ou_ready")
        s_ype, s_y = sem("proj_multiplied"), sem("attention_added")
        s_stored = sems("attention_stored")
        s_mx2, s_mh1 = sems("mlp_x2_loaded"), sems("mlp_h1_loaded")
        m_stats, m_aggr, m_ve, m_rstd = sem("m_stats"), sem("m_aggr"), sem("m_var_eps"), sem("m_rstd")
        m_xn, m_hi, m_lo, m_tpe, m_t = sem("m_xn"), sem("m_hi"), sem("m_lo"), sem("m_transposed"), sem("mT_ready")
        m_r1, m_res = sem("m_res_half"), sem("m_res")
        m_f1, m_g, m_f2, m_y = sem("fc1_multiplied"), sem("gelu_done"), sem("fc2_multiplied"), sem("mlp_added")
        s_out = sems("output_stored")

        block = ctx.enter_context(nc.Block())

        def kind(n):
            return "A" if n < PAIRS else "L" if n < PAIRS + LARGE else "S"

        def run_steps(eng, front, step):
            front(0, 0, "A")
            n = 0
            last = 2 * PAIRS - 1
            while n <= last:
                end = n
                while end < last and kind(end + 1) == kind(n):
                    end += 1
                for _ in range(2 if n == 0 else 0):
                    step(n, n % 2, kind(n), kind(n + 1))
                    n += 1
                pairs = (end - n) // 2
                with eng.Fori(n // 2, n // 2 + pairs) as j:
                    for u in range(2):
                        step((j, u), u, kind(n), kind(n))
                n += 2 * pairs
                while n <= end:
                    step(n, n % 2, kind(n), kind(n + 1) if n < last else None)
                    n += 1

        def plus(n, k):
            return n + k if isinstance(n, int) else (n[0], n[1] + k)

        def pair_of(n, k):
            base = 0 if k == "A" else PAIRS
            return n - base if isinstance(n, int) else n[0] * 2 + (n[1] - base)

        def run_mlp(eng, mstep):
            for lo, hi, k in ((0, LARGE, "L"), (LARGE, PAIRS, "S")):
                n = lo
                for _ in range(2):
                    mstep(n, n % 2, k, k)
                    n += 1
                with eng.Fori(n // 2, (hi - 2) // 2) as j:
                    for u in range(2):
                        mstep((j, u), u, k, k)
                mstep(hi - 2, 0, k, k)
                mstep(hi - 1, 1, k, "S" if hi < PAIRS else None)

        def at_parity(n, per):
            return per * (n // 2 + 1) if isinstance(n, int) else n[0] * per + per * (n[1] // 2 + 1)

        def hin_count(n):
            return 16 * (n // 2 + 1 - PAIRS // 2) if isinstance(n, int) else \
                n[0] * 16 + 16 * (n[1] // 2 + 1 - PAIRS // 2)

        def resx_count(n):
            return at(n, C, C - C * PAIRS)

        def mlp_at(m, k, per, c):
            return at(m, per, c) if k == "L" else at(m, 3 * per, c - 2 * per * LARGE)

        def branch_parity(m, k, br):
            off = m if isinstance(m, int) else m[1]
            return (off if k == "L" else off + br) % 2

        @block.sync
        def _(sp):
            n_w = 0

            def load(dst, src):
                sp.dma_start(dst, src).then_inc(s_w, 16)

            def load_rows(dst, src):
                load(dst[:, 0, :], src[0:P, :])
                load(dst[0:LO, 1, :], src[P:D, :])
                load(dst[LO:P, 1, :], src[P:D, :])

            load(tokw[:, :, :], a["tokw"].rearrange("(t p) n -> p t n", p=P))
            load_rows(raw_qkv[0], a["attn_W_qkv"])
            load_rows(raw_qkv[1], a["ffn_w_qkv"])
            load_rows(raw_prj[0], a["attn_W_proj"])
            load_rows(raw_prj[1], a["ffn_w_proj"])
            load_rows(raw_fc1, a["ffn_w_fc1"])
            load(w_fc2[0][:, :, :], a["ffn_w_fc2"].rearrange("(t p) n -> p t n", p=P))
            for i, name in enumerate(NORMS):
                for dst, src in ((bcol[:, i, 0:1], a[name][0:P]), (bcol[0:LO, i, 1:2], a[name][P:D]),
                                 (bcol[LO:P, i, 1:2], a[name][P:D])):
                    load(dst, src.rearrange("(p o) -> p o", o=1))
            load(b_qkv["A"][:, :], a["attn_b_qkv"].partition_broadcast(P))
            load(b_prj["A"][:, :], a["attn_b_proj"].partition_broadcast(P))
            load(b_prj["L"][:, :], a["ffn_b_proj"].partition_broadcast(P))
            load(b_fc2["L"][:, :], a["ffn_b_fc2"].partition_broadcast(P))
            load(tmpw[:, 0, 0:NHT], a["ffn_b_fc1"])
            load(gw[:, :], a["gumbel"].partition_broadcast(P))
            for i, (g, b) in enumerate((("attn_qn_g", "attn_qn_b"), ("attn_kn_g", "attn_kn_b"))):
                load(tmpw[:, 1, 32 * i:32 * i + HD], a[g].partition_broadcast(P))
                load(tmpw[:, 1, 32 * i + HD:32 * i + 2 * HD], a[b].partition_broadcast(P))

            def index(p):
                return p if isinstance(p, int) else sp.snap(p)

            def load_unit(n, u, k):
                p = index(pair_of(n, k))
                if k == "A":
                    txt = a["txt"].rearrange("(q b) t d -> q t b d", b=2)[bass.ds(p, 1), :, :, :]\
                        .rearrange("q t b d -> t (q b) d")
                    sp.dma_start(hin[u][:, 0:2, :], txt).then_inc(s_tokin[u], 16)
                    xp = a["patches"][bass.ds(p, 1), :, :, :].rearrange("o p t n -> p (o t) n")
                    sp.dma_start(patches[u][:, :, :], xp).then_inc(s_tokin[u], 16)
                else:
                    sp.wait_ge(s_stored[u], stored_count(n, u))
                    src = h1_dram[bass.ds(p, 1), :, :].rearrange("o p f -> p (o f)")
                    sp.dma_start(hin[u][:, :, :].rearrange("p c d -> p (c d)"), src).then_inc(s_hin[u], 16)

            def stored_count(n, u):
                return 16 * (n // 2 + 1 - PAIRS // 2) if isinstance(n, int) else \
                    n[0] * 16 + 16 * (n[1] // 2 + 1 - PAIRS // 2)

            def front(n, u, k):
                load_unit(n, u, k)

            def step(n, u, kb, kf):
                if kf:
                    load_unit(plus(n, 1), 1 - u, kf)
                p = index(pair_of(n, kb))
                sp.wait_ge(s_y, at(n, 3, 3))
                dst = h1_dram if kb == "A" else x2_dram
                sp.dma_start(dst[bass.ds(p, 1), :, :].rearrange("o p f -> p (o f)"),
                             outb[u][:, :, :].rearrange("p c d -> p (c d)")).then_inc(s_stored[u], 16)

            sp.wait_ge(s_zero, 1)
            run_steps(sp, front, step)

            for u in range(2):
                sp.wait_ge(s_stored[u], 16 * PAIRS)

            def mload(m, u):
                p = index(m if isinstance(m, int) else m[0] * 2 + m[1])
                for dst, src, s in ((x2in, x2_dram, s_mx2), (h1in, h1_dram, s_mh1)):
                    sp.dma_start(dst[u][:, :, :].rearrange("p c d -> p (c d)"),
                                 src[bass.ds(p, 1), :, :].rearrange("o p f -> p (o f)")).then_inc(s[u], 16)

            def mstep(m, u, kb, kf):
                if kf:
                    mload(plus(m, 1), 1 - u)
                p = index(m if isinstance(m, int) else m[0] * 2 + m[1])
                sp.wait_ge(m_y, at(m, 3, 3))
                both = a["out"].rearrange("(q b) s d -> q b s d", b=2)[bass.ds(p, 1), :, :, :]\
                    .rearrange("q b s d -> (q b) s d")
                sp.dma_start(both[:, IMG:SEQ, :].rearrange("b t d -> t b d"), outb[u][:, 0:2, :])\
                    .then_inc(s_out[u], 16)
                for b in range(2):
                    sp.dma_start(both[b:b + 1, 0:IMG, :].rearrange("b t d -> t (b d)"),
                                 outb[u][IMG_AT[b]:IMG_AT[b] + IMG, 2, :]).then_inc(s_out[u], 16)

            mload(0, 0)
            run_mlp(sp, mstep)
            for u in range(2):
                sp.wait_ge(s_out[u], 48 * (PAIRS // 2))

        @block.gpsimd
        def _(pool):
            nc.gpsimd.memset(idf[:, :], 0.0).then_inc(s_idm, 1)
            nc.gpsimd.memset(idh[:, :], 0.0).then_inc(s_idm, 1)
            pool.wait_ge(s_idm, 2)
            for m in (idf, idh):
                nc.gpsimd.affine_select(out=m[:, :], in_=m[:, :], compare_op=ALU.not_equal, fill=1.0, base=0,
                                        pattern=[[-1, P]], channel_multiplier=1).then_inc(s_cst, 1)
            nc.gpsimd.memset(ones[:, :], 1.0).then_inc(s_cst, 1)
            nc.gpsimd.memset(neghalf[:, :], -0.5).then_inc(s_cst, 1)
            nc.gpsimd.memset(zeros[:, :], 0.0)
            for t in hin:
                nc.gpsimd.memset(t[:, 2, :], 0.0)
            nc.gpsimd.memset(negmax[:, :, :], 0.0)
            nc.gpsimd.memset(oT[:, :, :, :], 1.0)
            nc.gpsimd.memset(qs[:, :, :], 0.0)
            nc.gpsimd.memset(ks[:, :, :], 0.0)
            for t in v1:
                nc.gpsimd.memset(t[:, :, :, :], 0.0)
            nc.gpsimd.memset(ve[:, 0, 0:1], 0.0).then_inc(s_idm, 1)
            pool.wait_ge(s_idm, 3)
            nc.gpsimd.memset(ks[:, :, 2 * HD:2 * HD + 2], 1.0)
            for t in v1:
                last = nc.gpsimd.memset(t[:, :, :, HD:HD + 1], 1.0)
            last.then_inc(s_zero, 1)
            pool.wait_ge(s_zero, 1)

            def front(n, u, k):
                pool.wait_ge(s_ve, at(n, 2, 2))
                nc.gpsimd.tensor_tensor(rstd[:, :, :], ve[:, :, :],
                                        neghalf[:, 0:2 * C].rearrange("p (a c) -> p a c", a=2),
                                        ALU.pow).then_inc(s_rstd, 1)
                if k == "A":
                    pool.wait_ge(s_toksb, at(n, 1, 1))
                    pool.wait_ge(s_tokin[u], at_parity(n, 32))
                    base = hin[u]
                else:
                    pool.wait_ge(s_resx, resx_count(n))
                    base = resx[u]
                if later(n, 2):
                    pool.wait_ge(s_y, at(plus(n, -2), 3, 3))
                nc.gpsimd.tensor_tensor(resb[u][:, :, :], base[:, :, :],
                                        b_prj[k][:, :].unsqueeze(1).to_broadcast([P, C, D]),
                                        ALU.add).then_inc(s_resb, 1)
                if k == "A":
                    pool.wait_ge(s_hve, at(n, 1, 1))
                    nc.gpsimd.tensor_tensor(hrstd[:, :], hvar[:, :], neghalf[:, :], ALU.pow).then_inc(s_hrstd, 1)
                if later(n, 1):
                    pool.wait_ge(s_qmpe, at(plus(n, -1), 2, 2))
                zero = zeros[:, 0:1].unsqueeze(2).to_broadcast([P, C * H, 2])
                nc.gpsimd.tensor_tensor(qs[:, :, 2 * HD:2 * HD + 2], zero, zero, ALU.add).then_inc(s_mz, 1)

            def step(n, u, kb, kf):
                if kf:
                    front(plus(n, 1), 1 - u, kf)

            pool.wait_ge(s_wv, SETUP_STEPS)
            run_steps(pool, front, step)

            def mfront(m, u):
                pool.wait_ge(m_ve, at(m, 1, 1))
                nc.gpsimd.tensor_tensor(rstd[:, 0, :], ve[:, 0, :], neghalf[:, 0:C], ALU.pow).then_inc(m_rstd, 1)

            def mres(m, u, k):
                for s in (s_mx2, s_mh1):
                    pool.wait_ge(s[u], at_parity(m, 16))
                if later(m, 2):
                    pool.wait_ge(m_y, at(plus(m, -2), 3, 3))
                nc.gpsimd.tensor_tensor(resb[u][:, :, :], x2in[u][:, :, :], h1in[u][:, :, :],
                                        ALU.add).then_inc(m_r1, 1)
                pool.wait_ge(m_r1, at(m, 1, 1))
                nc.gpsimd.tensor_tensor(resb[u][:, :, :], resb[u][:, :, :],
                                        b_fc2[k][:, :].unsqueeze(1).to_broadcast([P, C, D]),
                                        ALU.add).then_inc(m_res, 1)

            def mstep(m, u, kb, kf):
                if kf:
                    mfront(plus(m, 1), 1 - u)
                mres(m, u, kb)

            mfront(0, 0)
            run_mlp(pool, mstep)

        @block.scalar
        def _(act):
            def front_tok(n, u, k):
                if k != "A":
                    return
                act.wait_ge(s_tokmm, at(n, 1, 1))
                if later(n, 2):
                    act.wait_ge(s_y, at(plus(n, -2), 3, 3))
                nc.scalar.activation(hin[u][0:IMG_END, 2, :], G1[0:IMG_END, 0:D], ACT.Copy).then_inc(s_toksb, 1)

            def front_x(n, u, k):
                act.wait_ge(s_xn, at(n, C, C))
                if later(n, 1):
                    act.wait_ge(s_xtpe, at(plus(n, -1), 2, 2))
                nc.scalar.activation(xs[:, :, 0:D], xn[:, :, :], ACT.Copy).then_inc(s_xhi, 1)
                act.wait_ge(s_xtpe, at(n, 2, 2))
                nc.scalar.activation(xt[:, 2, :, :].rearrange("p t n -> p (t n)"), half(TP[1])[:, 0:3 * P],
                                     ACT.Copy).then_inc(s_xt, 1)

            def front_sq(n, u, k):
                if k != "A":
                    return
                act.wait_ge(s_qk, at(n, C, C))
                nc.scalar.activation(sq[:, :, :, :], qk[:, :, :, :], ACT.Square).then_inc(s_sq, 1)

            def front_hi(n, u, k):
                if k == "A":
                    act.wait_ge(s_qkb, at(n, 1, 1))
                else:
                    act.wait_ge(s_qk, at(n, C, C))
                if later(n, 1):
                    act.wait_ge(s_ktpe, at(plus(n, -1), 2, 2))
                src = qk[:, 1, :, :].rearrange("p c (h d) -> p (c h) d", h=H).unsqueeze(2)
                nc.scalar.activation(ks[:, :, 0:2 * HD].rearrange("p g (r d) -> p g r d", r=2),
                                     src.to_broadcast([P, C * H, 2, HD]), ACT.Copy).then_inc(s_khi, 1)
                if later(n, 1):
                    act.wait_ge(s_qmpe, at(plus(n, -1), 2, 2))
                src = qk[:, 0, :, :].rearrange("p c (h d) -> p (c h) d", h=H).unsqueeze(2)
                dst = qs[:, :, :].rearrange("p g (r d) -> p g r d", d=HD)[:, :, 0:4:3, :]
                nc.scalar.activation(dst, src.to_broadcast([P, C * H, 2, HD]), ACT.Copy,
                                     scale=SCALE).then_inc(s_qhi, 1)

            def front_t(n, u, k):
                act.wait_ge(s_ktpe, at(n, 2, 2))
                nc.scalar.activation(kT[:, :, SEQ:2 * SEQ], item(1), ACT.Copy).then_inc(s_kt, 1)
                act.wait_ge(s_qtpe, at(n, 2, 2))
                nc.scalar.activation(qT[:, :, SEQ:2 * SEQ], item(1), ACT.Copy).then_inc(s_qt, 1)

            def exps(n):
                act.wait_ge(s_qmpe, at(n, 2, 2))
                nc.scalar.activation(qT[:, :, SEQ:2 * SEQ], item(1), ACT.Copy).then_inc(s_qm, 1)
                for t in range(TILES):
                    c, g = divmod(t, NHG)
                    rows = P if c < 2 else IMG_END
                    act.wait_ge(s_st, at(n, TILES, t + 1))
                    if t == 0:
                        if later(n, 1):
                            act.wait_ge(s_otpe, at(plus(n, -1), 2, 2))
                    nc.scalar.activation(probs[0:rows, c, heads_of(g), :],
                                         SE[t % 2][0:rows, 0:HG * SEQ].rearrange("p (h s) -> p h s", h=HG),
                                         ACT.Exp).then_inc(s_ex, 1)

            def outs(n):
                for b, bk in enumerate((G1, G0)):
                    act.wait_ge(s_otpe, at(n, 2, b + 1))
                    if b == 0:
                        if later(n, 1):
                            act.wait_ge(s_onpe, at(plus(n, -1), 3, 3))
                    o = bk[:, 0:3 * SEQ].rearrange("p (g s) -> p g s", g=3)
                    nc.scalar.activation(oT[:, :, b, :], o[:, :, 0:TXT], ACT.Copy).then_inc(s_ot, 1)
                    nc.scalar.activation(oT[:, :, 2, IMG_AT[b]:IMG_AT[b] + IMG], o[:, :, TXT:SEQ],
                                         ACT.Copy).then_inc(s_ot, 1)
                act.wait_ge(s_on, at(n, 3, 3))
                if later(n, 1):
                    act.wait_ge(s_oupe, at(plus(n, -1), 2, 2))
                nc.scalar.activation(os_[:, :, 0:D], on[:, :, :], ACT.Copy).then_inc(s_ohi, 1)
                act.wait_ge(s_oupe, at(n, 2, 2))
                nc.scalar.activation(ou[:, 2, :, :].rearrange("p t n -> p (t n)"), half(TP[1])[:, 0:3 * P],
                                     ACT.Copy).then_inc(s_ou, 1)

            def front(n, u, k):
                front_tok(n, u, k)
                front_x(n, u, k)
                front_sq(n, u, k)
                front_hi(n, u, k)
                front_t(n, u, k)

            def step(n, u, kb, kf):
                nx, v = plus(n, 1), 1 - u
                if kf:
                    front_tok(nx, v, kf)
                    front_x(nx, v, kf)
                    front_sq(nx, v, kf)
                exps(n)
                if kf:
                    front_hi(nx, v, kf)
                outs(n)
                if kf:
                    front_t(nx, v, kf)

            act.wait_ge(s_wv, SETUP_STEPS)
            run_steps(act, front, step)

            def mfront(m, u):
                act.wait_ge(m_xn, at(m, C, C))
                if later(m, 1):
                    act.wait_ge(m_tpe, at(plus(m, -1), 2, 2))
                nc.scalar.activation(xs[:, :, 0:D], xn[:, :, :], ACT.Copy).then_inc(m_hi, 1)

            def gelus(m, k, branch, row):
                for t in range(NHT):
                    act.wait_ge(m_f1, mlp_at(m, k, NHT, NHT * branch + t + 1))
                    if t == 0:
                        if later(m, 1) or branch >= 2:
                            act.wait_ge(m_f2, mlp_at(m, k, 3, 3 * (branch - 1)))
                    nc.scalar.activation(gT[branch_parity(m, k, branch)][:, t, :],
                                         bank[t % 3][:, 0:C * P], ACT.Gelu,
                                         bias=b_fc1[:, row, t:t + 1], scale=1.0 / WS).then_inc(m_g, 1)

            def mstep(m, u, kb, kf):
                for br, row in enumerate((0,) if kb == "L" else (1, 2, 3)):
                    gelus(m, kb, br, row)
                    if br == 0 and kf:
                        mfront(plus(m, 1), 1 - u)

            mfront(0, 0)
            run_mlp(act, mstep)

        @block.vector
        def _(dve):
            steps = [0]

            def link(ins):
                ins.then_inc(s_wv, 1)
                steps[0] += 1
                dve.wait_ge(s_wv, steps[0])

            V = nc.vector
            dve.wait_ge(s_cst, 4)
            dve.wait_ge(s_w, 16 * SETUP_LOADS)

            def split(dst, raw):
                link(V.tensor_copy(dst[:, 0, :], raw[:, 0, :]))
                link(V.tensor_copy(dst[:, 2, :], raw[:, 1, :]))
                link(V.tensor_tensor(dst[:, 1, :], raw[:, 0, :], dst[:, 0, :], ALU.subtract))
                link(V.memset(dst[LO:P, 3, :], 0.0))
                link(V.tensor_tensor(dst[0:LO, 3, :], raw[0:LO, 1, :], dst[0:LO, 2, :], ALU.subtract))

            def center(t, lanes):
                v = t.rearrange("p (g d) -> p g d", d=HD)
                link(V.tensor_reduce(out=gmean[:, lanes, :], in_=v, op=ALU.add, axis=AX_X))
                link(V.tensor_scalar(gmean[:, lanes, :], gmean[:, lanes, :], 1.0 / HD, None, ALU.mult))
                link(V.tensor_tensor(v, v, gmean[:, lanes, :].unsqueeze(2).to_broadcast([P, 24, HD]),
                                     ALU.subtract))

            banks = 0
            scr = sq[:, :, :, :].rearrange("p a c d -> p (a c d)").rearrange("p (t n) -> p t n", t=2)
            for i, (k, raw, norm) in enumerate((("A", raw_qkv[0], 0), ("L", raw_qkv[1], 2), ("S", raw_qkv[1], 4))):
                for t in range(2):
                    link(V.tensor_scalar(bwide[:, t, :], ones[:, :], bcol[:, norm + 1, t:t + 1], None, ALU.mult))
                V.memset(gmean[:, 0, 0:1], 0.0).then_inc(s_bw, 1)
                dve.wait_ge(s_bmm, i + 1)
                if k == "A":
                    for o, w, bk in ((0, 2 * D, G0), (2 * D, D, G1)):
                        link(V.tensor_tensor(b_qkv[k][:, o:o + w], b_qkv[k][:, o:o + w], bk[:, 0:w], ALU.add))
                    center(b_qkv[k][:, 0:2 * D], 0)
                else:
                    for o, w, bk in ((0, 2 * D, G0), (2 * D, D, G1)):
                        link(V.tensor_copy(b_qkv[k][:, o:o + w], bk[:, 0:w]))
                for t in range(2):
                    link(V.tensor_scalar(scr[:, t, :], raw[:, t, :], bcol[:, norm, t:t + 1], WS,
                                         ALU.mult, ALU.mult))
                    if k == "A":
                        center(scr[:, t, 0:2 * D], t)
                split(w_qkv[k], scr)
            scp = scr[:, :, 0:D]
            for k, raw in (("A", raw_prj[0]), ("L", raw_prj[1])):
                for t in range(2):
                    link(V.tensor_scalar(scp[:, t, :], raw[:, t, :], WS, None, ALU.mult))
                split(w_prj[k], scp)
            raw = scr[:, :, D:2 * D]
            for t in range(2):
                link(V.tensor_scalar(raw[:, t, :], scp[:, t, :], gw[:, 0:1], None, ALU.mult))
            for i in (1, 2):
                r = KEEP[i]
                link(V.scalar_tensor_tensor(out=raw[0:r, 0, 0:r], in0=scp[0:r, 0, 0:r], scalar=gw[0:r, i:i + 1],
                                            in1=raw[0:r, 0, 0:r], op0=ALU.mult, op1=ALU.add))
            split(w_prj["S"], raw)
            link(V.tensor_scalar(coef[:, :], ones[:, 0:1].to_broadcast([P, D]), gw[:, 0:1], None, ALU.mult))
            for i in (1, 2):
                link(V.tensor_scalar(coef[:, 0:KEEP[i]], coef[:, 0:KEEP[i]], gw[:, i:i + 1], None, ALU.add))
            link(V.tensor_tensor(b_prj["S"][:, :], b_prj["L"][:, :], coef[:, :], ALU.mult))
            link(V.tensor_tensor(b_fc2["S"][:, :], b_fc2["L"][:, :], coef[:, :], ALU.mult))
            for i in range(3):
                link(V.tensor_scalar(w_fc2[i + 1][:, :, :], w_fc2[0][:, :, 0:KEEP[i]], gw[:, i:i + 1], None,
                                     ALU.mult))
            dve.wait_ge(s_bmm, 4)
            link(V.tensor_tensor(b_fc1[:, :, :], G0[:, 0:4 * NHT].rearrange("p (a t) -> p a t", a=4),
                                 tmpw[:, 0, 0:NHT].unsqueeze(1).to_broadcast([P, 4, NHT]), ALU.add))
            for k, norm in (("L", 6), ("S", 8)):
                for t in range(2):
                    link(V.tensor_scalar(gT[0][:, 2 * t:2 * t + 2, :].rearrange("p a n -> p (a n)"),
                                         raw_fc1[:, t, :], bcol[:, norm, t:t + 1], WS, ALU.mult, ALU.mult))
                split(w_fc1[k], gT[0][:, 0:4, :].rearrange("p (t a) n -> p t (a n)", t=2))
            for i in range(2):
                for dst, o in ((gains, 0), (shifts, HD)):
                    link(V.tensor_copy(dst[:, i, :].rearrange("p (h d) -> p h d", h=H),
                                       tmpw[:, 1, 32 * i + o:32 * i + o + HD].unsqueeze(1)
                                       .to_broadcast([P, H, HD])))
            assert steps[0] == SETUP_STEPS, steps

            def norm_stats(n, h, s_st, s_ag, s_v, lanes):
                for c in range(C):
                    V.bn_stats(out=stats[:, c, :], in_=h[:, c, :]).then_inc(s_st, 1)
                dve.wait_ge(s_st, at(n, C, C))
                V.memset(carrier[:, :], 0.0)
                for c in range(C):
                    V.bn_aggr(out=mv[:, c, :], in_=stats[:, c, :]).then_inc(s_ag, 1)
                dve.wait_ge(s_ag, at(n, C, C))
                for lane, (mul, add) in enumerate(lanes):
                    V.tensor_scalar(ve[:, lane, :], mv[:, :, 1], mul, add, ALU.mult, ALU.add).then_inc(s_v, 1)

            def lows(n, src, dst, s_hi, s_lo):
                dve.wait_ge(s_hi, at(n, 1, 1))
                V.tensor_tensor(dst[:, :, D:2 * P], src[:, :, P:D], dst[:, :, P:D],
                                ALU.subtract).then_inc(s_lo, 1)
                V.tensor_tensor(dst[:, :, 2 * P:3 * P], src[:, :, 0:P], dst[:, :, 0:P],
                                ALU.subtract).then_inc(s_lo, 1)

            def front_x(n, u, k):
                if k == "A":
                    dve.wait_ge(s_tokin[u], at_parity(n, 32))
                    dve.wait_ge(s_toksb, at(n, 1, 1))
                else:
                    dve.wait_ge(s_hin[u], hin_count(n))
                norm_stats(n, hin[u], s_stats, s_aggr, s_ve, ((1.0 + EPS, EPS * EPS), (1.0, EPS)))
                dve.wait_ge(s_rstd, at(n, 1, 1))
                if later(n, 1):
                    dve.wait_ge(s_xhi, at(plus(n, -1), 1, 1))
                for c in range(C):
                    V.tensor_scalar(xn[:, c, :], hin[u][:, c, :], mv[:, c, 0:1], rstd[:, 0, c:c + 1],
                                    ALU.subtract, ALU.mult).then_inc(s_xn, 1)
                if k != "A":
                    for c in range(C):
                        V.tensor_scalar(resx[u][:, c, :], hin[u][:, c, :], mv[:, c, 0:1], rstd[:, 1, c:c + 1],
                                        ALU.subtract, ALU.mult).then_inc(s_resx, 1)
                dve.wait_ge(s_xn, at(n, C, C))
                lows(n, xn, xs, s_xhi, s_xlo)
                dve.wait_ge(s_xtpe, at(n, 2, 1))
                V.tensor_copy(xt[:, 0:2, :, :].rearrange("p c t n -> p (c t n)"),
                              half(TP[0])[:, 0:6 * P]).then_inc(s_xt, 1)

            def front_qk(n, u, k, c):
                dve.wait_ge(s_qkmm, at(n, C, c + 1))
                if c == 0:
                    if later(n, 1):
                        dve.wait_ge(s_qhi, at(plus(n, -1), 1, 1))
                V.scalar_tensor_tensor(out=qk[:, :, c, :],
                                       in0=G0[:, 0:2 * D].rearrange("p (a d) -> p a d", a=2), scalar=1.0 / WS,
                                       in1=b_qkv[k][:, 0:2 * D].rearrange("p (a d) -> p a d", a=2),
                                       op0=ALU.mult, op1=ALU.add).then_inc(s_qk, 1)

            def front_v(n, u, k):
                for c in range(C):
                    dve.wait_ge(s_vmm, at(n, 2, 1 if c < 2 else 2))
                    o = 0 if c != 1 else D
                    if c == 0:
                        if later(n, 2):
                            dve.wait_ge(s_otpe, at(plus(n, -2), 2, 2))
                    V.scalar_tensor_tensor(out=v1[u][:, c, :, 0:HD],
                                           in0=G1[:, o:o + D].rearrange("p (h d) -> p h d", h=H), scalar=1.0 / WS,
                                           in1=b_qkv[k][:, 2 * D:3 * D].rearrange("p (h d) -> p h d", h=H),
                                           op0=ALU.mult, op1=ALU.add).then_inc(s_v, 1)

            def front_norm(n, u, k):
                if k != "A":
                    return
                heads = qk[:, :, :, :].rearrange("p a c (h d) -> p (a c h) d", h=H)
                dve.wait_ge(s_sq, at(n, 1, 1))
                V.tensor_reduce(out=hvar[:, :], in_=sq[:, :, :, :].rearrange("p a c (h d) -> p (a c h) d", h=H),
                                op=ALU.add, axis=AX_X).then_inc(s_hvar, 1)
                dve.wait_ge(s_hvar, at(n, 1, 1))
                V.tensor_scalar(hvar[:, :], hvar[:, :], 1.0 / HD, EPS, ALU.mult, ALU.add).then_inc(s_hve, 1)
                dve.wait_ge(s_hrstd, at(n, 1, 1))
                V.tensor_tensor(heads, heads, hrstd[:, :].unsqueeze(2).to_broadcast([P, 72, HD]),
                                ALU.mult).then_inc(s_qkn, 1)
                dve.wait_ge(s_qkn, at(n, 1, 1))
                V.tensor_tensor(qk[:, :, :, :], qk[:, :, :, :],
                                gains[:, :, :].unsqueeze(2).to_broadcast([P, 2, C, D]),
                                ALU.mult).then_inc(s_qkg, 1)
                dve.wait_ge(s_qkg, at(n, 1, 1))
                V.tensor_tensor(qk[:, :, :, :], qk[:, :, :, :],
                                shifts[:, :, :].unsqueeze(2).to_broadcast([P, 2, C, D]),
                                ALU.add).then_inc(s_qkb, 1)

            def front_lo(n, u, k):
                dve.wait_ge(s_khi, at(n, 1, 1))
                V.tensor_tensor(ks[:, :, 3 * HD:4 * HD],
                                qk[:, 1, :, :].rearrange("p c (h d) -> p (c h) d", h=H), ks[:, :, 0:HD],
                                ALU.subtract).then_inc(s_klo, 1)
                dve.wait_ge(s_qhi, at(n, 1, 1))
                V.scalar_tensor_tensor(out=qs[:, :, HD:2 * HD],
                                       in0=qk[:, 0, :, :].rearrange("p c (h d) -> p (c h) d", h=H),
                                       scalar=SCALE, in1=qs[:, :, 0:HD], op0=ALU.mult,
                                       op1=ALU.subtract).then_inc(s_qlo, 1)

            def front_t(n, u, k):
                dve.wait_ge(s_ktpe, at(n, 2, 1))
                V.tensor_copy(kT[:, :, 0:SEQ], item(0)).then_inc(s_kt, 1)
                dve.wait_ge(s_qtpe, at(n, 2, 1))
                V.tensor_copy(qT[:, :, 0:SEQ], item(0)).then_inc(s_qt, 1)

            def maxes(n, tiles):
                for t in tiles:
                    c, g = divmod(t, NHG)
                    rows = P if c < 2 else IMG_END
                    dve.wait_ge(s_sc, at(n, TILES, t + 1))
                    V.tensor_reduce(out=negmax[0:rows, c, heads_of(g)],
                                    in_=SM[t % 2][0:rows, 0:HG * SEQ].rearrange("p (h s) -> p h s", h=HG),
                                    op=ALU.max, axis=AX_X, negate=True).then_inc(s_mx, 1)

            def shift(n):
                dve.wait_ge(s_mx, at(n, TILES, TILES))
                nm = negmax[:, :, :].rearrange("p c h -> p (c h)")
                V.tensor_copy(qs[:, :, 2 * HD], nm).then_inc(s_mh, 1)
                dve.wait_ge(s_mh, at(n, 1, 1))
                V.tensor_tensor(qs[:, :, 2 * HD + 1], nm, qs[:, :, 2 * HD], ALU.subtract).then_inc(s_ml, 1)
                dve.wait_ge(s_qmpe, at(n, 2, 1))
                V.tensor_copy(qT[:, :, 0:SEQ], item(0)).then_inc(s_qm, 1)

            def outs(n, u):
                for c in range(C):
                    bk = (G1, G0)[c % 2]
                    o = bk[:, 0:3 * P].rearrange("p (h e) -> p h e", h=H)
                    dve.wait_ge(s_onpe, at(n, C, c + 1))
                    V.reciprocal(rden[:, c, :], o[:, :, HD]).then_inc(s_rden, 1)
                    dve.wait_ge(s_rden, at(n, C, c + 1))
                    if c == 0:
                        if later(n, 1):
                            dve.wait_ge(s_ohi, at(plus(n, -1), 1, 1))
                    V.tensor_tensor(on[:, c, :].rearrange("p (h d) -> p h d", h=H), o[:, :, 0:HD],
                                    rden[:, c, :].unsqueeze(2).to_broadcast([P, H, HD]),
                                    ALU.mult).then_inc(s_on, 1)
                dve.wait_ge(s_on, at(n, C, C))
                lows(n, on, os_, s_ohi, s_olo)
                dve.wait_ge(s_oupe, at(n, 2, 1))
                V.tensor_copy(ou[:, 0:2, :, :].rearrange("p c t n -> p (c t n)"),
                              half(TP[0])[:, 0:6 * P]).then_inc(s_ou, 1)

            def adds(n, u):
                dve.wait_ge(s_resb, at(n, 1, 1))
                if later(n, 2):
                    dve.wait_ge(s_stored[u], at_parity(plus(n, -2), 16))
                for c in range(C):
                    bk, o = ((G0, 0), (G0, D), (G1, 0))[c]
                    dve.wait_ge(s_ype, at(n, 2, 1 if c < 2 else 2))
                    V.scalar_tensor_tensor(out=outb[u][:, c, :], in0=bk[:, o:o + D], scalar=1.0 / WS,
                                           in1=resb[u][:, c, :], op0=ALU.mult, op1=ALU.add).then_inc(s_y, 1)

            def front(n, u, k):
                front_x(n, u, k)
                for c in range(C):
                    front_qk(n, u, k, c)
                front_v(n, u, k)
                front_norm(n, u, k)
                front_lo(n, u, k)
                front_t(n, u, k)

            def step(n, u, kb, kf):
                nx, v = plus(n, 1), 1 - u
                maxes(n, range(0, 2))
                if kf:
                    front_x(nx, v, kf)
                maxes(n, range(2, 6))
                if kf:
                    front_qk(nx, v, kf, 0)
                maxes(n, range(6, 8))
                if kf:
                    front_qk(nx, v, kf, 1)
                maxes(n, range(8, 10))
                if kf:
                    front_qk(nx, v, kf, 2)
                maxes(n, range(10, 12))
                shift(n)
                if kf:
                    front_v(nx, v, kf)
                    front_norm(nx, v, kf)
                    front_lo(nx, v, kf)
                outs(n, u)
                adds(n, u)
                if kf:
                    front_t(nx, v, kf)

            dve.wait_ge(s_zero, 1)
            run_steps(dve, front, step)

            def mfront(m, u):
                dve.wait_ge(s_mx2[u], at_parity(m, 16))
                norm_stats(m, x2in[u], m_stats, m_aggr, m_ve, ((1.0, EPS),))
                dve.wait_ge(m_rstd, at(m, 1, 1))
                if later(m, 1):
                    dve.wait_ge(m_hi, at(plus(m, -1), 1, 1))
                for c in range(C):
                    V.tensor_scalar(xn[:, c, :], x2in[u][:, c, :], mv[:, c, 0:1], rstd[:, 0, c:c + 1],
                                    ALU.subtract, ALU.mult).then_inc(m_xn, 1)
                dve.wait_ge(m_xn, at(m, C, C))
                lows(m, xn, xs, m_hi, m_lo)

            def mT_copy(m, u):
                for i, (c0, cn) in enumerate(((0, 2), (2, 1))):
                    dve.wait_ge(m_tpe, at(m, 2, i + 1))
                    V.tensor_copy(mT[:, :, :].rearrange("p t (c n) -> p c t n", c=C)[:, c0:c0 + cn, :, :],
                                  half(TP[i])[:, 0:cn * 3 * P].rearrange("p (c t n) -> p c t n", c=cn, t=3))\
                        .then_inc(m_t, 1)

            def madds(m, u, k):
                dve.wait_ge(m_res, at(m, 1, 1))
                if later(m, 2):
                    dve.wait_ge(s_out[u], at_parity(plus(m, -2), 48))
                for c in range(C):
                    dve.wait_ge(m_f2, mlp_at(m, k, C, C * (0 if k == "L" else 2) + c + 1))
                    V.tensor_tensor(outb[u][:, c, :], yacc[c][:, 0:D], resb[u][:, c, :],
                                    ALU.add).then_inc(m_y, 1)

            yacc = (bank[3], G0, G1)

            def mstep(m, u, kb, kf):
                if kf:
                    mfront(plus(m, 1), 1 - u)
                    mT_copy(plus(m, 1), 1 - u)
                madds(m, u, kb)

            mfront(0, 0)
            mT_copy(0, 0)
            run_mlp(dve, mstep)

        @block.tensor
        def _(pe):
            mm = nc.tensor.matmul
            tr = nc.tensor.transpose

            pe.wait_ge(s_cst, 4)
            pe.wait_ge(s_w, 16 * SETUP_LOADS)
            for i, raw in enumerate((raw_qkv[0], raw_qkv[1], raw_qkv[1])):
                pe.wait_ge(s_bw, i + 1)
                for o, w, bk in ((0, 2 * D, G0), (2 * D, D, G1)):
                    mm(bk[:, 0:w], bwide[:, 0, :], raw[:, 0, o:o + w], start=True, stop=False)
                    last = mm(bk[:, 0:w], bwide[0:LO, 1, :], raw[0:LO, 1, o:o + w], start=False, stop=True)
                last.then_inc(s_bmm, 1)
            pe.wait_ge(s_wv, AFTER_QKV)
            for row, (norm, rows) in enumerate(((7, D), (9, KEEP[0]), (9, KEEP[1]), (9, KEEP[2]))):
                for t in range(NHT):
                    o = G0[:, row * NHT + t:row * NHT + t + 1]
                    first = min(rows, P)
                    last = mm(o, raw_fc1[0:first, 0, t * P:(t + 1) * P], bcol[0:first, norm, 0:1],
                              start=True, stop=rows <= P)
                    if rows > P:
                        last = mm(o, raw_fc1[0:LO, 1, t * P:(t + 1) * P], bcol[0:LO, norm, 1:2],
                                  start=False, stop=True)
            last.then_inc(s_bmm, 1)
            pe.wait_ge(s_wv, SETUP_STEPS)

            def split_product(out, lhs, w, cols):
                for i, (t, slot) in enumerate(((0, 0), (0, 1), (2, 0), (1, 2), (1, 3))):
                    last = mm(out, lhs[:, t, :], w[:, slot, cols], start=i == 0, stop=i == 4)
                return last

            def transposes_rows(src, s_inc, before):
                for i, chunks in enumerate(((0, 1), (2,))):
                    before(i)
                    for m, c in enumerate(chunks):
                        for t in range(3):
                            last = tr(half(TP[i])[:, (3 * m + t) * P:(3 * m + t + 1) * P],
                                      src[:, c, t * P:(t + 1) * P], idh[:, :])
                    last.then_inc(s_inc, 1)

            def transposes_heads(src, s_inc, before):
                for b in range(2):
                    before(b)
                    r = IMG_AT[b]
                    for t in range(NPT):
                        tr(half(TP[b])[:, t * SEQ:t * SEQ + TXT],
                           src[:, H * b + 2 * t:H * b + 2 * t + 2, :].rearrange("p a k -> p (a k)"), idh[:, :])
                    for t in range(NPT):
                        last = tr(half(TP[b])[:, t * SEQ + TXT:(t + 1) * SEQ],
                                  src[r:r + IMG, 2 * H + 2 * t:2 * H + 2 * t + 2, :]
                                  .rearrange("p a k -> p (a k)"), idh[r:r + IMG, r:r + IMG])
                    last.then_inc(s_inc, 1)

            def front_tok(n, u, k):
                if k != "A":
                    return
                pe.wait_ge(s_tokin[u], at_parity(n, 32))
                if later(n, 2):
                    pe.wait_ge(s_y, at(plus(n, -2), 3, 3))
                if later(n, 1):
                    pe.wait_ge(s_v, at(plus(n, -1), 3, 3))
                for t in range(2):
                    last = mm(G1[0:IMG_END, 0:D], patches[u][:, t, :], tokw[:, t, :], start=t == 0, stop=t == 1)
                last.then_inc(s_tokmm, 1)

            def front_x(n, u, k):
                pe.wait_ge(s_xlo, at(n, 2, 2))

                def before(i):
                    if later(n, 1):
                        pe.wait_ge(s_qt, at(plus(n, -1), 2, 2))
                transposes_rows(xs, s_xtpe, before)

            def front_qk(n, u, k, c):
                pe.wait_ge(s_xt, at(n, 2, 2))
                if c == 0:
                    if later(n, 2):
                        pe.wait_ge(s_y, at(plus(n, -2), 3, 2))
                if later(n, 1) or c:
                    pe.wait_ge(s_qk, at(n, C, c))
                split_product(G0[:, 0:2 * D], xt[:, c, :, :], w_qkv[k], slice(0, 2 * D)).then_inc(s_qkmm, 1)

            def front_v(n, u, k):
                if k == "A":
                    pe.wait_ge(s_toksb, at(n, 1, 1))
                if later(n, 2):
                    pe.wait_ge(s_y, at(plus(n, -2), 3, 3))
                for c in range(C):
                    if c == 2:
                        pe.wait_ge(s_v, at(n, C, 2))
                    o = 0 if c != 1 else D
                    last = split_product(G1[:, o:o + D], xt[:, c, :, :], w_qkv[k], slice(2 * D, 3 * D))
                    if c:
                        last.then_inc(s_vmm, 1)

            def front_t(n, u, k):
                pe.wait_ge(s_klo, at(n, 1, 1))

                def before_k(i):
                    if later(n, 1):
                        pe.wait_ge(s_ou, at(plus(n, -1), 2, 2))
                transposes_heads(ks, s_ktpe, before_k)
                pe.wait_ge(s_qlo, at(n, 1, 1))
                pe.wait_ge(s_mz, at(n, 1, 1))

                def before_q(i):
                    pe.wait_ge(s_kt, at(n, 2, 2))
                transposes_heads(qs, s_qtpe, before_q)

            def scores(n, tiles, bank_of, keys_out, s_free, s_done):
                lhs, rhs = (kT, qT) if keys_out else (qT, kT)
                for t in tiles:
                    c, g = divmod(t, NHG)
                    if later(n, 1) or t >= 2:
                        pe.wait_ge(s_free, at(n, TILES, t - 1))
                    for i in range(HG):
                        h = heads_of(g).start + 2 * i
                        r = BLK * (h % 2)
                        cols = slice(i * SEQ, (i + 1) * SEQ)
                        for b in ((c,) if c < 2 else (0, 1)):
                            o = SEQ * b + (0 if c < 2 else TXT)
                            m = TXT if c < 2 else BLK if b == 0 else IMG
                            if c == 2 and i == 0 and b == 0:
                                m = IMG_END
                            q = 0 if c < 2 else IMG_AT[b]
                            last = mm(bank_of[t % 2][q:q + m, cols], lhs[r:r + BLK, h // 2, o:o + m],
                                      rhs[r:r + BLK, h // 2, SEQ * b:SEQ * (b + 1)], start=True, stop=True)
                    last.then_inc(s_done, 1)

            def shift(n, kf):
                pe.wait_ge(s_ml, at(n, 1, 1))

                def before(b):
                    if kf:
                        pe.wait_ge(s_xt, at(plus(n, 1), 2, 2))
                transposes_heads(qs, s_qmpe, before)
                pe.wait_ge(s_qm, at(n, 2, 2))

            def pv(n, u, kf):
                pe.wait_ge(s_ex, at(n, TILES, TILES))
                for b, bk in enumerate((G1, G0)):
                    if kf and b == 0:
                        pe.wait_ge(s_v, at(plus(n, 1), C, C))
                    elif kf:
                        pe.wait_ge(s_qk, at(plus(n, 1), C, C))
                    for g in range(3):
                        o = slice(g * SEQ, (g + 1) * SEQ)
                        for h in range(4 * g, 4 * g + 4):
                            q = 32 * (h % 4)
                            mm(bk[q:q + 32, o], v1[u][:, b, h, :], probs[:, b, h, :], start=True, stop=False,
                               tile_position=(0, q))
                        r = IMG_AT[b]
                        for h in range(4 * g, 4 * g + 4):
                            q = 32 * (h % 4)
                            last = mm(bk[q:q + 32, o], v1[u][r:r + IMG, 2, h, :], probs[r:r + IMG, 2, h, :],
                                      start=False, stop=True, tile_position=(r, q))
                    last.then_inc(s_otpe, 1)

            def outs(n, k):
                for c in range(C):
                    bk = (G1, G0)[c % 2]
                    pe.wait_ge(s_ot, at(n, 4, 4))
                    if c == 2:
                        pe.wait_ge(s_on, at(n, C, 1))
                    for g in range(3):
                        last = tr(bk[:, g * P:(g + 1) * P], oT[:, g, c, :], idf[:, :])
                    last.then_inc(s_onpe, 1)
                pe.wait_ge(s_olo, at(n, 2, 2))

                def before(i):
                    pe.wait_ge(s_qm, at(n, 2, 2))
                transposes_rows(os_, s_oupe, before)
                pe.wait_ge(s_ou, at(n, 2, 2))
                for c in range(C):
                    bk, o = ((G0, 0), (G0, D), (G1, 0))[c]
                    if c == 0 or c == 2:
                        pe.wait_ge(s_on, at(n, C, 3))
                    last = split_product(bk[:, o:o + D], ou[:, c, :, :], w_prj[k], slice(0, D))
                    if c:
                        last.then_inc(s_ype, 1)

            def front(n, u, k):
                front_tok(n, u, k)
                front_x(n, u, k)
                for c in range(C):
                    front_qk(n, u, k, c)
                front_v(n, u, k)
                front_t(n, u, k)

            def step(n, u, kb, kf):
                nx, v = plus(n, 1), 1 - u
                pe.wait_ge(s_kt, at(n, 2, 2))
                pe.wait_ge(s_qt, at(n, 2, 2))
                scores(n, range(0, 4), SM, False, s_mx, s_sc)
                if kf:
                    front_tok(nx, v, kf)
                    front_x(nx, v, kf)
                scores(n, range(4, 8), SM, False, s_mx, s_sc)
                if kf:
                    front_qk(nx, v, kf, 0)
                scores(n, range(8, 10), SM, False, s_mx, s_sc)
                if kf:
                    front_qk(nx, v, kf, 1)
                scores(n, range(10, 12), SM, False, s_mx, s_sc)
                if kf:
                    front_qk(nx, v, kf, 2)
                shift(n, kf)
                scores(n, range(0, 6), SE, True, s_ex, s_st)
                if kf:
                    front_v(nx, v, kf)
                scores(n, range(6, 12), SE, True, s_ex, s_st)
                pv(n, u, kf)
                outs(n, kb)
                if kf:
                    front_t(nx, v, kf)

            pe.wait_ge(s_zero, 1)
            run_steps(pe, front, step)

            yacc = (bank[3], G0, G1)

            def mT_transposes(m):
                pe.wait_ge(m_lo, at(m, 2, 2))

                def before(i):
                    if later(m, 1):
                        pe.wait_ge(m_t, at(plus(m, -1), 2, 2))
                transposes_rows(xs, m_tpe, before)

            def fc1(m, k, br):
                rows = D if k == "L" else KEEP[br]
                for t in range(NHT):
                    if later(m, 1) or br or t >= 3:
                        pe.wait_ge(m_g, mlp_at(m, k, NHT, NHT * br + t - 2))
                    o = bank[t % 3][:, 0:C * P]
                    cols = slice(t * P, (t + 1) * P)
                    if rows == D:
                        passes = ((0, 0), (1, 0), (0, 2), (2, 1), (3, 1))
                        r = P
                    else:
                        passes = ((0, 0), (1, 0), (0, 2))
                        r = rows
                    for i, (slot, xtile) in enumerate(passes):
                        last = mm(o, w_fc1[k][0:r, slot, cols], mT[0:r, xtile, :], start=i == 0,
                                  stop=i == len(passes) - 1)
                    last.then_inc(m_f1, 1)

            def fc2(m, k, br, n_br):
                w = w_fc2[0 if k == "L" else br + 1]
                ch = D if k == "L" else KEEP[br]
                g = gT[branch_parity(m, k, br)]
                pe.wait_ge(m_g, mlp_at(m, k, NHT, NHT * (br + 1)))
                for c in range(C):
                    if br == 0:
                        if later(m, 1):
                            pe.wait_ge(m_y, at(plus(m, -1), C, c + 1))
                    for t in range(NHT):
                        last = mm(yacc[c][:, 0:ch], g[:, t, c * P:(c + 1) * P], w[:, t, :],
                                  start=br == 0 and t == 0, stop=br == n_br - 1 and t == NHT - 1,
                                  skip_group_check=True)
                    last.then_inc(m_f2, 1)

            def mstep(m, u, kb, kf):
                n_br = 1 if kb == "L" else 3
                fc1(m, kb, 0)
                for br in range(1, n_br):
                    fc1(m, kb, br)
                    fc2(m, kb, br - 1, n_br)
                if kf:
                    mT_transposes(plus(m, 1))
                fc2(m, kb, n_br - 1, n_br)
                if kf:
                    pe.wait_ge(m_t, at(plus(m, 1), 2, 2))

            mT_transposes(0)
            pe.wait_ge(m_t, 2)
            run_mlp(pe, mstep)


NORMS = ("attn_ln_g", "attn_ln_b", "ffn_n1l_g", "ffn_n1l_b", "ffn_n1s_g", "ffn_n1s_b",
         "ffn_n2l_g", "ffn_n2l_b", "ffn_n2s_g", "ffn_n2s_b")
SETUP_LOADS = 1 + 5 * 3 + 1 + 3 * len(NORMS) + 6 + 4
AFTER_QKV = 20 + 11 + 4
SETUP_STEPS = 92


def kernel(x, txt, L0_tok_W, L0_attn_ln_g, L0_attn_ln_b, L0_attn_W_qkv, L0_attn_b_qkv, L0_attn_qn_g,
           L0_attn_qn_b, L0_attn_kn_g, L0_attn_kn_b, L0_attn_W_proj, L0_attn_b_proj, L0_ffn_gumbel_weights,
           L0_ffn_n1l_g, L0_ffn_n1l_b, L0_ffn_n1s_g, L0_ffn_n1s_b, L0_ffn_w_qkv, L0_ffn_w_proj,
           L0_ffn_b_proj, L0_ffn_n2l_g, L0_ffn_n2l_b, L0_ffn_n2s_g, L0_ffn_n2s_b, L0_ffn_w_fc1,
           L0_ffn_b_fc1, L0_ffn_w_fc2, L0_ffn_b_fc2):
    import numpy as np
    import concourse.bacc as bacc
    from concourse.bass_utils import run_bass_kernel_spmd

    x = np.asarray(x)
    pt = x.reshape(PAIRS, 2, 6, 16, 6, 16).transpose(0, 3, 5, 1, 2, 4).reshape(PAIRS, 2, P, 2, IMG)
    padded = np.zeros((PAIRS, P, 2, IMG_END), np.float32)
    for b in range(2):
        padded[:, :, :, IMG_AT[b]:IMG_AT[b] + IMG] = pt[:, :, :, b, :].transpose(0, 2, 1, 3)
    arrays = dict(
        patches=padded, txt=txt, tokw=np.asarray(L0_tok_W).T,
        attn_ln_g=L0_attn_ln_g, attn_ln_b=L0_attn_ln_b, attn_W_qkv=L0_attn_W_qkv, attn_b_qkv=L0_attn_b_qkv,
        attn_qn_g=L0_attn_qn_g, attn_qn_b=L0_attn_qn_b, attn_kn_g=L0_attn_kn_g, attn_kn_b=L0_attn_kn_b,
        attn_W_proj=L0_attn_W_proj, attn_b_proj=L0_attn_b_proj, gumbel=L0_ffn_gumbel_weights,
        ffn_n1l_g=L0_ffn_n1l_g, ffn_n1l_b=L0_ffn_n1l_b, ffn_n1s_g=L0_ffn_n1s_g, ffn_n1s_b=L0_ffn_n1s_b,
        ffn_w_qkv=L0_ffn_w_qkv, ffn_w_proj=L0_ffn_w_proj, ffn_b_proj=L0_ffn_b_proj,
        ffn_n2l_g=L0_ffn_n2l_g, ffn_n2l_b=L0_ffn_n2l_b, ffn_n2s_g=L0_ffn_n2s_g, ffn_n2s_b=L0_ffn_n2s_b,
        ffn_w_fc1=L0_ffn_w_fc1, ffn_b_fc1=np.asarray(L0_ffn_b_fc1).reshape(NHT, P).T, ffn_w_fc2=L0_ffn_w_fc2, ffn_b_fc2=L0_ffn_b_fc2)
    arrays = {k: np.ascontiguousarray(v) for k, v in arrays.items()}
    nc = bacc.Bacc("TRN2", target_bir_lowering=False, num_devices=1)
    a = {k: nc.dram_tensor(f"in_{k}", v.shape, mybir.dt.from_np(v.dtype), kind="ExternalInput").ap()
         for k, v in arrays.items()}
    a["out"] = nc.dram_tensor("out_0", (BATCH, SEQ, D), F32, kind="ExternalOutput").ap()
    build(nc, a)
    r = run_bass_kernel_spmd(nc, [{f"in_{k}": v for k, v in arrays.items()}], core_ids=[0])
    return r.results[0]["out_0"]
```

```python
from contextlib import ExitStack

import concourse.bass as bass
from concourse import mybir

F32 = mybir.dt.float32
F16 = mybir.dt.float16
ALU = mybir.AluOpType
ACT = mybir.ActivationFunctionType
AX_X = mybir.AxisListType.X

BATCH = 64
IMG = 36
TXT = 128
SEQ = IMG + TXT
D = 192
H = 12
HD = D // H
PK = 256
HID = 4 * D
EPS = 1e-5
PAIRS = BATCH // 2
LARGE = PAIRS // 2
KEEP = (D, D // 2, D // 3)

P = 128
C = 3
IMG_AT = (0, 64)
IMG_END = 64 + IMG
KT = D // 2
LO = D - P
BLK = 64
NPT = H // 2
HG = 3
NHG = H // HG
TILES = C * NHG
WS = 64.0
SCALE = HD ** -0.5
NHT = HID // P


def heads_of(g):
    h = 2 * HG * (g // 2) + g % 2
    return slice(h, h + 2 * HG - 1, 2)


def at(n, per, k):
    if isinstance(n, int):
        return n * per + k
    j, off = n
    return j * (2 * per) + (off * per + k)


def later(n, k):
    return not isinstance(n, int) or n >= k


def build(nc, a):
    ctx = ExitStack()
    with ctx:
        def sb(name, shape, dt=F32):
            return ctx.enter_context(nc.sbuf_tensor(name, shape, dt))

        def sem(name):
            return ctx.enter_context(nc.semaphore(name))

        def sems(name):
            return [sem(f"{name}{i}") for i in range(2)]

        h1_dram = nc.dram_tensor("h1_scratch", [PAIRS, P, C * D], F32, kind="Internal").ap()
        x2_dram = nc.dram_tensor("x2_scratch", [PAIRS, P, C * D], F32, kind="Internal").ap()

        bank = [ctx.enter_context(nc.psum_tensor(f"bank{i}", [P, 512], F32)) for i in range(8)]
        SM = [bank[0], bank[1]]
        SE = [bank[2], bank[3]]
        TP = [bank[4], bank[5]]
        G0, G1 = bank[6], bank[7]

        QK_BANK = (G0, G1, G0)
        V_BANK = ((G1, 0), (G1, D), (G0, 0))
        O_BANK = (SE[0], SE[1], SE[0])
        Y_BANK = ((SE[1], 0), (SE[1], D), (SE[0], 0))

        def half(b):
            return b[:, :].bitcast(F16)

        def item(b):
            return half(TP[b])[:, 0:NPT * SEQ].rearrange("p (t s) -> p t s", t=NPT)

        idf = sb("idf", [P, P])
        idh = sb("idh", [P, P], F16)
        ones = sb("ones", [P, P])
        neghalf = sb("neghalf", [P, 72])
        tokw = sb("tokw", [P, 2, D])
        w_qkv = {k: sb(f"w_qkv_{k}", [P, 4, 3 * D], F16) for k in ("A", "L", "S")}
        w_prj = {k: sb(f"w_prj_{k}", [P, 4, D], F16) for k in ("A", "L", "S")}
        w_fc1 = {k: sb(f"w_fc1_{k}", [P, 4, HID], F16) for k in ("L", "S")}
        w_fc2 = [sb(f"w_fc2_{i}", [P, NHT, k]) for i, k in enumerate((D,) + KEEP)]
        b_qkv = {k: sb(f"b_qkv_{k}", [P, 3 * D]) for k in ("A", "L", "S")}
        b_prj = {k: sb(f"b_prj_{k}", [P, D]) for k in ("A", "L", "S")}
        b_fc1 = sb("b_fc1", [P, 4, NHT])
        b_fc2 = {k: sb(f"b_fc2_{k}", [P, D]) for k in ("L", "S")}
        gains = sb("gains", [P, 2, D])
        shifts = sb("shifts", [P, 2, D])
        gw = sb("gw", [P, 3])
        zeros = sb("zeros", [P, 1])
        carrier = sb("carrier", [P, 1])

        hin = [sb(f"hin{i}", [P, C, D]) for i in range(2)]
        patches = [sb(f"patches{i}", [P, 2, IMG_END]) for i in range(2)]
        stats = sb("stats", [P, C, 6])
        mv = sb("mv", [P, C, 2])
        ve = sb("ve", [P, 2, C])
        rstd = sb("rstd", [P, 2, C])
        xn = sb("xn", [P, C, D])
        xs = sb("xs", [P, C, 3 * P], F16)
        xt = sb("xt", [P, C, 3, P], F16)
        resx = [sb(f"resx{i}", [P, C, D]) for i in range(2)]
        resb = [sb(f"resb{i}", [P, C, D]) for i in range(2)]
        qk = sb("qk", [P, 2, C, D])
        sq = sb("sq", [P, 2, C, D])
        hvar = sb("hvar", [P, 72])
        hrstd = sb("hrstd", [P, 72])
        newton = sb("newton", [P, 72])
        qs = sb("qs", [P, C * H, BLK], F16)
        ks = sb("ks", [P, C * H, BLK], F16)
        qT = sb("qT", [P, NPT, 2 * SEQ], F16)
        kT = sb("kT", [P, NPT, 2 * SEQ], F16)
        v1 = [sb(f"v1_{i}", [P, C, H, 32]) for i in range(2)]
        negmax = sb("negmax", [P, C, H])
        probs = sb("probs", [P, C, H, SEQ])
        oT = sb("oT", [P, 3, C, P])
        rden = sb("rden", [P, C, H])
        on = sb("on", [P, C, D])
        os_ = sb("os_", [P, C, 3 * P], F16)
        ou = sb("ou", [P, C, 3, P], F16)
        outb = [sb(f"outb{i}", [P, C, D]) for i in range(2)]
        flat = probs[:, :, :, :].rearrange("p c h s -> p (c h s)")
        raw_qkv = [flat[:, i * 1152:(i + 1) * 1152].rearrange("p (t n) -> p t n", t=2) for i in range(2)]
        raw_prj = [flat[:, 2304 + i * 384:2304 + (i + 1) * 384].rearrange("p (t n) -> p t n", t=2)
                   for i in range(2)]
        raw_fc1 = flat[:, 3072:3072 + 1536].rearrange("p (t n) -> p t n", t=2)
        bcol = sb("bcol", [P, 10, 2])
        bwide = sb("bwide", [P, 2, P])
        gmean = sb("gmean", [P, 2, 24])
        tmpw = sb("tmpw", [P, 2, D])
        coef = sb("coef", [P, D])
        x2in = [sb(f"x2in{i}", [P, C, D]) for i in range(2)]
        h1in = [sb(f"h1in{i}", [P, C, D]) for i in range(2)]
        mT = sb("mT", [P, 3, C * P], F16)
        gT = [sb(f"gT{i}", [P, NHT, C * P]) for i in range(2)]

        s_w = sem("weights_loaded")
        s_cst = sem("constants_set")
        s_idm = sem("identity_cleared")
        s_zero = sem("padding_set")
        s_bw = sem("shift_widened")
        s_bmm = sem("shift_multiplied")
        s_wv = sem("setup_vector_step")
        s_tokin, s_hin = sems("tokens_loaded"), sems("h1_loaded")
        s_tokmm, s_toksb = sem("tok_multiplied"), sem("tok_copied")
        s_stats, s_aggr, s_ve, s_rstd = sem("stats"), sem("aggr"), sem("var_eps"), sem("rstd")
        s_xn, s_resx, s_resb = sem("xn_ready"), sem("resx_ready"), sem("resb_ready")
        s_xhi, s_xlo, s_xtpe, s_xt = sem("x_hi"), sem("x_lo"), sem("x_transposed"), sem("xT_ready")
        s_qkmm, s_qk, s_vmm, s_v = sem("qk_multiplied"), sem("qk_copied"), sem("v_multiplied"), sem("v_copied")
        s_sq, s_hvar, s_hve, s_hrstd = sem("qk_squared"), sem("head_var"), sem("head_var_eps"), sem("head_rstd")
        s_hln, s_newton = sem("head_log"), sem("head_rstd_refined")
        s_qkn, s_qkg, s_qkb = sem("qk_normed"), sem("qk_gained"), sem("qk_shifted")
        s_qhi, s_khi, s_qlo, s_klo, s_mz = sem("q_hi"), sem("k_hi"), sem("q_lo"), sem("k_lo"), sem("shift_cleared")
        s_ktpe, s_kt, s_qtpe, s_qt = sem("k_transposed"), sem("kT_ready"), sem("q_transposed"), sem("qT_ready")
        s_sc, s_mx = sem("scores_for_max"), sem("max_taken")
        s_mh, s_ml = sem("max_hi"), sem("max_lo")
        s_qmpe, s_qm = sem("shifted_q_transposed"), sem("shifted_qT_ready")
        s_st, s_ex = sem("scores_for_exp"), sem("exp_done")
        s_otpe, s_ot = sem("pv_multiplied"), sem("oT_copied")
        s_onpe, s_rden, s_on = sem("o_transposed"), sem("denominators"), sem("o_normed")
        s_ohi, s_olo, s_oupe, s_ou = sem("o_hi"), sem("o_lo"), sem("ou_transposed"), sem("ou_ready")
        s_ype, s_y = sem("proj_multiplied"), sem("attention_added")
        s_stored = sems("attention_stored")
        s_mx2, s_mh1 = sems("mlp_x2_loaded"), sems("mlp_h1_loaded")
        m_stats, m_aggr, m_ve, m_rstd = sem("m_stats"), sem("m_aggr"), sem("m_var_eps"), sem("m_rstd")
        m_xn, m_hi, m_lo, m_tpe, m_t = sem("m_xn"), sem("m_hi"), sem("m_lo"), sem("m_transposed"), sem("mT_ready")
        m_r1, m_res = sem("m_res_half"), sem("m_res")
        m_f1, m_g, m_f2, m_y = sem("fc1_multiplied"), sem("gelu_done"), sem("fc2_multiplied"), sem("mlp_added")
        s_out = sems("output_stored")

        block = ctx.enter_context(nc.Block())

        UNITS = 2 * PAIRS

        def kind(n):
            if not 0 <= n < UNITS:
                return None
            return "A" if n < PAIRS else "L" if n < PAIRS + LARGE else "S"

        def run_steps(eng, step):
            n = -2
            while n <= UNITS:
                kinds = [kind(n + i) for i in (-1, 0, 1, 2)]
                end = n
                while [kind(end + i) for i in (-1, 0, 1, 2)] == kinds:
                    end += 1
                pairs = (end - n) // 2
                if n < 2 or n % 2 or pairs < 2:
                    step(n, n % 2, *kinds)
                    n += 1
                else:
                    with eng.Fori(n // 2, n // 2 + pairs) as j:
                        for u in range(2):
                            step((j, u), u, *kinds)
                    n += 2 * pairs

        def plus(n, k):
            return n + k if isinstance(n, int) else (n[0], n[1] + k)

        def pair_of(n, k):
            base = 0 if k == "A" else PAIRS
            return n - base if isinstance(n, int) else n[0] * 2 + (n[1] - base)

        def run_mlp(eng, mstep):
            for lo, hi, k in ((0, LARGE, "L"), (LARGE, PAIRS, "S")):
                n = lo
                for _ in range(2):
                    mstep(n, n % 2, k, k)
                    n += 1
                with eng.Fori(n // 2, (hi - 2) // 2) as j:
                    for u in range(2):
                        mstep((j, u), u, k, k)
                mstep(hi - 2, 0, k, k)
                mstep(hi - 1, 1, k, "S" if hi < PAIRS else None)

        def at_parity(n, per):
            return per * (n // 2 + 1) if isinstance(n, int) else n[0] * per + per * (n[1] // 2 + 1)

        def hin_count(n):
            return 16 * (n // 2 + 1 - PAIRS // 2) if isinstance(n, int) else \
                n[0] * 16 + 16 * (n[1] // 2 + 1 - PAIRS // 2)

        def resx_count(n):
            return at(n, C, C - C * PAIRS)

        def mlp_at(m, k, per, c):
            return at(m, per, c) if k == "L" else at(m, 3 * per, c - 2 * per * LARGE)

        def branch_parity(m, k, br):
            off = m if isinstance(m, int) else m[1]
            return (off if k == "L" else off + br) % 2

        @block.sync
        def _(sp):
            n_w = 0

            def load(dst, src):
                sp.dma_start(dst, src).then_inc(s_w, 16)

            def load_rows(dst, src):
                load(dst[:, 0, :], src[0:P, :])
                load(dst[0:LO, 1, :], src[P:D, :])
                load(dst[LO:P, 1, :], src[P:D, :])

            load(tokw[:, :, :], a["tokw"].rearrange("(t p) n -> p t n", p=P))
            load_rows(raw_qkv[0], a["attn_W_qkv"])
            load_rows(raw_qkv[1], a["ffn_w_qkv"])
            load_rows(raw_prj[0], a["attn_W_proj"])
            load_rows(raw_prj[1], a["ffn_w_proj"])
            load_rows(raw_fc1, a["ffn_w_fc1"])
            load(w_fc2[0][:, :, :], a["ffn_w_fc2"].rearrange("(t p) n -> p t n", p=P))
            for i, name in enumerate(NORMS):
                for dst, src in ((bcol[:, i, 0:1], a[name][0:P]), (bcol[0:LO, i, 1:2], a[name][P:D]),
                                 (bcol[LO:P, i, 1:2], a[name][P:D])):
                    load(dst, src.rearrange("(p o) -> p o", o=1))
            load(b_qkv["A"][:, :], a["attn_b_qkv"].partition_broadcast(P))
            load(b_prj["A"][:, :], a["attn_b_proj"].partition_broadcast(P))
            load(b_prj["L"][:, :], a["ffn_b_proj"].partition_broadcast(P))
            load(b_fc2["L"][:, :], a["ffn_b_fc2"].partition_broadcast(P))
            load(tmpw[:, 0, 0:NHT], a["ffn_b_fc1"])
            load(gw[:, :], a["gumbel"].partition_broadcast(P))
            for i, (g, b) in enumerate((("attn_qn_g", "attn_qn_b"), ("attn_kn_g", "attn_kn_b"))):
                load(tmpw[:, 1, 32 * i:32 * i + HD], a[g].partition_broadcast(P))
                load(tmpw[:, 1, 32 * i + HD:32 * i + 2 * HD], a[b].partition_broadcast(P))

            def index(p):
                return p if isinstance(p, int) else sp.snap(p)

            def load_unit(n, u, k):
                p = index(pair_of(n, k))
                if later(n, 2):
                    sp.wait_ge(s_resb, at(plus(n, -2), 1, 1))
                if k == "A":
                    txt = a["txt"].rearrange("(q b) t d -> q t b d", b=2)[bass.ds(p, 1), :, :, :]\
                        .rearrange("q t b d -> t (q b) d")
                    sp.dma_start(hin[u][:, 0:2, :], txt).then_inc(s_tokin[u], 16)
                    xp = a["patches"][bass.ds(p, 1), :, :, :].rearrange("o p t n -> p (o t) n")
                    sp.dma_start(patches[u][:, :, :], xp).then_inc(s_tokin[u], 16)
                else:
                    src = h1_dram[bass.ds(p, 1), :, :].rearrange("o p f -> p (o f)")
                    sp.dma_start(hin[u][:, :, :].rearrange("p c d -> p (c d)"), src).then_inc(s_hin[u], 16)

            def store_unit(n, u, k):
                p = index(pair_of(n, k))
                sp.wait_ge(s_y, at(n, C, C))
                dst = h1_dram if k == "A" else x2_dram
                sp.dma_start(dst[bass.ds(p, 1), :, :].rearrange("o p f -> p (o f)"),
                             outb[u][:, :, :].rearrange("p c d -> p (c d)")).then_inc(s_stored[u], 16)

            def step(n, u, ko, kb, kf, kp):
                if kp:
                    load_unit(plus(n, 2), u, kp)
                if ko:
                    store_unit(plus(n, -1), 1 - u, ko)

            sp.wait_ge(s_zero, 1)
            run_steps(sp, step)

            for u in range(2):
                sp.wait_ge(s_stored[u], 16 * PAIRS)

            def mload(m, u):
                p = index(m if isinstance(m, int) else m[0] * 2 + m[1])
                for dst, src, s in ((x2in, x2_dram, s_mx2), (h1in, h1_dram, s_mh1)):
                    sp.dma_start(dst[u][:, :, :].rearrange("p c d -> p (c d)"),
                                 src[bass.ds(p, 1), :, :].rearrange("o p f -> p (o f)")).then_inc(s[u], 16)

            def mstep(m, u, kb, kf):
                if kf:
                    mload(plus(m, 1), 1 - u)
                p = index(m if isinstance(m, int) else m[0] * 2 + m[1])
                sp.wait_ge(m_y, at(m, 3, 3))
                both = a["out"].rearrange("(q b) s d -> q b s d", b=2)[bass.ds(p, 1), :, :, :]\
                    .rearrange("q b s d -> (q b) s d")
                sp.dma_start(both[:, IMG:SEQ, :].rearrange("b t d -> t b d"), outb[u][:, 0:2, :])\
                    .then_inc(s_out[u], 16)
                for b in range(2):
                    sp.dma_start(both[b:b + 1, 0:IMG, :].rearrange("b t d -> t (b d)"),
                                 outb[u][IMG_AT[b]:IMG_AT[b] + IMG, 2, :]).then_inc(s_out[u], 16)

            mload(0, 0)
            run_mlp(sp, mstep)
            for u in range(2):
                sp.wait_ge(s_out[u], 48 * (PAIRS // 2))

        @block.gpsimd
        def _(pool):
            nc.gpsimd.memset(idf[:, :], 0.0).then_inc(s_idm, 1)
            nc.gpsimd.memset(idh[:, :], 0.0).then_inc(s_idm, 1)
            pool.wait_ge(s_idm, 2)
            for m in (idf, idh):
                nc.gpsimd.affine_select(out=m[:, :], in_=m[:, :], compare_op=ALU.not_equal, fill=1.0, base=0,
                                        pattern=[[-1, P]], channel_multiplier=1).then_inc(s_cst, 1)
            nc.gpsimd.memset(ones[:, :], 1.0).then_inc(s_cst, 1)
            nc.gpsimd.memset(neghalf[:, :], -0.5).then_inc(s_cst, 1)
            nc.gpsimd.memset(zeros[:, :], 0.0)
            for t in hin:
                nc.gpsimd.memset(t[:, 2, :], 0.0)
            nc.gpsimd.memset(negmax[:, :, :], 0.0)
            nc.gpsimd.memset(oT[:, :, :, :], 1.0)
            nc.gpsimd.memset(qs[:, :, :], 0.0)
            nc.gpsimd.memset(ks[:, :, :], 0.0)
            for t in v1:
                nc.gpsimd.memset(t[:, :, :, :], 0.0)
            nc.gpsimd.memset(ve[:, 0, 0:1], 0.0).then_inc(s_idm, 1)
            pool.wait_ge(s_idm, 3)
            nc.gpsimd.memset(ks[:, :, 2 * HD:2 * HD + 2], 1.0)
            for t in v1:
                last = nc.gpsimd.memset(t[:, :, :, HD:HD + 1], 1.0)
            last.then_inc(s_zero, 1)
            pool.wait_ge(s_zero, 1)

            def power(n):
                pool.wait_ge(s_ve, at(n, 2, 2))
                nc.gpsimd.tensor_tensor(rstd[:, :, :], ve[:, :, :],
                                        neghalf[:, 0:2 * C].rearrange("p (a c) -> p a c", a=2),
                                        ALU.pow).then_inc(s_rstd, 1)

            def residual(n, u, k):
                pool.wait_ge(s_xn, at(n, C, C))
                if k == "A":
                    pool.wait_ge(s_tokin[u], at_parity(n, 32))
                    pool.wait_ge(s_toksb, at(n, 1, 1))
                else:
                    pool.wait_ge(s_resx, resx_count(n))
                if later(n, 2):
                    pool.wait_ge(s_y, at(plus(n, -2), C, C))
                nc.gpsimd.tensor_tensor(resb[u][:, :, :], (hin if k == "A" else resx)[u][:, :, :],
                                        b_prj[k][:, :].unsqueeze(1).to_broadcast([P, C, D]),
                                        ALU.add).then_inc(s_resb, 1)

            def clear_shift(n):
                if later(n, 1):
                    pool.wait_ge(s_qmpe, at(plus(n, -1), 2, 2))
                zero = zeros[:, 0:1].unsqueeze(2).to_broadcast([P, C * H, 2])
                nc.gpsimd.tensor_tensor(qs[:, :, 2 * HD:2 * HD + 2], zero, zero, ALU.add).then_inc(s_mz, 1)

            def step(n, u, ko, kb, kf, kp):
                if kf:
                    residual(plus(n, 1), 1 - u, kf)
                    clear_shift(plus(n, 1))
                if kp:
                    power(plus(n, 2))

            pool.wait_ge(s_wv, SETUP_STEPS)
            run_steps(pool, step)

            def mfront(m, u):
                pool.wait_ge(m_ve, at(m, 1, 1))
                nc.gpsimd.tensor_tensor(rstd[:, 0, :], ve[:, 0, :], neghalf[:, 0:C], ALU.pow).then_inc(m_rstd, 1)

            def mres(m, u, k):
                for s in (s_mx2, s_mh1):
                    pool.wait_ge(s[u], at_parity(m, 16))
                if later(m, 2):
                    pool.wait_ge(m_y, at(plus(m, -2), 3, 3))
                nc.gpsimd.tensor_tensor(resb[u][:, :, :], x2in[u][:, :, :], h1in[u][:, :, :],
                                        ALU.add).then_inc(m_r1, 1)
                pool.wait_ge(m_r1, at(m, 1, 1))
                nc.gpsimd.tensor_tensor(resb[u][:, :, :], resb[u][:, :, :],
                                        b_fc2[k][:, :].unsqueeze(1).to_broadcast([P, C, D]),
                                        ALU.add).then_inc(m_res, 1)

            def mstep(m, u, kb, kf):
                if kf:
                    mfront(plus(m, 1), 1 - u)
                mres(m, u, kb)

            mfront(0, 0)
            run_mlp(pool, mstep)

        @block.scalar
        def _(act):
            def tok_copy(n, u, k):
                if k != "A":
                    return
                act.wait_ge(s_tokmm, at(n, 1, 1))
                if later(n, 2):
                    act.wait_ge(s_xn, at(plus(n, -2), C, C))
                    act.wait_ge(s_resb, at(plus(n, -2), 1, 1))
                nc.scalar.activation(hin[u][0:IMG_END, 2, :], G1[0:IMG_END, 0:D], ACT.Copy).then_inc(s_toksb, 1)

            def x_high(n):
                act.wait_ge(s_xn, at(n, C, C))
                if later(n, 1):
                    act.wait_ge(s_xtpe, at(plus(n, -1), 2, 2))
                nc.scalar.activation(xs[:, :, 0:D], xn[:, :, :], ACT.Copy).then_inc(s_xhi, 1)

            def rows_copy(n, dst, s_pe, s_done, i):
                c0, cn = ((0, 2), (2, 1))[i]
                act.wait_ge(s_pe, at(n, 2, i + 1))
                nc.scalar.activation(dst[:, c0:c0 + cn, :, :].rearrange("p c t n -> p (c t n)"),
                                     half(TP[i])[:, 0:3 * cn * P], ACT.Copy).then_inc(s_done, 1)

            def qk_square(n, k):
                if k != "A":
                    return
                act.wait_ge(s_qk, at(n, C, C))
                nc.scalar.activation(sq[:, :, :, :], qk[:, :, :, :], ACT.Square).then_inc(s_sq, 1)

            def head_power(n, k):
                if k != "A":
                    return
                act.wait_ge(s_hve, at(n, 1, 1))
                nc.scalar.activation(hrstd[:, :], hvar[:, :], ACT.Ln).then_inc(s_hln, 1)
                act.wait_ge(s_hln, at(n, 1, 1))
                nc.scalar.activation(hrstd[:, :], hrstd[:, :], ACT.Exp, scale=-0.5).then_inc(s_hrstd, 1)

            def qk_high(n, k):
                if k == "A":
                    act.wait_ge(s_qkb, at(n, 1, 1))
                else:
                    act.wait_ge(s_qk, at(n, C, C))
                if later(n, 1):
                    act.wait_ge(s_ktpe, at(plus(n, -1), 2, 2))
                src = qk[:, 1, :, :].rearrange("p c (h d) -> p (c h) d", h=H).unsqueeze(2)
                nc.scalar.activation(ks[:, :, 0:2 * HD].rearrange("p g (r d) -> p g r d", r=2),
                                     src.to_broadcast([P, C * H, 2, HD]), ACT.Copy).then_inc(s_khi, 1)
                if later(n, 1):
                    act.wait_ge(s_qmpe, at(plus(n, -1), 2, 2))
                src = qk[:, 0, :, :].rearrange("p c (h d) -> p (c h) d", h=H).unsqueeze(2)
                dst = qs[:, :, :].rearrange("p g (r d) -> p g r d", d=HD)[:, :, 0:4:3, :]
                nc.scalar.activation(dst, src.to_broadcast([P, C * H, 2, HD]), ACT.Copy,
                                     scale=SCALE).then_inc(s_qhi, 1)

            def heads_copy(n, dst, s_pe, s_done):
                act.wait_ge(s_pe, at(n, 2, 2))
                nc.scalar.activation(dst[:, :, SEQ:2 * SEQ], item(1), ACT.Copy).then_inc(s_done, 1)

            def exps(n, tiles):
                for t in tiles:
                    c, g = divmod(t, NHG)
                    rows = P if c < 2 else IMG_END
                    act.wait_ge(s_st, at(n, TILES, t + 1))
                    if t == 0 and later(n, 1):
                        act.wait_ge(s_otpe, at(plus(n, -1), 2, 2))
                    nc.scalar.activation(probs[0:rows, c, heads_of(g), :],
                                         SE[t % 2][0:rows, 0:HG * SEQ].rearrange("p (h s) -> p h s", h=HG),
                                         ACT.Exp).then_inc(s_ex, 1)

            def o_copy(n):
                for b in range(2):
                    act.wait_ge(s_otpe, at(n, 2, b + 1))
                    if b == 0 and later(n, 1):
                        act.wait_ge(s_onpe, at(plus(n, -1), C, C))
                    o = SM[b][:, 0:3 * SEQ].rearrange("p (g s) -> p g s", g=3)
                    nc.scalar.activation(oT[:, :, b, :], o[:, :, 0:TXT], ACT.Copy).then_inc(s_ot, 1)
                    nc.scalar.activation(oT[:, :, 2, IMG_AT[b]:IMG_AT[b] + IMG], o[:, :, TXT:SEQ],
                                         ACT.Copy).then_inc(s_ot, 1)

            def o_high(n):
                act.wait_ge(s_on, at(n, C, C))
                if later(n, 1):
                    act.wait_ge(s_oupe, at(plus(n, -1), 2, 2))
                nc.scalar.activation(os_[:, :, 0:D], on[:, :, :], ACT.Copy).then_inc(s_ohi, 1)

            def step(n, u, ko, kb, kf, kp):
                prev, nx, n2 = plus(n, -1), plus(n, 1), plus(n, 2)
                if kf:
                    rows_copy(nx, xt, s_xtpe, s_xt, 0)
                    rows_copy(nx, xt, s_xtpe, s_xt, 1)
                if ko:
                    o_high(prev)
                    rows_copy(prev, ou, s_oupe, s_ou, 0)
                    rows_copy(prev, ou, s_oupe, s_ou, 1)
                if kf:
                    qk_square(nx, kf)
                if kb:
                    heads_copy(n, qT, s_qmpe, s_qm)
                    exps(n, range(0, 4))
                if kf:
                    head_power(nx, kf)
                if kb:
                    exps(n, range(4, TILES))
                if kf:
                    qk_high(nx, kf)
                if kp:
                    tok_copy(n2, u, kp)
                if kb:
                    o_copy(n)
                if kf:
                    heads_copy(nx, kT, s_ktpe, s_kt)
                if kp:
                    x_high(n2)
                if kf:
                    heads_copy(nx, qT, s_qtpe, s_qt)

            act.wait_ge(s_wv, SETUP_STEPS)
            run_steps(act, step)

            def mfront(m, u):
                act.wait_ge(m_xn, at(m, C, C))
                if later(m, 1):
                    act.wait_ge(m_tpe, at(plus(m, -1), 2, 2))
                nc.scalar.activation(xs[:, :, 0:D], xn[:, :, :], ACT.Copy).then_inc(m_hi, 1)

            def gelus(m, k, branch, row):
                for t in range(NHT):
                    act.wait_ge(m_f1, mlp_at(m, k, NHT, NHT * branch + t + 1))
                    if t == 0:
                        if later(m, 1) or branch >= 2:
                            act.wait_ge(m_f2, mlp_at(m, k, 3, 3 * (branch - 1)))
                    nc.scalar.activation(gT[branch_parity(m, k, branch)][:, t, :],
                                         bank[t % 3][:, 0:C * P], ACT.Gelu,
                                         bias=b_fc1[:, row, t:t + 1], scale=1.0 / WS).then_inc(m_g, 1)

            def mstep(m, u, kb, kf):
                for br, row in enumerate((0,) if kb == "L" else (1, 2, 3)):
                    gelus(m, kb, br, row)
                    if br == 0 and kf:
                        mfront(plus(m, 1), 1 - u)

            mfront(0, 0)
            run_mlp(act, mstep)

        @block.vector
        def _(dve):
            steps = [0]

            def link(ins):
                ins.then_inc(s_wv, 1)
                steps[0] += 1
                dve.wait_ge(s_wv, steps[0])

            V = nc.vector
            dve.wait_ge(s_cst, 4)
            dve.wait_ge(s_w, 16 * SETUP_LOADS)

            def split(dst, raw):
                link(V.tensor_copy(dst[:, 0, :], raw[:, 0, :]))
                link(V.tensor_copy(dst[:, 2, :], raw[:, 1, :]))
                link(V.tensor_tensor(dst[:, 1, :], raw[:, 0, :], dst[:, 0, :], ALU.subtract))
                link(V.memset(dst[LO:P, 3, :], 0.0))
                link(V.tensor_tensor(dst[0:LO, 3, :], raw[0:LO, 1, :], dst[0:LO, 2, :], ALU.subtract))

            def center(t, lanes):
                v = t.rearrange("p (g d) -> p g d", d=HD)
                link(V.tensor_reduce(out=gmean[:, lanes, :], in_=v, op=ALU.add, axis=AX_X))
                link(V.tensor_scalar(gmean[:, lanes, :], gmean[:, lanes, :], 1.0 / HD, None, ALU.mult))
                link(V.tensor_tensor(v, v, gmean[:, lanes, :].unsqueeze(2).to_broadcast([P, 24, HD]),
                                     ALU.subtract))

            banks = 0
            scr = sq[:, :, :, :].rearrange("p a c d -> p (a c d)").rearrange("p (t n) -> p t n", t=2)
            for i, (k, raw, norm) in enumerate((("A", raw_qkv[0], 0), ("L", raw_qkv[1], 2), ("S", raw_qkv[1], 4))):
                for t in range(2):
                    link(V.tensor_scalar(bwide[:, t, :], ones[:, :], bcol[:, norm + 1, t:t + 1], None, ALU.mult))
                V.memset(gmean[:, 0, 0:1], 0.0).then_inc(s_bw, 1)
                dve.wait_ge(s_bmm, i + 1)
                if k == "A":
                    for o, w, bk in ((0, 2 * D, G0), (2 * D, D, G1)):
                        link(V.tensor_tensor(b_qkv[k][:, o:o + w], b_qkv[k][:, o:o + w], bk[:, 0:w], ALU.add))
                    center(b_qkv[k][:, 0:2 * D], 0)
                else:
                    for o, w, bk in ((0, 2 * D, G0), (2 * D, D, G1)):
                        link(V.tensor_copy(b_qkv[k][:, o:o + w], bk[:, 0:w]))
                for t in range(2):
                    link(V.tensor_scalar(scr[:, t, :], raw[:, t, :], bcol[:, norm, t:t + 1], WS,
                                         ALU.mult, ALU.mult))
                    if k == "A":
                        center(scr[:, t, 0:2 * D], t)
                split(w_qkv[k], scr)
            scp = scr[:, :, 0:D]
            for k, raw in (("A", raw_prj[0]), ("L", raw_prj[1])):
                for t in range(2):
                    link(V.tensor_scalar(scp[:, t, :], raw[:, t, :], WS, None, ALU.mult))
                split(w_prj[k], scp)
            raw = scr[:, :, D:2 * D]
            for t in range(2):
                link(V.tensor_scalar(raw[:, t, :], scp[:, t, :], gw[:, 0:1], None, ALU.mult))
            for i in (1, 2):
                r = KEEP[i]
                link(V.scalar_tensor_tensor(out=raw[0:r, 0, 0:r], in0=scp[0:r, 0, 0:r], scalar=gw[0:r, i:i + 1],
                                            in1=raw[0:r, 0, 0:r], op0=ALU.mult, op1=ALU.add))
            split(w_prj["S"], raw)
            link(V.tensor_scalar(coef[:, :], ones[:, 0:1].to_broadcast([P, D]), gw[:, 0:1], None, ALU.mult))
            for i in (1, 2):
                link(V.tensor_scalar(coef[:, 0:KEEP[i]], coef[:, 0:KEEP[i]], gw[:, i:i + 1], None, ALU.add))
            link(V.tensor_tensor(b_prj["S"][:, :], b_prj["L"][:, :], coef[:, :], ALU.mult))
            link(V.tensor_tensor(b_fc2["S"][:, :], b_fc2["L"][:, :], coef[:, :], ALU.mult))
            for i in range(3):
                link(V.tensor_scalar(w_fc2[i + 1][:, :, :], w_fc2[0][:, :, 0:KEEP[i]], gw[:, i:i + 1], None,
                                     ALU.mult))
            dve.wait_ge(s_bmm, 4)
            link(V.tensor_tensor(b_fc1[:, :, :], G0[:, 0:4 * NHT].rearrange("p (a t) -> p a t", a=4),
                                 tmpw[:, 0, 0:NHT].unsqueeze(1).to_broadcast([P, 4, NHT]), ALU.add))
            for k, norm in (("L", 6), ("S", 8)):
                for t in range(2):
                    link(V.tensor_scalar(gT[0][:, 2 * t:2 * t + 2, :].rearrange("p a n -> p (a n)"),
                                         raw_fc1[:, t, :], bcol[:, norm, t:t + 1], WS, ALU.mult, ALU.mult))
                split(w_fc1[k], gT[0][:, 0:4, :].rearrange("p (t a) n -> p t (a n)", t=2))
            for i in range(2):
                for dst, o in ((gains, 0), (shifts, HD)):
                    link(V.tensor_copy(dst[:, i, :].rearrange("p (h d) -> p h d", h=H),
                                       tmpw[:, 1, 32 * i + o:32 * i + o + HD].unsqueeze(1)
                                       .to_broadcast([P, H, HD])))
            assert steps[0] == SETUP_STEPS, steps

            def norm_stats(n, h, s_st, s_ag, s_v, lanes):
                for c in range(C):
                    V.bn_stats(out=stats[:, c, :], in_=h[:, c, :]).then_inc(s_st, 1)
                dve.wait_ge(s_st, at(n, C, C))
                V.memset(carrier[:, :], 0.0)
                for c in range(C):
                    V.bn_aggr(out=mv[:, c, :], in_=stats[:, c, :]).then_inc(s_ag, 1)
                dve.wait_ge(s_ag, at(n, C, C))
                for lane, (mul, add) in enumerate(lanes):
                    V.tensor_scalar(ve[:, lane, :], mv[:, :, 1], mul, add, ALU.mult, ALU.add).then_inc(s_v, 1)

            def lows(n, src, dst, s_hi, s_lo):
                dve.wait_ge(s_hi, at(n, 1, 1))
                V.tensor_tensor(dst[:, :, D:2 * P], src[:, :, P:D], dst[:, :, P:D],
                                ALU.subtract).then_inc(s_lo, 1)
                V.tensor_tensor(dst[:, :, 2 * P:3 * P], src[:, :, 0:P], dst[:, :, 0:P],
                                ALU.subtract).then_inc(s_lo, 1)

            def x_stats(n, u, k):
                if k == "A":
                    dve.wait_ge(s_tokin[u], at_parity(n, 32))
                    dve.wait_ge(s_toksb, at(n, 1, 1))
                else:
                    dve.wait_ge(s_hin[u], hin_count(n))
                norm_stats(n, hin[u], s_stats, s_aggr, s_ve, ((1.0 + EPS, EPS * EPS), (1.0, EPS)))

            def x_norm(n, u, k):
                dve.wait_ge(s_rstd, at(n, 1, 1))
                if later(n, 1):
                    dve.wait_ge(s_xhi, at(plus(n, -1), 1, 1))
                for c in range(C):
                    V.tensor_scalar(xn[:, c, :], hin[u][:, c, :], mv[:, c, 0:1], rstd[:, 0, c:c + 1],
                                    ALU.subtract, ALU.mult).then_inc(s_xn, 1)
                if k != "A":
                    dve.wait_ge(s_resb, at(plus(n, -2), 1, 1))
                    for c in range(C):
                        V.tensor_scalar(resx[u][:, c, :], hin[u][:, c, :], mv[:, c, 0:1], rstd[:, 1, c:c + 1],
                                        ALU.subtract, ALU.mult).then_inc(s_resx, 1)
                dve.wait_ge(s_xn, at(n, C, C))

            def qk_copy(n, k, c):
                dve.wait_ge(s_qkmm, at(n, C, c + 1))
                if c == 0 and later(n, 1):
                    dve.wait_ge(s_qhi, at(plus(n, -1), 1, 1))
                V.scalar_tensor_tensor(out=qk[:, :, c, :],
                                       in0=QK_BANK[c][:, 0:2 * D].rearrange("p (a d) -> p a d", a=2),
                                       scalar=1.0 / WS,
                                       in1=b_qkv[k][:, 0:2 * D].rearrange("p (a d) -> p a d", a=2),
                                       op0=ALU.mult, op1=ALU.add).then_inc(s_qk, 1)

            def v_copy(n, u, k, chunks):
                for c in chunks:
                    bk, o = V_BANK[c]
                    dve.wait_ge(s_vmm, at(n, 2, 1 if c < 2 else 2))
                    if c == 0 and later(n, 2):
                        dve.wait_ge(s_otpe, at(plus(n, -2), 2, 2))
                    V.scalar_tensor_tensor(out=v1[u][:, c, :, 0:HD],
                                           in0=bk[:, o:o + D].rearrange("p (h d) -> p h d", h=H), scalar=1.0 / WS,
                                           in1=b_qkv[k][:, 2 * D:3 * D].rearrange("p (h d) -> p h d", h=H),
                                           op0=ALU.mult, op1=ALU.add).then_inc(s_v, 1)

            def head_variance(n, k):
                if k != "A":
                    return
                dve.wait_ge(s_sq, at(n, 1, 1))
                V.tensor_reduce(out=hvar[:, :], in_=sq[:, :, :, :].rearrange("p a c (h d) -> p (a c h) d", h=H),
                                op=ALU.add, axis=AX_X).then_inc(s_hvar, 1)
                dve.wait_ge(s_hvar, at(n, 1, 1))
                V.tensor_scalar(hvar[:, :], hvar[:, :], 1.0 / HD, EPS, ALU.mult, ALU.add).then_inc(s_hve, 1)

            def head_norm(n, k):
                if k != "A":
                    return
                heads = qk[:, :, :, :].rearrange("p a c (h d) -> p (a c h) d", h=H)
                dve.wait_ge(s_hrstd, at(n, 1, 1))
                V.scalar_tensor_tensor(out=newton[:, :], in0=hrstd[:, :], scalar=-0.5, in1=hrstd[:, :],
                                       op0=ALU.mult, op1=ALU.mult).then_inc(s_newton, 1)
                dve.wait_ge(s_newton, at(n, 3, 1))
                V.tensor_tensor(newton[:, :], newton[:, :], hvar[:, :], ALU.mult).then_inc(s_newton, 1)
                dve.wait_ge(s_newton, at(n, 3, 2))
                V.scalar_tensor_tensor(out=hrstd[:, :], in0=newton[:, :], scalar=1.5, in1=hrstd[:, :],
                                       op0=ALU.add, op1=ALU.mult).then_inc(s_newton, 1)
                dve.wait_ge(s_newton, at(n, 3, 3))
                V.tensor_tensor(heads, heads, hrstd[:, :].unsqueeze(2).to_broadcast([P, 72, HD]),
                                ALU.mult).then_inc(s_qkn, 1)
                dve.wait_ge(s_qkn, at(n, 1, 1))
                V.tensor_tensor(qk[:, :, :, :], qk[:, :, :, :],
                                gains[:, :, :].unsqueeze(2).to_broadcast([P, 2, C, D]),
                                ALU.mult).then_inc(s_qkg, 1)
                dve.wait_ge(s_qkg, at(n, 1, 1))
                V.tensor_tensor(qk[:, :, :, :], qk[:, :, :, :],
                                shifts[:, :, :].unsqueeze(2).to_broadcast([P, 2, C, D]),
                                ALU.add).then_inc(s_qkb, 1)

            def qk_low(n):
                dve.wait_ge(s_khi, at(n, 1, 1))
                V.tensor_tensor(ks[:, :, 3 * HD:4 * HD],
                                qk[:, 1, :, :].rearrange("p c (h d) -> p (c h) d", h=H), ks[:, :, 0:HD],
                                ALU.subtract).then_inc(s_klo, 1)
                dve.wait_ge(s_qhi, at(n, 1, 1))
                V.scalar_tensor_tensor(out=qs[:, :, HD:2 * HD],
                                       in0=qk[:, 0, :, :].rearrange("p c (h d) -> p (c h) d", h=H),
                                       scalar=SCALE, in1=qs[:, :, 0:HD], op0=ALU.mult,
                                       op1=ALU.subtract).then_inc(s_qlo, 1)

            def heads_copy(n, dst, s_pe, s_done):
                dve.wait_ge(s_pe, at(n, 2, 1))
                V.tensor_copy(dst[:, :, 0:SEQ], item(0)).then_inc(s_done, 1)

            def maxes(n, tiles):
                for t in tiles:
                    c, g = divmod(t, NHG)
                    rows = P if c < 2 else IMG_END
                    dve.wait_ge(s_sc, at(n, TILES, t + 1))
                    V.tensor_reduce(out=negmax[0:rows, c, heads_of(g)],
                                    in_=SM[t % 2][0:rows, 0:HG * SEQ].rearrange("p (h s) -> p h s", h=HG),
                                    op=ALU.max, axis=AX_X, negate=True).then_inc(s_mx, 1)

            def shift(n):
                dve.wait_ge(s_mx, at(n, TILES, TILES))
                nm = negmax[:, :, :].rearrange("p c h -> p (c h)")
                V.tensor_copy(qs[:, :, 2 * HD], nm).then_inc(s_mh, 1)
                dve.wait_ge(s_mh, at(n, 1, 1))
                V.tensor_tensor(qs[:, :, 2 * HD + 1], nm, qs[:, :, 2 * HD], ALU.subtract).then_inc(s_ml, 1)

            def o_norm(n, c):
                o = O_BANK[c][:, 0:3 * P].rearrange("p (h e) -> p h e", h=H)
                dve.wait_ge(s_onpe, at(n, C, c + 1))
                V.reciprocal(rden[:, c, :], o[:, :, HD]).then_inc(s_rden, 1)
                dve.wait_ge(s_rden, at(n, C, c + 1))
                if c == 0 and later(n, 1):
                    dve.wait_ge(s_ohi, at(plus(n, -1), 1, 1))
                V.tensor_tensor(on[:, c, :].rearrange("p (h d) -> p h d", h=H), o[:, :, 0:HD],
                                rden[:, c, :].unsqueeze(2).to_broadcast([P, H, HD]),
                                ALU.mult).then_inc(s_on, 1)

            def adds(n, u):
                dve.wait_ge(s_resb, at(n, 1, 1))
                if later(n, 2):
                    dve.wait_ge(s_stored[u], at_parity(plus(n, -2), 16))
                for c in range(C):
                    bk, o = Y_BANK[c]
                    dve.wait_ge(s_ype, at(n, 2, 1 if c < 2 else 2))
                    V.scalar_tensor_tensor(out=outb[u][:, c, :], in0=bk[:, o:o + D], scalar=1.0 / WS,
                                           in1=resb[u][:, c, :], op0=ALU.mult, op1=ALU.add).then_inc(s_y, 1)

            def step(n, u, ko, kb, kf, kp):
                prev, nx, n2, v = plus(n, -1), plus(n, 1), plus(n, 2), 1 - u
                if kb:
                    maxes(n, (0, 1))
                if ko:
                    o_norm(prev, 0)
                    o_norm(prev, 1)
                if kb:
                    maxes(n, (2, 3))
                if ko:
                    o_norm(prev, 2)
                if kf:
                    qk_copy(nx, kf, 0)
                if kb:
                    maxes(n, (4, 5))
                if ko:
                    dve.wait_ge(s_on, at(prev, C, C))
                    lows(prev, on, os_, s_ohi, s_olo)
                if kf:
                    qk_copy(nx, kf, 1)
                if kb:
                    maxes(n, (6, 7))
                if kf:
                    qk_copy(nx, kf, 2)
                if kb:
                    maxes(n, (8, 9))
                if ko:
                    adds(prev, v)
                if kf:
                    v_copy(nx, v, kf, (0, 1))
                if kb:
                    maxes(n, (10, 11))
                    shift(n)
                if kf:
                    v_copy(nx, v, kf, (2,))
                if kb:
                    heads_copy(n, qT, s_qmpe, s_qm)
                if kf:
                    head_variance(nx, kf)
                    head_norm(nx, kf)
                if kp:
                    x_stats(n2, u, kp)
                if kf:
                    qk_low(nx)
                if kp:
                    x_norm(n2, u, kp)
                if kf:
                    heads_copy(nx, kT, s_ktpe, s_kt)
                if kp:
                    lows(n2, xn, xs, s_xhi, s_xlo)
                if kf:
                    heads_copy(nx, qT, s_qtpe, s_qt)

            dve.wait_ge(s_zero, 1)
            run_steps(dve, step)

            def mfront(m, u):
                dve.wait_ge(s_mx2[u], at_parity(m, 16))
                norm_stats(m, x2in[u], m_stats, m_aggr, m_ve, ((1.0, EPS),))
                dve.wait_ge(m_rstd, at(m, 1, 1))
                if later(m, 1):
                    dve.wait_ge(m_hi, at(plus(m, -1), 1, 1))
                for c in range(C):
                    V.tensor_scalar(xn[:, c, :], x2in[u][:, c, :], mv[:, c, 0:1], rstd[:, 0, c:c + 1],
                                    ALU.subtract, ALU.mult).then_inc(m_xn, 1)
                dve.wait_ge(m_xn, at(m, C, C))
                lows(m, xn, xs, m_hi, m_lo)

            def mT_copy(m, u):
                for i, (c0, cn) in enumerate(((0, 2), (2, 1))):
                    dve.wait_ge(m_tpe, at(m, 2, i + 1))
                    V.tensor_copy(mT[:, :, :].rearrange("p t (c n) -> p c t n", c=C)[:, c0:c0 + cn, :, :],
                                  half(TP[i])[:, 0:cn * 3 * P].rearrange("p (c t n) -> p c t n", c=cn, t=3))\
                        .then_inc(m_t, 1)

            def madds(m, u, k):
                dve.wait_ge(m_res, at(m, 1, 1))
                if later(m, 2):
                    dve.wait_ge(s_out[u], at_parity(plus(m, -2), 48))
                for c in range(C):
                    dve.wait_ge(m_f2, mlp_at(m, k, C, C * (0 if k == "L" else 2) + c + 1))
                    V.tensor_tensor(outb[u][:, c, :], yacc[c][:, 0:D], resb[u][:, c, :],
                                    ALU.add).then_inc(m_y, 1)

            yacc = (bank[3], G0, G1)

            def mstep(m, u, kb, kf):
                if kf:
                    mfront(plus(m, 1), 1 - u)
                    mT_copy(plus(m, 1), 1 - u)
                madds(m, u, kb)

            mfront(0, 0)
            mT_copy(0, 0)
            run_mlp(dve, mstep)

        @block.tensor
        def _(pe):
            mm = nc.tensor.matmul
            tr = nc.tensor.transpose

            pe.wait_ge(s_cst, 4)
            pe.wait_ge(s_w, 16 * SETUP_LOADS)
            for i, raw in enumerate((raw_qkv[0], raw_qkv[1], raw_qkv[1])):
                pe.wait_ge(s_bw, i + 1)
                for o, w, bk in ((0, 2 * D, G0), (2 * D, D, G1)):
                    mm(bk[:, 0:w], bwide[:, 0, :], raw[:, 0, o:o + w], start=True, stop=False)
                    last = mm(bk[:, 0:w], bwide[0:LO, 1, :], raw[0:LO, 1, o:o + w], start=False, stop=True)
                last.then_inc(s_bmm, 1)
            pe.wait_ge(s_wv, AFTER_QKV)
            for row, (norm, rows) in enumerate(((7, D), (9, KEEP[0]), (9, KEEP[1]), (9, KEEP[2]))):
                for t in range(NHT):
                    o = G0[:, row * NHT + t:row * NHT + t + 1]
                    first = min(rows, P)
                    last = mm(o, raw_fc1[0:first, 0, t * P:(t + 1) * P], bcol[0:first, norm, 0:1],
                              start=True, stop=rows <= P)
                    if rows > P:
                        last = mm(o, raw_fc1[0:LO, 1, t * P:(t + 1) * P], bcol[0:LO, norm, 1:2],
                                  start=False, stop=True)
            last.then_inc(s_bmm, 1)
            pe.wait_ge(s_wv, SETUP_STEPS)

            def split_product(out, lhs, w, cols):
                for i, (t, slot) in enumerate(((0, 0), (0, 1), (2, 0), (1, 2), (1, 3))):
                    last = mm(out, lhs[:, t, :], w[:, slot, cols], start=i == 0, stop=i == 4)
                return last

            def transposes_rows(src, s_inc, before):
                for i, chunks in enumerate(((0, 1), (2,))):
                    before(i)
                    for m, c in enumerate(chunks):
                        for t in range(3):
                            last = tr(half(TP[i])[:, (3 * m + t) * P:(3 * m + t + 1) * P],
                                      src[:, c, t * P:(t + 1) * P], idh[:, :])
                    last.then_inc(s_inc, 1)

            def transposes_heads(src, s_inc, before):
                for b in range(2):
                    before(b)
                    r = IMG_AT[b]
                    for t in range(NPT):
                        tr(half(TP[b])[:, t * SEQ:t * SEQ + TXT],
                           src[:, H * b + 2 * t:H * b + 2 * t + 2, :].rearrange("p a k -> p (a k)"), idh[:, :])
                    for t in range(NPT):
                        last = tr(half(TP[b])[:, t * SEQ + TXT:(t + 1) * SEQ],
                                  src[r:r + IMG, 2 * H + 2 * t:2 * H + 2 * t + 2, :]
                                  .rearrange("p a k -> p (a k)"), idh[r:r + IMG, r:r + IMG])
                    last.then_inc(s_inc, 1)

            def tok(n, u, k):
                if k != "A":
                    return
                pe.wait_ge(s_tokin[u], at_parity(n, 32))
                if later(n, 1):
                    pe.wait_ge(s_v, at(plus(n, -1), C, 2))
                for t in range(2):
                    last = mm(G1[0:IMG_END, 0:D], patches[u][:, t, :], tokw[:, t, :], start=t == 0, stop=t == 1)
                last.then_inc(s_tokmm, 1)

            def x_transposes(n):
                pe.wait_ge(s_xlo, at(n, 2, 2))

                def before(i):
                    if later(n, 1):
                        pe.wait_ge(s_qt, at(plus(n, -1), 2, 2))
                transposes_rows(xs, s_xtpe, before)

            def qk_product(n, k, c):
                if c == 0:
                    pe.wait_ge(s_xt, at(n, 2, 2))
                    if later(n, 1):
                        pe.wait_ge(s_v, at(plus(n, -1), C, C))
                elif c == 1 and k == "A":
                    pe.wait_ge(s_toksb, at(n, 1, 1))
                elif c == 2:
                    pe.wait_ge(s_qk, at(n, C, 1))
                split_product(QK_BANK[c][:, 0:2 * D], xt[:, c, :, :], w_qkv[k],
                              slice(0, 2 * D)).then_inc(s_qkmm, 1)

            def v_product(n, k, chunks):
                pe.wait_ge(s_qk, at(n, C, 2 if chunks[0] == 0 else 3))
                for c in chunks:
                    bk, o = V_BANK[c]
                    last = split_product(bk[:, o:o + D], xt[:, c, :, :], w_qkv[k], slice(2 * D, 3 * D))
                last.then_inc(s_vmm, 1)

            def k_transposes(n):
                pe.wait_ge(s_klo, at(n, 1, 1))

                def before(b):
                    if later(n, 1):
                        pe.wait_ge(s_qm, at(plus(n, -1), 2, 2))
                    else:
                        pe.wait_ge(s_xt, at(n, 2, 2))
                transposes_heads(ks, s_ktpe, before)

            def q_transposes(n):
                pe.wait_ge(s_qlo, at(n, 1, 1))
                pe.wait_ge(s_mz, at(n, 1, 1))

                def before(b):
                    pe.wait_ge(s_kt, at(n, 2, 2))
                transposes_heads(qs, s_qtpe, before)

            def scores(n, tiles, bank_of, keys_out, s_free, s_done):
                lhs, rhs = (kT, qT) if keys_out else (qT, kT)
                for t in tiles:
                    c, g = divmod(t, NHG)
                    if t >= 2:
                        pe.wait_ge(s_free, at(n, TILES, t - 1))
                    for i in range(HG):
                        h = heads_of(g).start + 2 * i
                        r = BLK * (h % 2)
                        cols = slice(i * SEQ, (i + 1) * SEQ)
                        for b in ((c,) if c < 2 else (0, 1)):
                            o = SEQ * b + (0 if c < 2 else TXT)
                            m = TXT if c < 2 else BLK if b == 0 else IMG
                            if c == 2 and i == 0 and b == 0:
                                m = IMG_END
                            q = 0 if c < 2 else IMG_AT[b]
                            last = mm(bank_of[t % 2][q:q + m, cols], lhs[r:r + BLK, h // 2, o:o + m],
                                      rhs[r:r + BLK, h // 2, SEQ * b:SEQ * (b + 1)], start=True, stop=True)
                    last.then_inc(s_done, 1)

            def max_scores(n, tiles):
                if tiles[0] == 0:
                    pe.wait_ge(s_kt, at(n, 2, 2))
                    pe.wait_ge(s_qt, at(n, 2, 2))
                    if later(n, 1):
                        pe.wait_ge(s_ot, at(plus(n, -1), 4, 4))
                scores(n, tiles, SM, False, s_mx, s_sc)

            def exp_scores(n):
                if later(n, 1):
                    pe.wait_ge(s_y, at(plus(n, -1), C, C))
                pe.wait_ge(s_qm, at(n, 2, 2))
                scores(n, range(TILES), SE, True, s_ex, s_st)

            def shift(n, ko, kf):
                pe.wait_ge(s_ml, at(n, 1, 1))

                def before(b):
                    if ko:
                        pe.wait_ge(s_ou, at(plus(n, -1), 2, 2))
                    else:
                        pe.wait_ge(s_xt, at(plus(n, 1), 2, 2))
                transposes_heads(qs, s_qmpe, before)

            def pv(n, u):
                pe.wait_ge(s_ex, at(n, TILES, TILES))
                pe.wait_ge(s_v, at(n, C, C))
                for b in range(2):
                    for g in range(3):
                        o = slice(g * SEQ, (g + 1) * SEQ)
                        for h in range(4 * g, 4 * g + 4):
                            q = 32 * (h % 4)
                            mm(SM[b][q:q + 32, o], v1[u][:, b, h, :], probs[:, b, h, :], start=True, stop=False,
                               tile_position=(0, q))
                        r = IMG_AT[b]
                        for h in range(4 * g, 4 * g + 4):
                            q = 32 * (h % 4)
                            last = mm(SM[b][q:q + 32, o], v1[u][r:r + IMG, 2, h, :], probs[r:r + IMG, 2, h, :],
                                      start=False, stop=True, tile_position=(r, q))
                    last.then_inc(s_otpe, 1)

            def o_transposes(n, c):
                if c == 0:
                    pe.wait_ge(s_ot, at(n, 4, 4))
                elif c == 2:
                    pe.wait_ge(s_on, at(n, C, 1))
                for g in range(3):
                    last = tr(O_BANK[c][:, g * P:(g + 1) * P], oT[:, g, c, :], idf[:, :])
                last.then_inc(s_onpe, 1)

            def ou_transposes(n, kf):
                pe.wait_ge(s_olo, at(n, 2, 2))

                def before(i):
                    if kf:
                        pe.wait_ge(s_xt, at(plus(n, 2), 2, 2))
                transposes_rows(os_, s_oupe, before)

            def proj(n, k):
                pe.wait_ge(s_ou, at(n, 2, 2))
                pe.wait_ge(s_on, at(n, C, C))
                for c in range(C):
                    bk, o = Y_BANK[c]
                    last = split_product(bk[:, o:o + D], ou[:, c, :, :], w_prj[k], slice(0, D))
                    if c:
                        last.then_inc(s_ype, 1)

            def step(n, u, ko, kb, kf, kp):
                prev, nx, n2 = plus(n, -1), plus(n, 1), plus(n, 2)
                if kf:
                    x_transposes(nx)
                if kb:
                    max_scores(n, (0, 1))
                if ko:
                    o_transposes(prev, 0)
                    o_transposes(prev, 1)
                if kb:
                    max_scores(n, (2, 3))
                if kf:
                    qk_product(nx, kf, 0)
                if ko:
                    o_transposes(prev, 2)
                if kb:
                    max_scores(n, (4, 5))
                if kf:
                    qk_product(nx, kf, 1)
                if kb:
                    max_scores(n, (6, 7))
                if ko:
                    ou_transposes(prev, kf)
                if kf:
                    qk_product(nx, kf, 2)
                if kb:
                    max_scores(n, (8, 9))
                if ko:
                    proj(prev, ko)
                if kf:
                    v_product(nx, kf, (0, 1))
                if kb:
                    max_scores(n, (10, 11))
                if kf:
                    v_product(nx, kf, (2,))
                if kb:
                    shift(n, ko, kf)
                    exp_scores(n)
                if kp:
                    tok(n2, u, kp)
                if kb:
                    pv(n, u)
                if kf:
                    k_transposes(nx)
                    q_transposes(nx)

            pe.wait_ge(s_zero, 1)
            run_steps(pe, step)

            yacc = (bank[3], G0, G1)

            def mT_transposes(m):
                pe.wait_ge(m_lo, at(m, 2, 2))

                def before(i):
                    if later(m, 1):
                        pe.wait_ge(m_t, at(plus(m, -1), 2, 2))
                transposes_rows(xs, m_tpe, before)

            def fc1(m, k, br):
                rows = D if k == "L" else KEEP[br]
                for t in range(NHT):
                    if later(m, 1) or br or t >= 3:
                        pe.wait_ge(m_g, mlp_at(m, k, NHT, NHT * br + t - 2))
                    o = bank[t % 3][:, 0:C * P]
                    cols = slice(t * P, (t + 1) * P)
                    if rows == D:
                        passes = ((0, 0), (1, 0), (0, 2), (2, 1), (3, 1))
                        r = P
                    else:
                        passes = ((0, 0), (1, 0), (0, 2))
                        r = rows
                    for i, (slot, xtile) in enumerate(passes):
                        last = mm(o, w_fc1[k][0:r, slot, cols], mT[0:r, xtile, :], start=i == 0,
                                  stop=i == len(passes) - 1)
                    last.then_inc(m_f1, 1)

            def fc2(m, k, br, n_br):
                w = w_fc2[0 if k == "L" else br + 1]
                ch = D if k == "L" else KEEP[br]
                g = gT[branch_parity(m, k, br)]
                pe.wait_ge(m_g, mlp_at(m, k, NHT, NHT * (br + 1)))
                for c in range(C):
                    if br == 0:
                        if later(m, 1):
                            pe.wait_ge(m_y, at(plus(m, -1), C, c + 1))
                    for t in range(NHT):
                        last = mm(yacc[c][:, 0:ch], g[:, t, c * P:(c + 1) * P], w[:, t, :],
                                  start=br == 0 and t == 0, stop=br == n_br - 1 and t == NHT - 1,
                                  skip_group_check=True)
                    last.then_inc(m_f2, 1)

            def mstep(m, u, kb, kf):
                n_br = 1 if kb == "L" else 3
                fc1(m, kb, 0)
                for br in range(1, n_br):
                    fc1(m, kb, br)
                    fc2(m, kb, br - 1, n_br)
                if kf:
                    mT_transposes(plus(m, 1))
                fc2(m, kb, n_br - 1, n_br)
                if kf:
                    pe.wait_ge(m_t, at(plus(m, 1), 2, 2))

            mT_transposes(0)
            pe.wait_ge(m_t, 2)
            run_mlp(pe, mstep)


NORMS = ("attn_ln_g", "attn_ln_b", "ffn_n1l_g", "ffn_n1l_b", "ffn_n1s_g", "ffn_n1s_b",
         "ffn_n2l_g", "ffn_n2l_b", "ffn_n2s_g", "ffn_n2s_b")
SETUP_LOADS = 1 + 5 * 3 + 1 + 3 * len(NORMS) + 6 + 4
AFTER_QKV = 20 + 11 + 4
SETUP_STEPS = 92


def kernel(x, txt, L0_tok_W, L0_attn_ln_g, L0_attn_ln_b, L0_attn_W_qkv, L0_attn_b_qkv, L0_attn_qn_g,
           L0_attn_qn_b, L0_attn_kn_g, L0_attn_kn_b, L0_attn_W_proj, L0_attn_b_proj, L0_ffn_gumbel_weights,
           L0_ffn_n1l_g, L0_ffn_n1l_b, L0_ffn_n1s_g, L0_ffn_n1s_b, L0_ffn_w_qkv, L0_ffn_w_proj,
           L0_ffn_b_proj, L0_ffn_n2l_g, L0_ffn_n2l_b, L0_ffn_n2s_g, L0_ffn_n2s_b, L0_ffn_w_fc1,
           L0_ffn_b_fc1, L0_ffn_w_fc2, L0_ffn_b_fc2):
    import numpy as np
    import concourse.bacc as bacc
    from concourse.bass_utils import run_bass_kernel_spmd

    x = np.asarray(x)
    pt = x.reshape(PAIRS, 2, 6, 16, 6, 16).transpose(0, 3, 5, 1, 2, 4).reshape(PAIRS, 2, P, 2, IMG)
    padded = np.zeros((PAIRS, P, 2, IMG_END), np.float32)
    for b in range(2):
        padded[:, :, :, IMG_AT[b]:IMG_AT[b] + IMG] = pt[:, :, :, b, :].transpose(0, 2, 1, 3)
    arrays = dict(
        patches=padded, txt=txt, tokw=np.asarray(L0_tok_W).T,
        attn_ln_g=L0_attn_ln_g, attn_ln_b=L0_attn_ln_b, attn_W_qkv=L0_attn_W_qkv, attn_b_qkv=L0_attn_b_qkv,
        attn_qn_g=L0_attn_qn_g, attn_qn_b=L0_attn_qn_b, attn_kn_g=L0_attn_kn_g, attn_kn_b=L0_attn_kn_b,
        attn_W_proj=L0_attn_W_proj, attn_b_proj=L0_attn_b_proj, gumbel=L0_ffn_gumbel_weights,
        ffn_n1l_g=L0_ffn_n1l_g, ffn_n1l_b=L0_ffn_n1l_b, ffn_n1s_g=L0_ffn_n1s_g, ffn_n1s_b=L0_ffn_n1s_b,
        ffn_w_qkv=L0_ffn_w_qkv, ffn_w_proj=L0_ffn_w_proj, ffn_b_proj=L0_ffn_b_proj,
        ffn_n2l_g=L0_ffn_n2l_g, ffn_n2l_b=L0_ffn_n2l_b, ffn_n2s_g=L0_ffn_n2s_g, ffn_n2s_b=L0_ffn_n2s_b,
        ffn_w_fc1=L0_ffn_w_fc1, ffn_b_fc1=np.asarray(L0_ffn_b_fc1).reshape(NHT, P).T, ffn_w_fc2=L0_ffn_w_fc2, ffn_b_fc2=L0_ffn_b_fc2)
    arrays = {k: np.ascontiguousarray(v) for k, v in arrays.items()}
    nc = bacc.Bacc("TRN2", target_bir_lowering=False, num_devices=1)
    a = {k: nc.dram_tensor(f"in_{k}", v.shape, mybir.dt.from_np(v.dtype), kind="ExternalInput").ap()
         for k, v in arrays.items()}
    a["out"] = nc.dram_tensor("out_0", (BATCH, SEQ, D), F32, kind="ExternalOutput").ap()
    build(nc, a)
    r = run_bass_kernel_spmd(nc, [{f"in_{k}": v for k, v in arrays.items()}], core_ids=[0])
    return r.results[0]["out_0"]
```

```python
from contextlib import ExitStack

import concourse.bass as bass
from concourse import mybir

F32 = mybir.dt.float32
F16 = mybir.dt.float16
ALU = mybir.AluOpType
ACT = mybir.ActivationFunctionType
AX_X = mybir.AxisListType.X

BATCH = 64
IMG = 36
TXT = 128
SEQ = IMG + TXT
D = 192
H = 12
HD = D // H
PK = 256
HID = 4 * D
EPS = 1e-5
PAIRS = BATCH // 2
LARGE = PAIRS // 2
KEEP = (D, D // 2, D // 3)

P = 128
C = 3
IMG_AT = (0, 64)
IMG_END = 64 + IMG
LO = D - P
BLK = 64
NPT = H // 2
HG = 3
NHG = H // HG
TILES = C * NHG
WS = 64.0
SCALE = HD ** -0.5
LOW_ROW = 32
NHT = HID // P


def heads_of(g):
    h = 2 * HG * (g // 2) + g % 2
    return slice(h, h + 2 * HG - 1, 2)


def at(n, per, k):
    if isinstance(n, int):
        return n * per + k
    j, off = n
    return j * (2 * per) + (off * per + k)


def later(n, k):
    return not isinstance(n, int) or n >= k


def build(nc, a):
    ctx = ExitStack()
    with ctx:
        def sb(name, shape, dt=F32):
            return ctx.enter_context(nc.sbuf_tensor(name, shape, dt))

        def sem(name):
            return ctx.enter_context(nc.semaphore(name))

        def sems(name):
            return [sem(f"{name}{i}") for i in range(2)]

        h1_dram = nc.dram_tensor("h1_scratch", [PAIRS, P, C * D], F32, kind="Internal").ap()
        x2_dram = nc.dram_tensor("x2_scratch", [PAIRS, P, C * D], F32, kind="Internal").ap()

        bank = [ctx.enter_context(nc.psum_tensor(f"bank{i}", [P, 512], F32)) for i in range(8)]
        SM = [bank[0], bank[1]]
        SE = [bank[2], bank[3]]
        TP = [bank[4], bank[5]]
        G0, G1 = bank[6], bank[7]

        QK_BANK = (G0, G1, G0)
        V_BANK = ((G1, 0), (G1, D), (G0, 0))
        O_BANK = (SE[0], SE[1], SE[0])
        Y_BANK = ((SE[1], 0), (SE[1], D), (SE[0], 0))

        def half(b):
            return b[:, :].bitcast(F16)

        def item(b):
            return half(TP[b])[:, 0:NPT * SEQ].rearrange("p (t s) -> p t s", t=NPT)

        idf = sb("idf", [P, P])
        idh = sb("idh", [P, P], F16)
        ones = sb("ones", [P, P])
        neghalf = sb("neghalf", [P, 72])
        tokw = sb("tokw", [P, 2, D])
        w_qkv = {k: sb(f"w_qkv_{k}", [P, 4, 3 * D], F16) for k in ("A", "L", "S")}
        w_prj = {k: sb(f"w_prj_{k}", [P, 4, D], F16) for k in ("A", "L", "S")}
        w_fc1 = {k: sb(f"w_fc1_{k}", [P, 4, HID], F16) for k in ("L", "S")}
        w_fc2 = [sb(f"w_fc2_{i}", [P, 2, NHT, k], F16) for i, k in enumerate((D,) + KEEP)]
        vectors = sb("vectors", [P, VEC_END])
        b_qkv = {k: sb(f"b_qkv_{k}", [P, 3 * D]) for k in ("L", "S")}
        b_qkv["A"] = vectors[:, 0:VEC_PRJ["A"]]
        b_row = {k: sb(f"b_row_{k}", [P, 3 * D], F16) for k in ("A", "L", "S")}
        both_rows = sb("both_rows", [P, P], F16)
        b_prj = {k: vectors[:, VEC_PRJ[k]:VEC_PRJ[k] + D] for k in ("A", "L")}
        b_prj["S"] = sb("b_prj_S", [P, D])
        b_fc1 = sb("b_fc1", [P, 4, NHT])
        b_fc2 = {"L": vectors[:, VEC_FC2:VEC_FC2 + D], "S": sb("b_fc2_S", [P, D])}
        gains = sb("gains", [P, 2, D])
        shifts = sb("shifts", [P, 2, D])
        gw = vectors[:, VEC_GW:VEC_GW + 3]
        zeros = sb("zeros", [P, 1])
        carrier = sb("carrier", [P, 1])

        hin = [sb(f"hin{i}", [P, C, D]) for i in range(2)]
        patches = [sb(f"patches{i}", [P, 2, IMG_END]) for i in range(2)]
        stats = sb("stats", [P, C, 6])
        mv = sb("mv", [P, C, 2])
        ve = sb("ve", [P, 2, C])
        rstd = sb("rstd", [P, 2, C])
        xn = sb("xn", [P, C, D])
        xs = sb("xs", [P, C, 3 * P], F16)
        xt = sb("xt", [P, C, 3, P], F16)
        resx = [sb(f"resx{i}", [P, C, D]) for i in range(2)]
        resb = [sb(f"resb{i}", [P, C, D]) for i in range(2)]
        qk = sb("qk", [P, 2, C, D])
        sq = sb("sq", [P, 2, C, D])
        hvar = sb("hvar", [P, 72])
        hrstd = sb("hrstd", [P, 72])
        newton = sb("newton", [P, 72])
        qs = sb("qs", [P, C * H, BLK], F16)
        ks = sb("ks", [P, C * H, BLK], F16)
        qT = [sb(f"qT{i}", [P, NPT, 2 * SEQ], F16) for i in range(2)]
        kT = [sb(f"kT{i}", [P, NPT, 2 * SEQ], F16) for i in range(2)]
        v1 = [sb(f"v1_{i}", [P, C, H, 32]) for i in range(2)]
        negmax = sb("negmax", [P, C, H])
        probs = sb("probs", [P, C, H, SEQ])
        oT = sb("oT", [P, 3, C, P])
        rden = sb("rden", [P, C, H])
        on = sb("on", [P, C, D])
        os_ = sb("os_", [P, C, 3 * P], F16)
        ou = sb("ou", [P, C, 3, P], F16)
        outb = [sb(f"outb{i}", [P, C, D]) for i in range(2)]
        flat = probs[:, :, :, :].rearrange("p c h s -> p (c h s)")
        raw_qkv = [flat[:, i * 1152:(i + 1) * 1152].rearrange("p (t n) -> p t n", t=2) for i in range(2)]
        raw_prj = [flat[:, 2304 + i * 384:2304 + (i + 1) * 384].rearrange("p (t n) -> p t n", t=2)
                   for i in range(2)]
        raw_fc1 = flat[:, 3072:3072 + 1536].rearrange("p (t n) -> p t n", t=2)
        columns = sb("columns", [P, 2 * len(NORMS) + NHT])
        bcol = columns[:, 0:2 * len(NORMS)].rearrange("p (i t) -> p i t", t=2)
        bwide = sb("bwide", [P, 2, P])
        gmean = sb("gmean", [P, 2, 24])
        coef = sb("coef", [P, D])
        x2in = [sb(f"x2in{i}", [P, C, D]) for i in range(2)]
        h1in = [sb(f"h1in{i}", [P, C, D]) for i in range(2)]
        mT = sb("mT", [P, 3, C * P], F16)
        gT = sb("gT", [P, NHT, C * P])
        parts = [flat[:, i * NHT * C * P // 2:(i + 1) * NHT * C * P // 2].bitcast(F16)
                 .rearrange("p (t n) -> p t n", t=NHT) for i in range(4)]
        gH, gL = parts[0:2], parts[2:4]
        raw_fc2, scaled_fc2 = [gT[:, i * NHT // 2:(i + 1) * NHT // 2, :].rearrange("p t n -> p (t n)")
                               .rearrange("p (t n) -> p t n", t=NHT) for i in range(2)]

        s_wa, s_w = sem("attention_weights_loaded"), sem("weights_loaded")
        s_cst = sem("constants_set")
        s_idm = sem("identity_cleared")
        s_zero = sem("padding_set")
        s_bw = sem("shift_widened")
        s_bmm = sem("shift_multiplied")
        s_wv = sem("setup_vector_step")
        s_tokin, s_hin = sems("tokens_loaded"), sems("h1_loaded")
        s_tokmm, s_toksb = sem("tok_multiplied"), sem("tok_copied")
        s_stats, s_aggr, s_ve, s_rstd = sem("stats"), sem("aggr"), sem("var_eps"), sem("rstd")
        s_xn, s_resx, s_resb = sem("xn_ready"), sem("resx_ready"), sem("resb_ready")
        s_xhi, s_xlo, s_xtpe, s_xt = sem("x_hi"), sem("x_lo"), sem("x_transposed"), sem("xT_ready")
        s_qkmm, s_qk, s_vmm, s_v = sem("qk_multiplied"), sem("qk_copied"), sem("v_multiplied"), sem("v_copied")
        s_sq, s_hvar, s_hve, s_hrstd = sem("qk_squared"), sem("head_var"), sem("head_var_eps"), sem("head_rstd")
        s_hln, s_newton = sem("head_log"), sem("head_rstd_refined")
        s_qkn, s_qkg, s_qkb = sem("qk_normed"), sem("qk_gained"), sem("qk_shifted")
        s_qhi, s_khi, s_qlo, s_klo, s_mz = sem("q_hi"), sem("k_hi"), sem("q_lo"), sem("k_lo"), sem("shift_cleared")
        s_ktpe, s_kt, s_qtpe, s_qt = sem("k_transposed"), sem("kT_ready"), sem("q_transposed"), sem("qT_ready")
        s_sc, s_mx = sem("scores_for_max"), sem("max_taken")
        s_mh, s_ml = sem("max_hi"), sem("max_lo")
        s_qmpe, s_qm = sem("shifted_q_transposed"), sem("shifted_qT_ready")
        s_st, s_ex = sem("scores_for_exp"), sem("exp_done")
        s_otpe, s_ot = sem("pv_multiplied"), sem("oT_copied")
        s_onpe, s_rden, s_on = sem("o_transposed"), sem("denominators"), sem("o_normed")
        s_ohi, s_olo, s_oupe, s_ou = sem("o_hi"), sem("o_lo"), sem("ou_transposed"), sem("ou_ready")
        s_ype, s_y = sem("proj_multiplied"), sem("attention_added")
        s_stored = sems("attention_stored")
        s_mx2, s_mh1 = sems("mlp_x2_loaded"), sems("mlp_h1_loaded")
        m_stats, m_aggr, m_ve, m_rstd = sem("m_stats"), sem("m_aggr"), sem("m_var_eps"), sem("m_rstd")
        m_xn, m_hi, m_lo, m_tpe, m_t = sem("m_xn"), sem("m_hi"), sem("m_lo"), sem("m_transposed"), sem("mT_ready")
        m_r1, m_res = sem("m_res_half"), sem("m_res")
        m_gh, m_gle, m_glo = sem("gelu_hi"), sem("gelu_lo_even"), sem("gelu_lo_odd")
        m_f1, m_g, m_f2, m_y = sem("fc1_multiplied"), sem("gelu_done"), sem("fc2_multiplied"), sem("mlp_added")
        s_out = sems("output_stored")

        block = ctx.enter_context(nc.Block())

        UNITS = 2 * PAIRS

        def kind(n):
            if not 0 <= n < UNITS:
                return None
            return "A" if n < PAIRS else "L" if n < PAIRS + LARGE else "S"

        def run_steps(eng, step):
            n = -2
            while n <= UNITS:
                kinds = [kind(n + i) for i in (-1, 0, 1, 2)]
                end = n
                while [kind(end + i) for i in (-1, 0, 1, 2)] == kinds:
                    end += 1
                pairs = (end - n) // 2
                if n < 2 or n % 2 or pairs < 2:
                    step(n, n % 2, *kinds)
                    n += 1
                else:
                    with eng.Fori(n // 2, n // 2 + pairs) as j:
                        for u in range(2):
                            step((j, u), u, *kinds)
                    n += 2 * pairs

        def plus(n, k):
            return n + k if isinstance(n, int) else (n[0], n[1] + k)

        def pair_of(n, k):
            base = 0 if k == "A" else PAIRS
            return n - base if isinstance(n, int) else n[0] * 2 + (n[1] - base)

        def run_mlp(eng, mstep):
            def kinds(m):
                return [None if not 0 <= m + i < PAIRS else "L" if m + i < LARGE else "S"
                        for i in (-1, 0, 1, 2)]

            for lo, hi in ((0, LARGE), (LARGE, PAIRS)):
                for m in (lo, lo + 1):
                    mstep(m, m % 2, *kinds(m))
                with eng.Fori(lo // 2 + 1, (hi - 2) // 2) as j:
                    for u in range(2):
                        mstep((j, u), u, *kinds(lo + 2))
                for m in (hi - 2, hi - 1):
                    mstep(m, m % 2, *kinds(m))
            mstep(PAIRS, PAIRS % 2, "S", None, None, None)

        def at_parity(n, per):
            return per * (n // 2 + 1) if isinstance(n, int) else n[0] * per + per * (n[1] // 2 + 1)

        def hin_count(n):
            return 16 * (n // 2 + 1 - PAIRS // 2) if isinstance(n, int) else \
                n[0] * 16 + 16 * (n[1] // 2 + 1 - PAIRS // 2)

        def resx_count(n):
            return at(n, C, C - C * PAIRS)

        def mlp_at(m, k, per, c):
            return at(m, per, c) if k == "L" else at(m, 3 * per, c - 2 * per * LARGE)

        def last_branch(k):
            return 0 if k == "L" else 2

        def branch_parity(m, k, br):
            off = m if isinstance(m, int) else m[1]
            return (off if k == "L" else off + br) % 2

        @block.sync
        def _(sp):
            def load(dst, src, s_done=s_w):
                sp.dma_start(dst, src).then_inc(s_done, 16)

            def weights(name):
                return a[name].rearrange("p t n -> p (t n)")

            def flat_of(t):
                return t.rearrange("p t n -> p (t n)")

            load(columns[:, :], a["columns"], s_wa)
            load(flat_of(raw_qkv[0]), weights("attn_W_qkv"), s_wa)
            load(vectors[:, :], a["vectors"].partition_broadcast(P), s_wa)
            load(flat_of(raw_qkv[1]), weights("ffn_w_qkv"))
            load(flat_of(raw_prj[0]), weights("attn_W_proj"))
            load(flat_of(raw_prj[1]), weights("ffn_w_proj"))
            load(flat_of(raw_fc1), weights("ffn_w_fc1"))
            load(raw_fc2, a["ffn_w_fc2"].rearrange("(t p) n -> p t n", p=P))
            load(tokw[:, :, :], a["tokw"].rearrange("(t p) n -> p t n", p=P))

            def index(p):
                return p if isinstance(p, int) else sp.snap(p)

            def load_unit(n, u, k):
                p = index(pair_of(n, k))
                if later(n, 2):
                    sp.wait_ge(s_resb, at(plus(n, -2), 1, 1))
                if k == "A":
                    txt = a["txt"].rearrange("(q b) t d -> q t b d", b=2)[bass.ds(p, 1), :, :, :]\
                        .rearrange("q t b d -> t (q b) d")
                    sp.dma_start(hin[u][:, 0:2, :], txt).then_inc(s_tokin[u], 16)
                    xp = a["patches"][bass.ds(p, 1), :, :, :].rearrange("o p t n -> p (o t) n")
                    sp.dma_start(patches[u][:, :, :], xp).then_inc(s_tokin[u], 16)
                else:
                    src = h1_dram[bass.ds(p, 1), :, :].rearrange("o p f -> p (o f)")
                    sp.dma_start(hin[u][:, :, :].rearrange("p c d -> p (c d)"), src).then_inc(s_hin[u], 16)

            def store_unit(n, u, k):
                p = index(pair_of(n, k))
                sp.wait_ge(s_y, at(n, C, C))
                dst = h1_dram if k == "A" else x2_dram
                sp.dma_start(dst[bass.ds(p, 1), :, :].rearrange("o p f -> p (o f)"),
                             outb[u][:, :, :].rearrange("p c d -> p (c d)")).then_inc(s_stored[u], 16)

            def step(n, u, ko, kb, kf, kp):
                if kp:
                    load_unit(plus(n, 2), u, kp)
                if ko:
                    store_unit(plus(n, -1), 1 - u, ko)

            sp.wait_ge(s_zero, 1)
            run_steps(sp, step)

            for u in range(2):
                sp.wait_ge(s_stored[u], 16 * PAIRS)

            def mload(m, u):
                p = index(m if isinstance(m, int) else m[0] * 2 + m[1])
                if later(m, 2):
                    sp.wait_ge(m_res, at(plus(m, -2), 1, 1))
                for dst, src, s in ((x2in, x2_dram, s_mx2), (h1in, h1_dram, s_mh1)):
                    sp.dma_start(dst[u][:, :, :].rearrange("p c d -> p (c d)"),
                                 src[bass.ds(p, 1), :, :].rearrange("o p f -> p (o f)")).then_inc(s[u], 16)

            def store(m, u):
                p = index(m if isinstance(m, int) else m[0] * 2 + m[1])
                sp.wait_ge(m_y, at(m, 3, 3))
                both = a["out"].rearrange("(q b) s d -> q b s d", b=2)[bass.ds(p, 1), :, :, :]\
                    .rearrange("q b s d -> (q b) s d")
                sp.dma_start(both[:, IMG:SEQ, :].rearrange("b t d -> t b d"), outb[u][:, 0:2, :])\
                    .then_inc(s_out[u], 16)
                for b in range(2):
                    sp.dma_start(both[b:b + 1, 0:IMG, :].rearrange("b t d -> t (b d)"),
                                 outb[u][IMG_AT[b]:IMG_AT[b] + IMG, 2, :]).then_inc(s_out[u], 16)

            def mstep(m, u, ko, kb, kf, k2):
                if k2:
                    mload(plus(m, 2), u)
                if ko:
                    store(plus(m, -1), 1 - u)

            mload(0, 0)
            mload(1, 1)
            run_mlp(sp, mstep)
            for u in range(2):
                sp.wait_ge(s_out[u], 48 * (PAIRS // 2))

        @block.gpsimd
        def _(pool):
            nc.gpsimd.memset(idf[:, :], 0.0).then_inc(s_idm, 1)
            nc.gpsimd.memset(idh[:, :], 0.0).then_inc(s_idm, 1)
            pool.wait_ge(s_idm, 2)
            for m in (idf, idh):
                nc.gpsimd.affine_select(out=m[:, :], in_=m[:, :], compare_op=ALU.not_equal, fill=1.0, base=0,
                                        pattern=[[-1, P]], channel_multiplier=1).then_inc(s_cst, 1)
            nc.gpsimd.memset(ones[:, :], 1.0).then_inc(s_cst, 1)
            nc.gpsimd.memset(neghalf[:, :], -0.5).then_inc(s_cst, 1)
            nc.gpsimd.memset(zeros[:, :], 0.0)
            for t in hin:
                nc.gpsimd.memset(t[:, 2, :], 0.0)
            nc.gpsimd.memset(negmax[:, :, :], 0.0)
            nc.gpsimd.memset(oT[:, :, :, :], 1.0)
            nc.gpsimd.memset(qs[:, :, :], 0.0)
            nc.gpsimd.memset(ks[:, :, :], 0.0)
            for t in v1:
                nc.gpsimd.memset(t[:, :, :, :], 0.0)
            nc.gpsimd.memset(ve[:, 0, 0:1], 0.0).then_inc(s_idm, 1)
            pool.wait_ge(s_idm, 3)
            nc.gpsimd.memset(ks[:, :, 2 * HD:2 * HD + 2], 1.0)
            for t in v1:
                last = nc.gpsimd.memset(t[:, :, :, HD:HD + 1], 1.0)
            last.then_inc(s_zero, 1)
            pool.wait_ge(s_zero, 1)

            def power(n):
                pool.wait_ge(s_ve, at(n, 2, 2))
                nc.gpsimd.tensor_tensor(rstd[:, :, :], ve[:, :, :],
                                        neghalf[:, 0:2 * C].rearrange("p (a c) -> p a c", a=2),
                                        ALU.pow).then_inc(s_rstd, 1)

            def residual(n, u, k):
                pool.wait_ge(s_xn, at(n, C, C))
                if k == "A":
                    pool.wait_ge(s_tokin[u], at_parity(n, 32))
                    pool.wait_ge(s_toksb, at(n, 1, 1))
                else:
                    pool.wait_ge(s_resx, resx_count(n))
                if later(n, 2):
                    pool.wait_ge(s_y, at(plus(n, -2), C, C))
                nc.gpsimd.tensor_tensor(resb[u][:, :, :], (hin if k == "A" else resx)[u][:, :, :],
                                        b_prj[k][:, :].unsqueeze(1).to_broadcast([P, C, D]),
                                        ALU.add).then_inc(s_resb, 1)

            def gain(n, k):
                if k != "A":
                    return
                pool.wait_ge(s_sq, at(n, 1, 1))
                nc.gpsimd.tensor_tensor(qk[:, :, :, :], qk[:, :, :, :],
                                        gains[:, :, :].unsqueeze(2).to_broadcast([P, 2, C, D]),
                                        ALU.mult).then_inc(s_qkg, 1)

            def lows(n, src, dst, s_hi, s_lo):
                pool.wait_ge(s_hi, at(n, 1, 1))
                nc.gpsimd.tensor_tensor(dst[:, :, D:2 * P], src[:, :, P:D], dst[:, :, P:D],
                                        ALU.subtract).then_inc(s_lo, 1)
                nc.gpsimd.tensor_tensor(dst[:, :, 2 * P:3 * P], src[:, :, 0:P], dst[:, :, 0:P],
                                        ALU.subtract).then_inc(s_lo, 1)

            def clear_shift(n):
                if later(n, 1):
                    pool.wait_ge(s_qmpe, at(plus(n, -1), 2, 2))
                zero = zeros[:, 0:1].unsqueeze(2).to_broadcast([P, C * H, 2])
                nc.gpsimd.tensor_tensor(qs[:, :, 2 * HD:2 * HD + 2], zero, zero, ALU.add).then_inc(s_mz, 1)

            def step(n, u, ko, kb, kf, kp):
                if ko:
                    lows(plus(n, -1), on, os_, s_ohi, s_olo)
                if kf:
                    gain(plus(n, 1), kf)
                    residual(plus(n, 1), 1 - u, kf)
                    clear_shift(plus(n, 1))
                if kp:
                    power(plus(n, 2))
                    lows(plus(n, 2), xn, xs, s_xhi, s_xlo)

            run_steps(pool, step)

            def mfront(m, u):
                pool.wait_ge(m_ve, at(m, 1, 1))
                nc.gpsimd.tensor_tensor(rstd[:, 0, :], ve[:, 0, :], neghalf[:, 0:C], ALU.pow).then_inc(m_rstd, 1)

            def mres(m, u, k):
                for s in (s_mx2, s_mh1):
                    pool.wait_ge(s[u], at_parity(m, 16))
                pool.wait_ge(m_xn, at(m, C, C))
                if later(m, 2):
                    pool.wait_ge(m_y, at(plus(m, -2), 3, 3))
                nc.gpsimd.tensor_tensor(resb[u][:, :, :], x2in[u][:, :, :], h1in[u][:, :, :],
                                        ALU.add).then_inc(m_r1, 1)
                pool.wait_ge(m_r1, at(m, 1, 1))
                nc.gpsimd.tensor_tensor(resb[u][:, :, :], resb[u][:, :, :],
                                        b_fc2[k][:, :].unsqueeze(1).to_broadcast([P, C, D]),
                                        ALU.add).then_inc(m_res, 1)

            def gelu_lows(m, k, br):
                i = branch_parity(m, k, br)
                for t in range(1, NHT, 2):
                    pool.wait_ge(m_gh, mlp_at(m, k, NHT, NHT * br + t + 1))
                    nc.gpsimd.tensor_tensor(gL[i][:, t, :], gT[:, t, :], gH[i][:, t, :],
                                            ALU.subtract).then_inc(m_glo, 1)

            def mstep(m, u, ko, kb, kf, k2):
                if kb:
                    mres(m, u, kb)
                if kf:
                    mfront(plus(m, 1), 1 - u)
                if kb:
                    for br in range(last_branch(kb) + 1):
                        gelu_lows(m, kb, br)

            mfront(0, 0)
            run_mlp(pool, mstep)

        @block.scalar
        def _(act):
            def tok_copy(n, u, k):
                if k != "A":
                    return
                act.wait_ge(s_tokmm, at(n, 1, 1))
                if later(n, 2):
                    act.wait_ge(s_xn, at(plus(n, -2), C, C))
                    act.wait_ge(s_resb, at(plus(n, -2), 1, 1))
                nc.scalar.activation(hin[u][0:IMG_END, 2, :], G1[0:IMG_END, 0:D], ACT.Copy).then_inc(s_toksb, 1)

            def x_high(n):
                act.wait_ge(s_xn, at(n, C, C))
                if later(n, 1):
                    act.wait_ge(s_xtpe, at(plus(n, -1), 2, 2))
                nc.scalar.activation(xs[:, :, 0:D], xn[:, :, :], ACT.Copy).then_inc(s_xhi, 1)

            def rows_copy(n, dst, s_pe, s_done, i):
                c0, cn = ((0, 2), (2, 1))[i]
                if dst is xt and i == 0 and later(n, 1):
                    act.wait_ge(s_vmm, at(plus(n, -1), 2, 2))
                act.wait_ge(s_pe, at(n, 2, i + 1))
                nc.scalar.activation(dst[:, c0:c0 + cn, :, :].rearrange("p c t n -> p (c t n)"),
                                     half(TP[i])[:, 0:3 * cn * P], ACT.Copy).then_inc(s_done, 1)

            def qk_copy(n, c):
                act.wait_ge(s_qkmm, at(n, C, c + 1))
                if c == 0 and later(n, 1):
                    act.wait_ge(s_qlo, at(plus(n, -1), 1, 1))
                nc.scalar.activation(qk[:, :, c, :],
                                     QK_BANK[c][:, 0:2 * D].rearrange("p (a d) -> p a d", a=2),
                                     ACT.Copy, scale=1.0 / WS).then_inc(s_qk, 1)

            def v_copy(n, u, chunks):
                c0, cn = chunks[0], len(chunks)
                bk, o = V_BANK[c0]
                act.wait_ge(s_vmm, at(n, 2, 1 if c0 < 2 else 2))
                if c0 == 0 and later(n, 2):
                    act.wait_ge(s_otpe, at(plus(n, -2), 2, 2))
                nc.scalar.activation(v1[u][:, c0:c0 + cn, :, 0:HD],
                                     bk[:, o:o + cn * D].rearrange("p (c h d) -> p c h d", c=cn, h=H),
                                     ACT.Copy, scale=1.0 / WS).then_inc(s_v, 1)

            def qk_square(n, k):
                if k != "A":
                    return
                act.wait_ge(s_qk, at(n, C, C))
                nc.scalar.activation(sq[:, :, :, :], qk[:, :, :, :], ACT.Square).then_inc(s_sq, 1)

            def head_power(n, k):
                if k != "A":
                    return
                act.wait_ge(s_hve, at(n, 1, 1))
                nc.scalar.activation(hrstd[:, :], hvar[:, :], ACT.Ln).then_inc(s_hln, 1)
                act.wait_ge(s_hln, at(n, 1, 1))
                nc.scalar.activation(hrstd[:, :], hrstd[:, :], ACT.Exp, scale=-0.5).then_inc(s_hrstd, 1)

            def k_high(n, k):
                if k == "A":
                    act.wait_ge(s_qkb, at(n, 1, 1))
                else:
                    act.wait_ge(s_qk, at(n, C, C))
                if later(n, 1):
                    act.wait_ge(s_ktpe, at(plus(n, -1), 2, 2))
                src = qk[:, 1, :, :].rearrange("p c (h d) -> p (c h) d", h=H).unsqueeze(2)
                nc.scalar.activation(ks[:, :, 0:2 * HD].rearrange("p g (r d) -> p g r d", r=2),
                                     src.to_broadcast([P, C * H, 2, HD]), ACT.Copy).then_inc(s_khi, 1)

            def q_high(n):
                if later(n, 1):
                    act.wait_ge(s_qmpe, at(plus(n, -1), 2, 2))
                src = qk[:, 0, :, :].rearrange("p c (h d) -> p (c h) d", h=H).unsqueeze(2)
                dst = qs[:, :, :].rearrange("p g (r d) -> p g r d", d=HD)[:, :, 0:4:3, :]
                nc.scalar.activation(dst, src.to_broadcast([P, C * H, 2, HD]), ACT.Copy,
                                     scale=SCALE).then_inc(s_qhi, 1)

            def heads_copy(n, dst, s_pe, s_done):
                act.wait_ge(s_pe, at(n, 2, 2))
                nc.scalar.activation(dst[:, :, SEQ:2 * SEQ], item(1), ACT.Copy).then_inc(s_done, 1)

            def exps(n, tiles):
                for t in tiles:
                    c, g = divmod(t, NHG)
                    rows = P if c < 2 else IMG_END
                    act.wait_ge(s_st, at(n, TILES, t + 1))
                    if t == 0 and later(n, 1):
                        act.wait_ge(s_otpe, at(plus(n, -1), 2, 2))
                    nc.scalar.activation(probs[0:rows, c, heads_of(g), :],
                                         SE[t % 2][0:rows, 0:HG * SEQ].rearrange("p (h s) -> p h s", h=HG),
                                         ACT.Exp).then_inc(s_ex, 1)

            def o_copy(n):
                for b in range(2):
                    act.wait_ge(s_otpe, at(n, 2, b + 1))
                    if b == 0 and later(n, 1):
                        act.wait_ge(s_onpe, at(plus(n, -1), C, C))
                    o = SM[b][:, 0:3 * SEQ].rearrange("p (g s) -> p g s", g=3)
                    nc.scalar.activation(oT[:, :, b, :], o[:, :, 0:TXT], ACT.Copy).then_inc(s_ot, 1)
                    nc.scalar.activation(oT[:, :, 2, IMG_AT[b]:IMG_AT[b] + IMG], o[:, :, TXT:SEQ],
                                         ACT.Copy).then_inc(s_ot, 1)

            def o_high(n):
                act.wait_ge(s_on, at(n, C, C))
                if later(n, 1):
                    act.wait_ge(s_oupe, at(plus(n, -1), 2, 2))
                nc.scalar.activation(os_[:, :, 0:D], on[:, :, :], ACT.Copy).then_inc(s_ohi, 1)

            def step(n, u, ko, kb, kf, kp):
                prev, nx, n2, v = plus(n, -1), plus(n, 1), plus(n, 2), 1 - u
                if kf:
                    qk_copy(nx, 0)
                    qk_copy(nx, 1)
                if ko:
                    o_high(prev)
                if kf:
                    qk_copy(nx, 2)
                    qk_square(nx, kf)
                if kp:
                    tok_copy(n2, u, kp)
                if ko:
                    rows_copy(prev, ou, s_oupe, s_ou, 0)
                    rows_copy(prev, ou, s_oupe, s_ou, 1)
                if kf:
                    head_power(nx, kf)
                if kf in ("L", "S"):
                    k_high(nx, kf)
                if kb:
                    heads_copy(n, qT[u], s_qmpe, s_qm)
                    exps(n, range(0, 2))
                if kf:
                    v_copy(nx, v, (0, 1))
                if kb:
                    exps(n, range(2, 4))
                if kf == "A":
                    k_high(nx, kf)
                if kb:
                    exps(n, range(4, 6))
                if kf:
                    v_copy(nx, v, (2,))
                if kf == "A":
                    q_high(nx)
                if kf in ("L", "S"):
                    q_high(nx)
                if kb:
                    exps(n, range(6, 8))
                    exps(n, range(8, 10))
                if kp:
                    x_high(n2)
                if kb:
                    exps(n, range(10, TILES))
                    o_copy(n)
                if kp:
                    rows_copy(n2, xt, s_xtpe, s_xt, 0)
                    rows_copy(n2, xt, s_xtpe, s_xt, 1)

            act.wait_ge(s_zero, 1)
            run_steps(act, step)

            def mfront(m, u):
                act.wait_ge(m_xn, at(m, C, C))
                if later(m, 1):
                    act.wait_ge(m_tpe, at(plus(m, -1), 2, 2))
                nc.scalar.activation(xs[:, :, 0:D], xn[:, :, :], ACT.Copy).then_inc(m_hi, 1)

            def gelus(m, k, branch, row, tiles=range(NHT)):
                for t in tiles:
                    act.wait_ge(m_f1, mlp_at(m, k, NHT, NHT * branch + t + 1))
                    if later(m, 1) or branch:
                        act.wait_ge((m_gle, m_glo)[t % 2], mlp_at(m, k, NHT // 2, NHT // 2 * (branch - 1) + t // 2 + 1))
                    nc.scalar.activation(gT[:, t, :], bank[t % 3][:, 0:C * P], ACT.Gelu,
                                         bias=b_fc1[:, row, t:t + 1], scale=1.0 / WS).then_inc(m_g, 1)

            def mstep(m, u, ko, kb, kf, k2):
                for br, row in enumerate({"L": (0,), "S": (1, 2, 3)}.get(kb, ())):
                    if br == 0 and kf:
                        gelus(m, kb, br, row, range(0, 3))
                        mfront(plus(m, 1), 1 - u)
                        gelus(m, kb, br, row, range(3, NHT))
                    else:
                        gelus(m, kb, br, row)

            mfront(0, 0)
            run_mlp(act, mstep)

        @block.vector
        def _(dve):
            steps = [0]

            def free(ins):
                ins.then_inc(s_wv, 1)
                steps[0] += 1

            def link(ins):
                free(ins)
                dve.wait_ge(s_wv, steps[0])

            V = nc.vector
            link(V.memset(both_rows[:, :], 0.0))
            for r in (0, LOW_ROW):
                link(V.memset(both_rows[r:r + 1, :], 1.0))
            dve.wait_ge(s_cst, 4)
            dve.wait_ge(s_wa, 16 * FIRST_LOADS)

            def split(dst, raw0, raw1):
                free(V.tensor_copy(dst[:, 0, :], raw0))
                free(V.memset(dst[LO:P, 3, :], 0.0))
                link(V.tensor_copy(dst[:, 2, :], raw1))
                free(V.tensor_tensor(dst[:, 1, :], raw0, dst[:, 0, :], ALU.subtract))
                link(V.tensor_tensor(dst[0:LO, 3, :], raw1[0:LO, :], dst[0:LO, 2, :], ALU.subtract))

            def center(t, lanes):
                v = t.rearrange("p (g d) -> p g d", d=HD)
                link(V.tensor_reduce(out=gmean[:, lanes, :], in_=v, op=ALU.add, axis=AX_X))
                link(V.tensor_scalar(gmean[:, lanes, :], gmean[:, lanes, :], 1.0 / HD, None, ALU.mult))
                link(V.tensor_tensor(v, v, gmean[:, lanes, :].unsqueeze(2).to_broadcast([P, 24, HD]),
                                     ALU.subtract))

            scr = sq[:, :, :, :].rearrange("p a c d -> p (a c d)").rearrange("p (t n) -> p t n", t=2)
            for i, (k, raw, norm) in enumerate((("A", raw_qkv[0], 0), ("L", raw_qkv[1], 2), ("S", raw_qkv[1], 4))):
                if k == "L":
                    dve.wait_ge(s_w, 16 * SETUP_LOADS)
                for t in range(2):
                    link(V.tensor_scalar(bwide[:, t, :], ones[:, :], bcol[:, norm + 1, t:t + 1], None, ALU.mult))
                V.memset(gmean[:, 0, 0:1], 0.0).then_inc(s_bw, 1)
                dve.wait_ge(s_bmm, i + 1)
                if k == "A":
                    for o, w, bk in ((0, 2 * D, G0), (2 * D, D, G1)):
                        link(V.tensor_tensor(b_qkv[k][:, o:o + w], b_qkv[k][:, o:o + w], bk[:, 0:w], ALU.add))
                    center(b_qkv[k][:, 0:2 * D], 0)
                else:
                    for o, w, bk in ((0, 2 * D, G0), (2 * D, D, G1)):
                        (free if o == 0 else link)(V.tensor_copy(b_qkv[k][:, o:o + w], bk[:, 0:w]))
                scaled = b_qkv[k][:, :]
                link(V.tensor_scalar(scaled, scaled, WS, None, ALU.mult))
                link(V.tensor_copy(b_row[k][:, :], scaled))
                link(V.tensor_tensor(b_row[k][LOW_ROW:LOW_ROW + 1, :], scaled[LOW_ROW:LOW_ROW + 1, :],
                                     b_row[k][LOW_ROW:LOW_ROW + 1, :], ALU.subtract))
                for t in range(2):
                    link(V.tensor_scalar(scr[:, t, :], raw[:, t, :], bcol[:, norm, t:t + 1], WS,
                                         ALU.mult, ALU.mult))
                    if k == "A":
                        center(scr[:, t, 0:2 * D], t)
                split(w_qkv[k], scr[:, 0, :], scr[:, 1, :])
            scp = scr[:, :, 0:D]
            for k, raw in (("A", raw_prj[0]), ("L", raw_prj[1])):
                for t in range(2):
                    link(V.tensor_scalar(scp[:, t, :], raw[:, t, :], WS, None, ALU.mult))
                split(w_prj[k], scp[:, 0, :], scp[:, 1, :])
            raw = scr[:, :, D:2 * D]
            for t in range(2):
                link(V.tensor_scalar(raw[:, t, :], scp[:, t, :], gw[:, 0:1], None, ALU.mult))
            for i in (1, 2):
                r = KEEP[i]
                link(V.scalar_tensor_tensor(out=raw[0:r, 0, 0:r], in0=scp[0:r, 0, 0:r], scalar=gw[0:r, i:i + 1],
                                            in1=raw[0:r, 0, 0:r], op0=ALU.mult, op1=ALU.add))
            split(w_prj["S"], raw[:, 0, :], raw[:, 1, :])
            link(V.tensor_scalar(coef[:, :], ones[:, 0:1].to_broadcast([P, D]), gw[:, 0:1], None, ALU.mult))
            for i in (1, 2):
                link(V.tensor_scalar(coef[:, 0:KEEP[i]], coef[:, 0:KEEP[i]], gw[:, i:i + 1], None, ALU.add))
            link(V.tensor_tensor(b_prj["S"][:, :], b_prj["L"][:, :], coef[:, :], ALU.mult))
            link(V.tensor_tensor(b_fc2["S"][:, :], b_fc2["L"][:, :], coef[:, :], ALU.mult))
            dve.wait_ge(s_bmm, 4)
            link(V.tensor_tensor(b_fc1[:, :, :], G0[:, 0:4 * NHT].rearrange("p (a t) -> p a t", a=4),
                                 columns[:, 2 * len(NORMS):].unsqueeze(1).to_broadcast([P, 4, NHT]), ALU.add))
            raw0, raw1 = [t.rearrange("p a n -> p (a n)")[:, 0:HID] for t in (gT[:, NHT // 2:NHT, :], scr)]
            for k, norm in (("L", 6), ("S", 8)):
                for t, r in enumerate((raw0, raw1)):
                    link(V.tensor_scalar(r, raw_fc1[:, t, :], bcol[:, norm, t:t + 1], WS, ALU.mult, ALU.mult))
                split(w_fc1[k], raw0, raw1)
            for i in range(2):
                for dst, o in ((gains, 0), (shifts, HD)):
                    link(V.tensor_copy(dst[:, i, :].rearrange("p (h d) -> p h d", h=H),
                                       vectors[:, VEC_HEADS + 2 * HD * i + o:VEC_HEADS + 2 * HD * i + o + HD]
                                       .unsqueeze(1).to_broadcast([P, H, HD])))
            assert steps[0] == SETUP_STEPS, steps

            def prepare_fc2():
                for i, n in enumerate((D,) + KEEP):
                    if i:
                        link(V.tensor_scalar(scaled_fc2[:, :, 0:n], raw_fc2[:, :, 0:n], gw[:, i - 1:i], WS,
                                             ALU.mult, ALU.mult))
                    else:
                        link(V.tensor_scalar(scaled_fc2, raw_fc2, WS, None, ALU.mult))
                    link(V.tensor_copy(w_fc2[i][:, 0, :, :], scaled_fc2[:, :, 0:n]))
                    link(V.tensor_tensor(w_fc2[i][:, 1, :, :], scaled_fc2[:, :, 0:n], w_fc2[i][:, 0, :, :],
                                         ALU.subtract))

            def norm_stats(n, h, s_st, s_ag, s_v, lanes):
                for c in range(C):
                    V.bn_stats(out=stats[:, c, :], in_=h[:, c, :]).then_inc(s_st, 1)
                dve.wait_ge(s_st, at(n, C, C))
                V.memset(carrier[:, :], 0.0)
                for c in range(C):
                    V.bn_aggr(out=mv[:, c, :], in_=stats[:, c, :]).then_inc(s_ag, 1)
                dve.wait_ge(s_ag, at(n, C, C))
                for lane, (mul, add) in enumerate(lanes):
                    V.tensor_scalar(ve[:, lane, :], mv[:, :, 1], mul, add, ALU.mult, ALU.add).then_inc(s_v, 1)

            def lows(n, src, dst, s_hi, s_lo):
                dve.wait_ge(s_hi, at(n, 1, 1))
                V.tensor_tensor(dst[:, :, D:2 * P], src[:, :, P:D], dst[:, :, P:D],
                                ALU.subtract).then_inc(s_lo, 1)
                V.tensor_tensor(dst[:, :, 2 * P:3 * P], src[:, :, 0:P], dst[:, :, 0:P],
                                ALU.subtract).then_inc(s_lo, 1)

            def x_stats(n, u, k):
                if k == "A":
                    dve.wait_ge(s_tokin[u], at_parity(n, 32))
                    dve.wait_ge(s_toksb, at(n, 1, 1))
                else:
                    dve.wait_ge(s_hin[u], hin_count(n))
                norm_stats(n, hin[u], s_stats, s_aggr, s_ve, ((1.0 + EPS, EPS * EPS), (1.0, EPS)))

            def x_norm(n, u, k):
                dve.wait_ge(s_rstd, at(n, 1, 1))
                if later(n, 1):
                    dve.wait_ge(s_xhi, at(plus(n, -1), 1, 1))
                for c in range(C):
                    V.tensor_scalar(xn[:, c, :], hin[u][:, c, :], mv[:, c, 0:1], rstd[:, 0, c:c + 1],
                                    ALU.subtract, ALU.mult).then_inc(s_xn, 1)
                if k != "A":
                    dve.wait_ge(s_resb, at(plus(n, -2), 1, 1))
                    for c in range(C):
                        V.tensor_scalar(resx[u][:, c, :], hin[u][:, c, :], mv[:, c, 0:1], rstd[:, 1, c:c + 1],
                                        ALU.subtract, ALU.mult).then_inc(s_resx, 1)
                dve.wait_ge(s_xn, at(n, C, C))

            def head_variance(n, k):
                if k != "A":
                    return
                dve.wait_ge(s_sq, at(n, 1, 1))
                V.tensor_reduce(out=hvar[:, :], in_=sq[:, :, :, :].rearrange("p a c (h d) -> p (a c h) d", h=H),
                                op=ALU.add, axis=AX_X).then_inc(s_hvar, 1)
                dve.wait_ge(s_hvar, at(n, 1, 1))
                V.tensor_scalar(hvar[:, :], hvar[:, :], 1.0 / HD, EPS, ALU.mult, ALU.add).then_inc(s_hve, 1)

            def head_norm(n, k):
                if k != "A":
                    return
                heads = qk[:, :, :, :].rearrange("p a c (h d) -> p (a c h) d", h=H)
                dve.wait_ge(s_hrstd, at(n, 1, 1))
                V.scalar_tensor_tensor(out=newton[:, :], in0=hrstd[:, :], scalar=-0.5, in1=hrstd[:, :],
                                       op0=ALU.mult, op1=ALU.mult).then_inc(s_newton, 1)
                dve.wait_ge(s_newton, at(n, 3, 1))
                V.tensor_tensor(newton[:, :], newton[:, :], hvar[:, :], ALU.mult).then_inc(s_newton, 1)
                dve.wait_ge(s_newton, at(n, 3, 2))
                V.scalar_tensor_tensor(out=hrstd[:, :], in0=newton[:, :], scalar=1.5, in1=hrstd[:, :],
                                       op0=ALU.add, op1=ALU.mult).then_inc(s_newton, 1)
                dve.wait_ge(s_newton, at(n, 3, 3))
                dve.wait_ge(s_qkg, at(n, 1, 1))
                V.tensor_tensor(heads, heads, hrstd[:, :].unsqueeze(2).to_broadcast([P, 72, HD]),
                                ALU.mult).then_inc(s_qkn, 1)
                dve.wait_ge(s_qkn, at(n, 1, 1))
                V.tensor_tensor(qk[:, :, :, :], qk[:, :, :, :],
                                shifts[:, :, :].unsqueeze(2).to_broadcast([P, 2, C, D]),
                                ALU.add).then_inc(s_qkb, 1)

            def k_low(n):
                dve.wait_ge(s_khi, at(n, 1, 1))
                V.tensor_tensor(ks[:, :, 3 * HD:4 * HD],
                                qk[:, 1, :, :].rearrange("p c (h d) -> p (c h) d", h=H), ks[:, :, 0:HD],
                                ALU.subtract).then_inc(s_klo, 1)

            def q_low(n):
                dve.wait_ge(s_qhi, at(n, 1, 1))
                V.scalar_tensor_tensor(out=qs[:, :, HD:2 * HD],
                                       in0=qk[:, 0, :, :].rearrange("p c (h d) -> p (c h) d", h=H),
                                       scalar=SCALE, in1=qs[:, :, 0:HD], op0=ALU.mult,
                                       op1=ALU.subtract).then_inc(s_qlo, 1)

            def heads_copy(n, dst, s_pe, s_done):
                dve.wait_ge(s_pe, at(n, 2, 1))
                V.tensor_copy(dst[:, :, 0:SEQ], item(0)).then_inc(s_done, 1)

            def heads_copy_1(n, dst, s_pe, s_done):
                dve.wait_ge(s_pe, at(n, 2, 2))
                V.tensor_copy(dst[:, :, SEQ:2 * SEQ], item(1)).then_inc(s_done, 1)

            def maxes(n, tiles):
                for t in tiles:
                    c, g = divmod(t, NHG)
                    rows = P if c < 2 else IMG_END
                    dve.wait_ge(s_sc, at(n, TILES, t + 1))
                    V.tensor_reduce(out=negmax[0:rows, c, heads_of(g)],
                                    in_=SM[t % 2][0:rows, 0:HG * SEQ].rearrange("p (h s) -> p h s", h=HG),
                                    op=ALU.max, axis=AX_X, negate=True).then_inc(s_mx, 1)

            def shift(n):
                dve.wait_ge(s_mx, at(n, TILES, TILES))
                nm = negmax[:, :, :].rearrange("p c h -> p (c h)")
                V.tensor_copy(qs[:, :, 2 * HD], nm).then_inc(s_mh, 1)
                dve.wait_ge(s_mh, at(n, 1, 1))
                V.tensor_tensor(qs[:, :, 2 * HD + 1], nm, qs[:, :, 2 * HD], ALU.subtract).then_inc(s_ml, 1)

            def o_norm(n, c):
                o = O_BANK[c][:, 0:3 * P].rearrange("p (h e) -> p h e", h=H)
                dve.wait_ge(s_onpe, at(n, C, c + 1))
                V.reciprocal(rden[:, c, :], o[:, :, HD]).then_inc(s_rden, 1)
                dve.wait_ge(s_rden, at(n, C, c + 1))
                if c == 0 and later(n, 1):
                    dve.wait_ge(s_ohi, at(plus(n, -1), 1, 1))
                V.tensor_tensor(on[:, c, :].rearrange("p (h d) -> p h d", h=H), o[:, :, 0:HD],
                                rden[:, c, :].unsqueeze(2).to_broadcast([P, H, HD]),
                                ALU.mult).then_inc(s_on, 1)

            def adds(n, u):
                dve.wait_ge(s_resb, at(n, 1, 1))
                if later(n, 2):
                    dve.wait_ge(s_stored[u], at_parity(plus(n, -2), 16))
                for c in range(C):
                    bk, o = Y_BANK[c]
                    dve.wait_ge(s_ype, at(n, 2, 1 if c < 2 else 2))
                    V.scalar_tensor_tensor(out=outb[u][:, c, :], in0=bk[:, o:o + D], scalar=1.0 / WS,
                                           in1=resb[u][:, c, :], op0=ALU.mult, op1=ALU.add).then_inc(s_y, 1)

            def step(n, u, ko, kb, kf, kp):
                prev, nx, n2, v = plus(n, -1), plus(n, 1), plus(n, 2), 1 - u
                if isinstance(n, int) and n == -1:
                    prepare_fc2()
                if kb:
                    maxes(n, (0, 1))
                if ko:
                    o_norm(prev, 0)
                    o_norm(prev, 1)
                if kb:
                    maxes(n, (2, 3))
                if ko:
                    o_norm(prev, 2)
                if kb:
                    maxes(n, (4, 5))
                    maxes(n, (6, 7))
                if kf:
                    head_variance(nx, kf)
                if kb:
                    maxes(n, (8, 9))
                    maxes(n, (10, 11))
                    shift(n)
                if ko:
                    adds(prev, v)
                if kb:
                    heads_copy(n, qT[u], s_qmpe, s_qm)
                if kf:
                    head_norm(nx, kf)
                if kf in ("L", "S"):
                    k_low(nx)
                if kp:
                    x_stats(n2, u, kp)
                if kf == "A":
                    k_low(nx)
                if kp:
                    x_norm(n2, u, kp)
                if kf:
                    q_low(nx)
                    heads_copy(nx, kT[v], s_ktpe, s_kt)
                    heads_copy_1(nx, kT[v], s_ktpe, s_kt)
                    heads_copy(nx, qT[v], s_qtpe, s_qt)
                    heads_copy_1(nx, qT[v], s_qtpe, s_qt)

            dve.wait_ge(s_zero, 1)
            run_steps(dve, step)

            def mstats(m, u):
                dve.wait_ge(s_mx2[u], at_parity(m, 16))
                norm_stats(m, x2in[u], m_stats, m_aggr, m_ve, ((1.0, EPS),))

            def mnorm(m, u):
                dve.wait_ge(m_rstd, at(m, 1, 1))
                if later(m, 1):
                    dve.wait_ge(m_hi, at(plus(m, -1), 1, 1))
                for c in range(C):
                    V.tensor_scalar(xn[:, c, :], x2in[u][:, c, :], mv[:, c, 0:1], rstd[:, 0, c:c + 1],
                                    ALU.subtract, ALU.mult).then_inc(m_xn, 1)
                dve.wait_ge(m_xn, at(m, C, C))

            def mlows(m):
                lows(m, xn, xs, m_hi, m_lo)

            def mT_copy(m, u):
                for i, (c0, cn) in enumerate(((0, 2), (2, 1))):
                    dve.wait_ge(m_tpe, at(m, 2, i + 1))
                    V.tensor_copy(mT[:, :, :].rearrange("p t (c n) -> p c t n", c=C)[:, c0:c0 + cn, :, :],
                                  half(TP[i])[:, 0:cn * 3 * P].rearrange("p (c t n) -> p c t n", c=cn, t=3))\
                        .then_inc(m_t, 1)

            def madds(m, u, k):
                dve.wait_ge(m_res, at(m, 1, 1))
                if later(m, 2):
                    dve.wait_ge(s_out[u], at_parity(plus(m, -2), 48))
                for c in range(C):
                    dve.wait_ge(m_f2, mlp_at(m, k, C, C * last_branch(k) + c + 1))
                    V.scalar_tensor_tensor(out=outb[u][:, c, :], in0=yacc[c][:, 0:D], scalar=1.0 / WS,
                                           in1=resb[u][:, c, :], op0=ALU.mult, op1=ALU.add).then_inc(m_y, 1)

            def gelu_split(m, k, br, tiles=range(NHT)):
                i = branch_parity(m, k, br)
                if tiles[0] == 0 and (later(m, 1) or br >= 2):
                    dve.wait_ge(m_f2, mlp_at(m, k, C, C * (br - 1)))
                for t in tiles:
                    dve.wait_ge(m_g, mlp_at(m, k, NHT, NHT * br + t + 1))
                    V.tensor_copy(gH[i][:, t, :], gT[:, t, :]).then_inc(m_gh, 1)
                    if t % 2 == 0:
                        dve.wait_ge(m_gh, mlp_at(m, k, NHT, NHT * br + t + 1))
                        V.tensor_tensor(gL[i][:, t, :], gT[:, t, :], gH[i][:, t, :],
                                        ALU.subtract).then_inc(m_gle, 1)

            yacc = (bank[3], G0, G1)

            def mstep(m, u, ko, kb, kf, k2):
                if kf:
                    mstats(plus(m, 1), 1 - u)
                if kb:
                    gelu_split(m, kb, 0, range(0, 2))
                if kf:
                    mnorm(plus(m, 1), 1 - u)
                if kb:
                    gelu_split(m, kb, 0, range(2, 4))
                if kf:
                    mlows(plus(m, 1))
                if kb:
                    gelu_split(m, kb, 0, range(4, NHT))
                if kf and kb == "L":
                    mT_copy(plus(m, 1), 1 - u)
                if ko:
                    madds(plus(m, -1), 1 - u, ko)
                if kb == "S":
                    gelu_split(m, kb, 1)
                    gelu_split(m, kb, 2)
                    if kf:
                        mT_copy(plus(m, 1), 1 - u)

            mstats(0, 0)
            mnorm(0, 0)
            mlows(0)
            mT_copy(0, 0)
            run_mlp(dve, mstep)

        @block.tensor
        def _(pe):
            mm = nc.tensor.matmul
            tr = nc.tensor.transpose

            pe.wait_ge(s_cst, 4)
            pe.wait_ge(s_wa, 16 * FIRST_LOADS)
            for i, raw in enumerate((raw_qkv[0], raw_qkv[1], raw_qkv[1])):
                if i == 1:
                    pe.wait_ge(s_w, 16 * SETUP_LOADS)
                pe.wait_ge(s_bw, i + 1)
                for o, w, bk in ((0, 2 * D, G0), (2 * D, D, G1)):
                    mm(bk[:, 0:w], bwide[:, 0, :], raw[:, 0, o:o + w], start=True, stop=False)
                    last = mm(bk[:, 0:w], bwide[0:LO, 1, :], raw[0:LO, 1, o:o + w], start=False, stop=True)
                last.then_inc(s_bmm, 1)
            pe.wait_ge(s_wv, AFTER_QKV)
            for row, (norm, rows) in enumerate(((7, D), (9, KEEP[0]), (9, KEEP[1]), (9, KEEP[2]))):
                for t in range(NHT):
                    o = G0[:, row * NHT + t:row * NHT + t + 1]
                    first = min(rows, P)
                    last = mm(o, raw_fc1[0:first, 0, t * P:(t + 1) * P], bcol[0:first, norm, 0:1],
                              start=True, stop=rows <= P)
                    if rows > P:
                        last = mm(o, raw_fc1[0:LO, 1, t * P:(t + 1) * P], bcol[0:LO, norm, 1:2],
                                  start=False, stop=True)
            last.then_inc(s_bmm, 1)

            def split_product(out, lhs, w, cols, bias=None):
                if bias is not None:
                    mm(out, both_rows[:, :], bias[:, cols], start=True, stop=False)
                for i, (t, slot) in enumerate(((0, 0), (0, 1), (2, 0), (1, 2), (1, 3))):
                    last = mm(out, lhs[:, t, :], w[:, slot, cols], start=i == 0 and bias is None, stop=i == 4)
                return last

            def transposes_rows(src, s_inc, before):
                for i, chunks in enumerate(((0, 1), (2,))):
                    before(i)
                    for m, c in enumerate(chunks):
                        for t in range(3):
                            last = tr(half(TP[i])[:, (3 * m + t) * P:(3 * m + t + 1) * P],
                                      src[:, c, t * P:(t + 1) * P], idh[:, :])
                    last.then_inc(s_inc, 1)

            def transposes_heads(src, s_inc, before):
                for b in range(2):
                    before(b)
                    r = IMG_AT[b]
                    for t in range(NPT):
                        tr(half(TP[b])[:, t * SEQ:t * SEQ + TXT],
                           src[:, H * b + 2 * t:H * b + 2 * t + 2, :].rearrange("p a k -> p (a k)"), idh[:, :])
                    for t in range(NPT):
                        last = tr(half(TP[b])[:, t * SEQ + TXT:(t + 1) * SEQ],
                                  src[r:r + IMG, 2 * H + 2 * t:2 * H + 2 * t + 2, :]
                                  .rearrange("p a k -> p (a k)"), idh[r:r + IMG, r:r + IMG])
                    last.then_inc(s_inc, 1)

            def tok(n, u, k):
                if k != "A":
                    return
                pe.wait_ge(s_tokin[u], at_parity(n, 32))
                if later(n, 1):
                    pe.wait_ge(s_qk, at(plus(n, -1), C, 2))
                for t in range(2):
                    last = mm(G1[0:IMG_END, 0:D], patches[u][:, t, :], tokw[:, t, :], start=t == 0, stop=t == 1)
                last.then_inc(s_tokmm, 1)

            def x_transposes(n):
                pe.wait_ge(s_xlo, at(n, 2, 2))

                def before(i):
                    if later(n, 1):
                        pe.wait_ge(s_qt, at(plus(n, -1), 2, 2))
                transposes_rows(xs, s_xtpe, before)

            def qk_product(n, k, c):
                if c == 0:
                    pe.wait_ge(s_xt, at(n, 2, 2))
                    if later(n, 1):
                        pe.wait_ge(s_v, at(plus(n, -1), 2, 2))
                elif c == 2:
                    pe.wait_ge(s_qk, at(n, C, 1))
                split_product(QK_BANK[c][:, 0:2 * D], xt[:, c, :, :], w_qkv[k],
                              slice(0, 2 * D), b_row[k]).then_inc(s_qkmm, 1)

            def v_product(n, k, chunks, kp):
                pe.wait_ge(s_qk, at(n, C, 2 if chunks[0] == 0 else 3))
                if kp == "A" and chunks[0] == 0:
                    pe.wait_ge(s_toksb, at(plus(n, 1), 1, 1))
                for c in chunks:
                    bk, o = V_BANK[c]
                    last = split_product(bk[:, o:o + D], xt[:, c, :, :], w_qkv[k], slice(2 * D, 3 * D),
                                         b_row[k])
                last.then_inc(s_vmm, 1)

            def k_transposes(n):
                pe.wait_ge(s_klo, at(n, 1, 1))

                def before(b):
                    if later(n, 1):
                        pe.wait_ge(s_qm, at(plus(n, -1), 2, 2))
                    else:
                        pe.wait_ge(s_xt, at(n, 2, 2))
                transposes_heads(ks, s_ktpe, before)

            def q_transposes(n):
                pe.wait_ge(s_qlo, at(n, 1, 1))
                pe.wait_ge(s_mz, at(n, 1, 1))

                def before(b):
                    pe.wait_ge(s_kt, at(n, 2, 2))
                transposes_heads(qs, s_qtpe, before)

            def scores(n, u, tiles, bank_of, keys_out, s_free, s_done):
                lhs, rhs = (kT[u], qT[u]) if keys_out else (qT[u], kT[u])
                for t in tiles:
                    c, g = divmod(t, NHG)
                    if t >= 2:
                        pe.wait_ge(s_free, at(n, TILES, t - 1))
                    for i in range(HG):
                        h = heads_of(g).start + 2 * i
                        r = BLK * (h % 2)
                        cols = slice(i * SEQ, (i + 1) * SEQ)
                        for b in ((c,) if c < 2 else (0, 1)):
                            o = SEQ * b + (0 if c < 2 else TXT)
                            m = TXT if c < 2 else BLK if b == 0 else IMG
                            if c == 2 and i == 0 and b == 0:
                                m = IMG_END
                            q = 0 if c < 2 else IMG_AT[b]
                            last = mm(bank_of[t % 2][q:q + m, cols], lhs[r:r + BLK, h // 2, o:o + m],
                                      rhs[r:r + BLK, h // 2, SEQ * b:SEQ * (b + 1)], start=True, stop=True)
                    last.then_inc(s_done, 1)

            def max_scores(n, u, tiles):
                if tiles[0] == 0:
                    pe.wait_ge(s_kt, at(n, 2, 2))
                    pe.wait_ge(s_qt, at(n, 2, 2))
                    if later(n, 1):
                        pe.wait_ge(s_ot, at(plus(n, -1), 4, 4))
                scores(n, u, tiles, SM, False, s_mx, s_sc)

            def exp_scores(n, u, tiles):
                if tiles[0] == 0:
                    if later(n, 1):
                        pe.wait_ge(s_y, at(plus(n, -1), C, C))
                    pe.wait_ge(s_qm, at(n, 2, 2))
                scores(n, u, tiles, SE, True, s_ex, s_st)

            def shift(n, ko, kf):
                pe.wait_ge(s_ml, at(n, 1, 1))

                def before(b):
                    if ko:
                        pe.wait_ge(s_ou, at(plus(n, -1), 2, 2))
                    else:
                        pe.wait_ge(s_xt, at(plus(n, 1), 2, 2))
                transposes_heads(qs, s_qmpe, before)

            def pv_text(n, u, b, groups):
                for g in groups:
                    for h in range(4 * g, 4 * g + 4):
                        q = 32 * (h % 4)
                        mm(SM[b][q:q + 32, g * SEQ:(g + 1) * SEQ], v1[u][:, b, h, :], probs[:, b, h, :],
                           start=g == 0, stop=False, tile_position=(0, q), skip_group_check=True)

            def pv_first(n, u, b, groups):
                pe.wait_ge(s_ex, at(n, TILES, NHG * (b + 1)))
                if b == 0 and groups[0] == 0:
                    pe.wait_ge(s_v, at(n, 2, 2))
                pv_text(n, u, b, groups)

            def pv_image(n, u, half_of):
                pe.wait_ge(s_ex, at(n, TILES, TILES - 2 + 2 * half_of))
                pv_text(n, u, 1, (1 + half_of,))
                for b in range(2):
                    r = IMG_AT[b]
                    for h in range(H // 2 * half_of, H // 2 * (half_of + 1)):
                        g, q = h // 4, 32 * (h % 4)
                        last = mm(SM[b][q:q + 32, g * SEQ:(g + 1) * SEQ], v1[u][r:r + IMG, 2, h, :],
                                  probs[r:r + IMG, 2, h, :], start=False, stop=g == 2, tile_position=(r, q),
                                  skip_group_check=True)
                    if half_of:
                        last.then_inc(s_otpe, 1)

            def o_transposes(n, c):
                if c == 0:
                    pe.wait_ge(s_ot, at(n, 4, 4))
                elif c == 2:
                    pe.wait_ge(s_on, at(n, C, 1))
                for g in range(3):
                    last = tr(O_BANK[c][:, g * P:(g + 1) * P], oT[:, g, c, :], idf[:, :])
                last.then_inc(s_onpe, 1)

            def ou_transposes(n, kf):
                pe.wait_ge(s_olo, at(n, 2, 2))

                def before(i):
                    if kf:
                        pe.wait_ge(s_xt, at(plus(n, 2), 2, 2))
                transposes_rows(os_, s_oupe, before)

            def proj(n, k):
                pe.wait_ge(s_ou, at(n, 2, 2))
                pe.wait_ge(s_on, at(n, C, C))
                for c in range(C):
                    bk, o = Y_BANK[c]
                    last = split_product(bk[:, o:o + D], ou[:, c, :, :], w_prj[k], slice(0, D))
                    if c:
                        last.then_inc(s_ype, 1)

            def step(n, u, ko, kb, kf, kp):
                prev, nx, n2 = plus(n, -1), plus(n, 1), plus(n, 2)
                if isinstance(n, int) and n == -1:
                    pe.wait_ge(s_wv, SETUP_STEPS)
                if kb:
                    max_scores(n, u, (0, 1))
                if ko:
                    o_transposes(prev, 0)
                    o_transposes(prev, 1)
                if kf:
                    qk_product(nx, kf, 0)
                if kb:
                    max_scores(n, u, (2, 3))
                if ko:
                    o_transposes(prev, 2)
                if kf:
                    qk_product(nx, kf, 1)
                if kb:
                    max_scores(n, u, (4, 5))
                if kf:
                    qk_product(nx, kf, 2)
                if kb:
                    max_scores(n, u, (6, 7))
                if kp:
                    tok(n2, u, kp)
                if kb:
                    max_scores(n, u, (8, 9))
                if ko:
                    ou_transposes(prev, kf)
                if kb:
                    max_scores(n, u, (10, 11))
                if ko:
                    proj(prev, ko)
                if kb:
                    shift(n, ko, kf)
                if kf:
                    v_product(nx, kf, (0, 1), kp)
                if kb:
                    exp_scores(n, u, range(0, 4))
                if kf:
                    v_product(nx, kf, (2,), kp)
                if kb:
                    exp_scores(n, u, range(4, 6))
                    pv_first(n, u, 0, (0, 1, 2))
                    exp_scores(n, u, range(6, 8))
                if kf:
                    k_transposes(nx)
                if kb:
                    exp_scores(n, u, range(8, 10))
                    pv_first(n, u, 1, (0,))
                    exp_scores(n, u, range(10, TILES))
                if kf:
                    q_transposes(nx)
                if kb:
                    pv_image(n, u, 0)
                    pv_image(n, u, 1)
                if kp:
                    x_transposes(n2)

            pe.wait_ge(s_zero, 1)
            pe.wait_ge(s_w, 16 * SETUP_LOADS)
            run_steps(pe, step)

            yacc = (bank[3], G0, G1)

            def mT_transposes(m):
                pe.wait_ge(m_lo, at(m, 2, 2))

                def before(i):
                    if later(m, 1):
                        pe.wait_ge(m_t, at(plus(m, -1), 2, 2))
                transposes_rows(xs, m_tpe, before)

            def fc1(m, k, br):
                rows = D if k == "L" else KEEP[br]
                for t in range(NHT):
                    if later(m, 1) or br or t >= 3:
                        pe.wait_ge(m_g, mlp_at(m, k, NHT, NHT * br + t - 2))
                    o = bank[t % 3][:, 0:C * P]
                    cols = slice(t * P, (t + 1) * P)
                    if rows == D:
                        passes = ((0, 0), (1, 0), (0, 2), (2, 1), (3, 1))
                        r = P
                    else:
                        passes = ((0, 0), (1, 0), (0, 2))
                        r = rows
                    for i, (slot, xtile) in enumerate(passes):
                        last = mm(o, w_fc1[k][0:r, slot, cols], mT[0:r, xtile, :], start=i == 0,
                                  stop=i == len(passes) - 1)
                    last.then_inc(m_f1, 1)

            def fc2(m, k, br, ahead=None):
                w = w_fc2[0 if k == "L" else br + 1]
                ch = D if k == "L" else KEEP[br]
                i = branch_parity(m, k, br)
                pe.wait_ge(m_gle, mlp_at(m, k, NHT // 2, NHT // 2 * (br + 1)))
                pe.wait_ge(m_glo, mlp_at(m, k, NHT // 2, NHT // 2 * (br + 1)))
                for c in range(C):
                    if c == C - 1 and ahead is not None:
                        mT_transposes(ahead)
                    if br == 0:
                        if later(m, 1):
                            pe.wait_ge(m_y, at(plus(m, -1), C, c + 1))
                    for t in range(NHT):
                        for g, slot in ((gH, 0), (gL, 0), (gH, 1)):
                            first = br == 0 and t == 0 and g is gH and slot == 0
                            last = mm(yacc[c][:, 0:ch], g[i][:, t, c * P:(c + 1) * P], w[:, slot, t, :],
                                      start=first, stop=br == last_branch(k) and t == NHT - 1 and slot == 1,
                                      skip_group_check=True)
                    last.then_inc(m_f2, 1)

            def mstep(m, u, ko, kb, kf, k2):
                n_br = last_branch(kb) + 1 if kb else 1
                for br in range(n_br):
                    if kb:
                        if br == 0 and ko:
                            pe.wait_ge(m_t, at(m, 2, 2))
                        fc1(m, kb, br)
                    ahead = plus(m, 1) if br == n_br - 1 and kf else None
                    if br:
                        fc2(m, kb, br - 1, ahead)
                    elif ko:
                        fc2(plus(m, -1), ko, last_branch(ko), ahead)
                    elif ahead is not None:
                        mT_transposes(ahead)

            mT_transposes(0)
            pe.wait_ge(m_t, 2)
            run_mlp(pe, mstep)


NORMS = ("attn_ln_g", "attn_ln_b", "ffn_n1l_g", "ffn_n1l_b", "ffn_n1s_g", "ffn_n1s_b",
         "ffn_n2l_g", "ffn_n2l_b", "ffn_n2s_g", "ffn_n2s_b")
FIRST_LOADS = 3
SETUP_LOADS = 6
VEC_PRJ = {"A": 3 * D, "L": 4 * D}
VEC_FC2 = 5 * D
VEC_GW = 6 * D
VEC_HEADS = VEC_GW + 4
VEC_END = VEC_HEADS + 4 * HD
AFTER_QKV = 3 + 23 + 14 + 4
SETUP_STEPS = 101


def kernel(x, txt, L0_tok_W, L0_attn_ln_g, L0_attn_ln_b, L0_attn_W_qkv, L0_attn_b_qkv, L0_attn_qn_g,
           L0_attn_qn_b, L0_attn_kn_g, L0_attn_kn_b, L0_attn_W_proj, L0_attn_b_proj, L0_ffn_gumbel_weights,
           L0_ffn_n1l_g, L0_ffn_n1l_b, L0_ffn_n1s_g, L0_ffn_n1s_b, L0_ffn_w_qkv, L0_ffn_w_proj,
           L0_ffn_b_proj, L0_ffn_n2l_g, L0_ffn_n2l_b, L0_ffn_n2s_g, L0_ffn_n2s_b, L0_ffn_w_fc1,
           L0_ffn_b_fc1, L0_ffn_w_fc2, L0_ffn_b_fc2):
    import numpy as np
    import concourse.bacc as bacc
    from concourse.bass_utils import run_bass_kernel_spmd

    x = np.asarray(x)
    pt = x.reshape(PAIRS, 2, 6, 16, 6, 16).transpose(0, 3, 5, 1, 2, 4).reshape(PAIRS, 2, P, 2, IMG)
    padded = np.zeros((PAIRS, P, 2, IMG_END), np.float32)
    for b in range(2):
        padded[:, :, :, IMG_AT[b]:IMG_AT[b] + IMG] = pt[:, :, :, b, :].transpose(0, 2, 1, 3)

    def rows(w):
        w = np.asarray(w)
        return np.stack([w[0:P], np.concatenate([w[P:D], w[P:D]])], axis=1)

    norms = dict(attn_ln_g=L0_attn_ln_g, attn_ln_b=L0_attn_ln_b, ffn_n1l_g=L0_ffn_n1l_g, ffn_n1l_b=L0_ffn_n1l_b,
                 ffn_n1s_g=L0_ffn_n1s_g, ffn_n1s_b=L0_ffn_n1s_b, ffn_n2l_g=L0_ffn_n2l_g,
                 ffn_n2l_b=L0_ffn_n2l_b, ffn_n2s_g=L0_ffn_n2s_g, ffn_n2s_b=L0_ffn_n2s_b)
    columns = np.concatenate([rows(np.asarray(norms[k])[:, None])[:, :, 0] for k in NORMS]
                             + [np.asarray(L0_ffn_b_fc1).reshape(NHT, P).T], axis=1)
    vectors = np.concatenate([np.asarray(v) for v in (
        L0_attn_b_qkv, L0_attn_b_proj, L0_ffn_b_proj, L0_ffn_b_fc2, L0_ffn_gumbel_weights,
        np.zeros(1, np.float32), L0_attn_qn_g, L0_attn_qn_b, L0_attn_kn_g, L0_attn_kn_b)])
    arrays = dict(
        patches=padded, txt=txt, tokw=np.asarray(L0_tok_W).T, columns=columns, vectors=vectors,
        attn_W_qkv=rows(L0_attn_W_qkv), attn_W_proj=rows(L0_attn_W_proj), ffn_w_qkv=rows(L0_ffn_w_qkv),
        ffn_w_proj=rows(L0_ffn_w_proj), ffn_w_fc1=rows(L0_ffn_w_fc1), ffn_w_fc2=L0_ffn_w_fc2)
    arrays = {k: np.ascontiguousarray(v) for k, v in arrays.items()}
    nc = bacc.Bacc("TRN2", target_bir_lowering=False, num_devices=1)
    a = {k: nc.dram_tensor(f"in_{k}", v.shape, mybir.dt.from_np(v.dtype), kind="ExternalInput").ap()
         for k, v in arrays.items()}
    a["out"] = nc.dram_tensor("out_0", (BATCH, SEQ, D), F32, kind="ExternalOutput").ap()
    build(nc, a)
    r = run_bass_kernel_spmd(nc, [{f"in_{k}": v for k, v in arrays.items()}], core_ids=[0])
    return r.results[0]["out_0"]
```
